# Optimizing a Trainium2 kernel written in Bass

```python
import numpy as np
import jax
import jax.numpy as jnp

def _softmax(x, axis=-1):
    return jax.nn.softmax(x, axis=axis)

def _gelu(x):
    return jax.nn.gelu(x, approximate=True)

def _silu(x):
    return jax.nn.silu(x)

def _sigmoid(x):
    return jax.nn.sigmoid(x)

def _layernorm(x, axis=-1, eps=1e-05):
    m = jnp.mean(x, axis=axis, keepdims=True)
    v = jnp.var(x, axis=axis, keepdims=True)
    return (x - m) / jnp.sqrt(v + eps)

def _scatter_add(tgt, idx, src, axis=0):
    return tgt.at[idx].add(src)

def _segment_sum(src, seg, n):
    return jax.ops.segment_sum(src, seg, n)
kernel_name = 'mk_conv_attn_hybrid_d4_conv_nchw128_r2_2c6f0f'

def setup_inputs(seed: int=0):
    np.random.seed(seed)
    _w = jnp.asarray

    def _rec_inputs():
        import jax
        import jax.numpy as jnp
        _gk = jax.random.key(seed)
        x = -0.0002928 + 1 * jax.random.normal(jax.random.fold_in(_gk, 1), (8, 64, 32, 32), jnp.float32)
        return x
    x = _rec_inputs()

    def _L0_conv_setup():
        import jax, jax.numpy as jnp
        import numpy as np
        key = jax.random.key(seed)
        k = jax.random.split(key, 5)
        C, Cb = (64, 32)
        x = jax.random.normal(k[0], (8, C, 32, 32), dtype=jnp.float32)
        s_in = 1.0 / np.sqrt(C)
        s_b = 1.0 / np.sqrt(Cb)
        w_theta = jax.random.normal(k[1], (Cb, C), dtype=jnp.float32) * s_in
        w_phi = jax.random.normal(k[2], (Cb, C), dtype=jnp.float32) * s_in
        w_g = jax.random.normal(k[3], (Cb, C), dtype=jnp.float32) * s_in
        w_last = jax.random.normal(k[4], (C, Cb), dtype=jnp.float32) * s_b
        return {'x': x, 'w_theta': w_theta, 'w_phi': w_phi, 'w_g': w_g, 'w_last': w_last}
    _L0_conv_all = _L0_conv_setup()
    _L0_conv_in = {k: v for k, v in _L0_conv_all.items() if k in ('w_theta', 'w_phi', 'w_g', 'w_last')}
    del _L0_conv_all

    def _L1_conv_setup():
        import jax, jax.numpy as jnp
        import numpy as np
        import math
        B, C, H, W = (16, 64, 36, 100)
        K = 9
        PAD = 4

        def _conv1d(x, w, b):
            y = jax.lax.conv_general_dilated(x, w, window_strides=(1,), padding=[(PAD, PAD)], dimension_numbers=('NCH', 'OIH', 'NCH'))
            return y + b[None, :, None]

        def _pass_fwd(out, w, b, axis):
            rows = jnp.moveaxis(out, axis, 0)

            def step(carry, x):
                new = x + jax.nn.relu(_conv1d(carry, w, b))
                return (new, new)
            _, updated = jax.lax.scan(step, rows[0], rows[1:])
            res = jnp.concatenate([rows[:1], updated], axis=0)
            return jnp.moveaxis(res, 0, axis)

        def _pass_bwd(out, w, b, axis):
            rows = jnp.moveaxis(out, axis, 0)
            L = rows.shape[0]

            def step(carry, x):
                new = x + jax.nn.relu(_conv1d(carry, w, b))
                return (new, new)
            xs = rows[1:L - 1][::-1]
            _, updated = jax.lax.scan(step, rows[L - 1], xs)
            res = jnp.concatenate([rows[:1], updated[::-1], rows[L - 1:]], axis=0)
            return jnp.moveaxis(res, 0, axis)
        key = jax.random.key(seed)
        ks = jax.random.split(key, 9)
        x = jax.random.normal(ks[0], (B, C, H, W), dtype=jnp.float32)
        bound = math.sqrt(2.0 / (C * K * 5))
        b_bound = 1.0 / math.sqrt(C * K)

        def mkw(k):
            return jax.random.uniform(k, (C, C, K), jnp.float32, -bound, bound)

        def mkb(k):
            return jax.random.uniform(k, (C,), jnp.float32, -b_bound, b_bound)
        return {'x': x, 'w_d': mkw(ks[1]), 'b_d': mkb(ks[2]), 'w_u': mkw(ks[3]), 'b_u': mkb(ks[4]), 'w_r': mkw(ks[5]), 'b_r': mkb(ks[6]), 'w_l': mkw(ks[7]), 'b_l': mkb(ks[8])}
    _L1_conv_all = _L1_conv_setup()
    _L1_conv_in = {k: v for k, v in _L1_conv_all.items() if k in ('w_d', 'b_d', 'w_u', 'b_u', 'w_r', 'b_r', 'w_l', 'b_l')}
    del _L1_conv_all

    def _L2_attn_setup():
        import jax, jax.numpy as jnp
        import numpy as np
        EMB, HEADS, K = (64, 8, 32)
        key = jax.random.key(seed)
        ks = jax.random.split(key, 6)
        b, t, e, h = (2, 1024, EMB, HEADS)
        s = 1.0 / np.sqrt(e).astype(np.float32)
        x = jax.random.normal(ks[0], (b, t, e), jnp.float32)
        Wq = jax.random.normal(ks[1], (e * h, e), jnp.float32) * s
        Wk = jax.random.normal(ks[2], (e * h, e), jnp.float32) * s
        Wv = jax.random.normal(ks[3], (e * h, e), jnp.float32) * s
        Wu = jax.random.normal(ks[4], (e, h * e), jnp.float32) * (1.0 / np.sqrt(h * e).astype(np.float32))
        bu = jnp.zeros((e,), jnp.float32)
        return {'x': x, 'Wq': Wq, 'Wk': Wk, 'Wv': Wv, 'Wu': Wu, 'bu': bu}
    _L2_attn_all = _L2_attn_setup()
    _L2_attn_in = {k: v for k, v in _L2_attn_all.items() if k in ('Wq', 'Wk', 'Wv', 'Wu', 'bu')}
    del _L2_attn_all

    def _L2_ffn_setup():
        import jax, jax.numpy as jnp
        import numpy as np
        PADDED_SL = 4096
        TEMPERATURE = 1.0
        SIGMA_POW = 0.25

        def _stu_conv(phi, u, n):
            b, sl, d = u.shape
            sgn = jnp.where(jnp.arange(sl) % 2 == 0, 1.0, -1.0).astype(u.dtype)
            sgn3 = sgn[None, :, None]
            Vf = jnp.fft.rfft(phi, n=n, axis=0)
            Uf_p = jnp.fft.rfft(u, n=n, axis=1)
            Uf_m = jnp.fft.rfft(u * sgn3, n=n, axis=1)
            U_plus = jnp.fft.irfft(Vf[None, :, :, None] * Uf_p[:, :, None, :], n=n, axis=1)[:, :sl]
            U_minus = jnp.fft.irfft(Vf[None, :, :, None] * Uf_m[:, :, None, :], n=n, axis=1)[:, :sl]
            U_minus = U_minus * sgn[None, :, None, None]
            return (U_plus, U_minus)

        def _compute_spectral(u, sigma, phi, Mpp, Mpm):
            U_plus, U_minus = _stu_conv(phi, u, PADDED_SL)
            s = sigma ** SIGMA_POW
            out = jnp.einsum('btkd,k,kde->bte', U_plus, s, Mpp)
            out = out + jnp.einsum('btkd,k,kde->bte', U_minus, s, Mpm)
            return out

        def _compute_ar_u(Mu, u):
            sl = u.shape[1]
            out = jnp.zeros(u.shape[:2] + (Mu.shape[-1],), dtype=u.dtype)
            for i in range(Mu.shape[0]):
                ui = jnp.pad(u, ((0, 0), (i, 0), (0, 0)))[:, :sl]
                out = out + jnp.einsum('btd,de->bte', ui, Mu[i])
            return out

        def _stu(u, sigma, phi, Mu, Mpp, Mpm):
            return _compute_spectral(u, sigma, phi, Mpp, Mpm) + _compute_ar_u(Mu, u)
        key = jax.random.key(seed)
        ks = jax.random.split(key, 8)
        b, sl, d, K, k_u = (2, 2048, 64, 16, 3)
        x = jax.random.normal(ks[0], (b, sl, d), dtype=jnp.float32)
        sigma = jax.random.uniform(ks[1], (K,), dtype=jnp.float32, minval=0.001, maxval=1.0)
        phi = jax.random.normal(ks[2], (sl, K), dtype=jnp.float32) / np.sqrt(sl)
        M_u = jax.random.normal(ks[3], (4, k_u, d, d), dtype=jnp.float32) * 0.02
        M_phi_plus = jax.random.normal(ks[4], (4, K, d, d), dtype=jnp.float32) * 0.02
        M_phi_minus = jax.random.normal(ks[5], (4, K, d, d), dtype=jnp.float32) * 0.02
        log_weights = jnp.ones((4,), dtype=jnp.float32)
        u01 = jax.random.uniform(ks[6], (4,), dtype=jnp.float32, minval=1e-06, maxval=1.0 - 1e-06)
        gumbel = -jnp.log(-jnp.log(u01))
        return {'x': x, 'sigma': sigma, 'phi': phi, 'M_u': M_u, 'M_phi_plus': M_phi_plus, 'M_phi_minus': M_phi_minus, 'log_weights': log_weights, 'gumbel': gumbel}
    _L2_ffn_all = _L2_ffn_setup()
    _L2_ffn_in = {k: v for k, v in _L2_ffn_all.items() if k in ('sigma', 'phi', 'M_u', 'M_phi_plus', 'M_phi_minus', 'log_weights', 'gumbel')}
    del _L2_ffn_all

    def _L3_attn_setup():
        import jax, jax.numpy as jnp
        import numpy as np
        BS, L, D_MODEL, N_HEADS = (8, 8192, 64, 8)
        HEAD_DIM = D_MODEL // N_HEADS
        EPS = 1e-05
        key = jax.random.key(seed)
        ks = jax.random.split(key, 9)
        scale = 1.0 / np.sqrt(D_MODEL)
        return {'Q': jax.random.normal(ks[0], (BS, L, D_MODEL), dtype=jnp.float32), 'Wq': jax.random.normal(ks[1], (D_MODEL, D_MODEL), dtype=jnp.float32) * scale, 'bq': jax.random.normal(ks[2], (D_MODEL,), dtype=jnp.float32) * 0.01, 'Wk': jax.random.normal(ks[3], (D_MODEL, D_MODEL), dtype=jnp.float32) * scale, 'bk': jax.random.normal(ks[4], (D_MODEL,), dtype=jnp.float32) * 0.01, 'Wv': jax.random.normal(ks[5], (D_MODEL, D_MODEL), dtype=jnp.float32) * scale, 'bv': jax.random.normal(ks[6], (D_MODEL,), dtype=jnp.float32) * 0.01, 'Wo': jax.random.normal(ks[7], (D_MODEL, D_MODEL), dtype=jnp.float32) * scale, 'bo': jax.random.normal(ks[8], (D_MODEL,), dtype=jnp.float32) * 0.01}
    _L3_attn_all = _L3_attn_setup()
    _L3_attn_in = {k: v for k, v in _L3_attn_all.items() if k in ('Wq', 'bq', 'Wk', 'bk', 'Wv', 'bv', 'Wo', 'bo')}
    del _L3_attn_all

    def _L3_ffn_setup():
        import jax, jax.numpy as jnp
        import numpy as np
        B, S, D, E, H, O, K = (256, 1024, 64, 32, 256, 64, 8)
        key = jax.random.key(seed)
        k0, k1, k2, k3 = jax.random.split(key, 4)
        x = jax.random.normal(k0, (B, S, D), dtype=jnp.float32)
        gate_w = jax.random.normal(k1, (E, D), dtype=jnp.float32) * (1.0 / np.sqrt(D))
        gate_b = jnp.zeros((E,), dtype=jnp.float32)
        weight1 = jax.random.uniform(k2, (E, D + 1, H), dtype=jnp.float32, minval=-1.0, maxval=1.0) * (1.0 / np.sqrt(D + 1))
        weight2 = jax.random.uniform(k3, (E, H + 1, O), dtype=jnp.float32, minval=-1.0, maxval=1.0) * (1.0 / np.sqrt(H + 1))
        return {'x': x, 'gate_w': gate_w, 'gate_b': gate_b, 'weight1': weight1, 'weight2': weight2}
    _L3_ffn_all = _L3_ffn_setup()
    _L3_ffn_in = {k: v for k, v in _L3_ffn_all.items() if k in ('gate_w', 'gate_b', 'weight1', 'weight2')}
    del _L3_ffn_all
    return {'x': x, 'L0_conv_w_theta': _L0_conv_in['w_theta'], 'L0_conv_w_phi': _L0_conv_in['w_phi'], 'L0_conv_w_g': _L0_conv_in['w_g'], 'L0_conv_w_last': _L0_conv_in['w_last'], 'L1_conv_w_d': _L1_conv_in['w_d'], 'L1_conv_b_d': _L1_conv_in['b_d'], 'L1_conv_w_u': _L1_conv_in['w_u'], 'L1_conv_b_u': _L1_conv_in['b_u'], 'L1_conv_w_r': _L1_conv_in['w_r'], 'L1_conv_b_r': _L1_conv_in['b_r'], 'L1_conv_w_l': _L1_conv_in['w_l'], 'L1_conv_b_l': _L1_conv_in['b_l'], 'L2_attn_Wq': _L2_attn_in['Wq'], 'L2_attn_Wk': _L2_attn_in['Wk'], 'L2_attn_Wv': _L2_attn_in['Wv'], 'L2_attn_Wu': _L2_attn_in['Wu'], 'L2_attn_bu': _L2_attn_in['bu'], 'L2_ffn_sigma': _L2_ffn_in['sigma'], 'L2_ffn_phi': _L2_ffn_in['phi'], 'L2_ffn_M_u': _L2_ffn_in['M_u'], 'L2_ffn_M_phi_plus': _L2_ffn_in['M_phi_plus'], 'L2_ffn_M_phi_minus': _L2_ffn_in['M_phi_minus'], 'L2_ffn_log_weights': _L2_ffn_in['log_weights'], 'L2_ffn_gumbel': _L2_ffn_in['gumbel'], 'L3_attn_Wq': _L3_attn_in['Wq'], 'L3_attn_bq': _L3_attn_in['bq'], 'L3_attn_Wk': _L3_attn_in['Wk'], 'L3_attn_bk': _L3_attn_in['bk'], 'L3_attn_Wv': _L3_attn_in['Wv'], 'L3_attn_bv': _L3_attn_in['bv'], 'L3_attn_Wo': _L3_attn_in['Wo'], 'L3_attn_bo': _L3_attn_in['bo'], 'L3_ffn_gate_w': _L3_ffn_in['gate_w'], 'L3_ffn_gate_b': _L3_ffn_in['gate_b'], 'L3_ffn_weight1': _L3_ffn_in['weight1'], 'L3_ffn_weight2': _L3_ffn_in['weight2']}

def reference(x, L0_conv_w_theta, L0_conv_w_phi, L0_conv_w_g, L0_conv_w_last, L1_conv_w_d, L1_conv_b_d, L1_conv_w_u, L1_conv_b_u, L1_conv_w_r, L1_conv_b_r, L1_conv_w_l, L1_conv_b_l, L2_attn_Wq, L2_attn_Wk, L2_attn_Wv, L2_attn_Wu, L2_attn_bu, L2_ffn_sigma, L2_ffn_phi, L2_ffn_M_u, L2_ffn_M_phi_plus, L2_ffn_M_phi_minus, L2_ffn_log_weights, L2_ffn_gumbel, L3_attn_Wq, L3_attn_bq, L3_attn_Wk, L3_attn_bk, L3_attn_Wv, L3_attn_bv, L3_attn_Wo, L3_attn_bo, L3_ffn_gate_w, L3_ffn_gate_b, L3_ffn_weight1, L3_ffn_weight2):
    import jax
    import jax.numpy as jnp

    def _L0_conv_ref(x, w_theta, w_phi, w_g, w_last):
        import jax, jax.numpy as jnp
        import numpy as np
        B, C, H, W = x.shape
        xf = x.reshape(B, C, H * W)
        theta = jnp.einsum('kc,bcn->bkn', w_theta, xf)
        phi = jnp.einsum('kc,bcn->bkn', w_phi, xf)
        g = jnp.einsum('kc,bcn->bkn', w_g, xf)
        attn = jax.nn.softmax(jnp.einsum('bkn,bkm->bnm', theta, phi), axis=-1)
        y = jnp.einsum('bnm,bkm->bkn', attn, g)
        out = jnp.einsum('ck,bkn->bcn', w_last, y).reshape(B, C, H, W)
        return out + x

    def _L1_conv_ref(x, w_d, b_d, w_u, b_u, w_r, b_r, w_l, b_l):
        import jax, jax.numpy as jnp
        import numpy as np
        import math
        B, C, H, W = (16, 64, 36, 100)
        K = 9
        PAD = 4

        def _conv1d(x, w, b):
            y = jax.lax.conv_general_dilated(x, w, window_strides=(1,), padding=[(PAD, PAD)], dimension_numbers=('NCH', 'OIH', 'NCH'))
            return y + b[None, :, None]

        def _pass_fwd(out, w, b, axis):
            rows = jnp.moveaxis(out, axis, 0)

            def step(carry, x):
                new = x + jax.nn.relu(_conv1d(carry, w, b))
                return (new, new)
            _, updated = jax.lax.scan(step, rows[0], rows[1:])
            res = jnp.concatenate([rows[:1], updated], axis=0)
            return jnp.moveaxis(res, 0, axis)

        def _pass_bwd(out, w, b, axis):
            rows = jnp.moveaxis(out, axis, 0)
            L = rows.shape[0]

            def step(carry, x):
                new = x + jax.nn.relu(_conv1d(carry, w, b))
                return (new, new)
            xs = rows[1:L - 1][::-1]
            _, updated = jax.lax.scan(step, rows[L - 1], xs)
            res = jnp.concatenate([rows[:1], updated[::-1], rows[L - 1:]], axis=0)
            return jnp.moveaxis(res, 0, axis)
        out = _pass_fwd(x, w_d, b_d, axis=2)
        out = _pass_bwd(out, w_u, b_u, axis=2)
        out = _pass_fwd(out, w_r, b_r, axis=3)
        out = _pass_bwd(out, w_l, b_l, axis=3)
        return out

    def _L2_attn_ref(x, Wq, Wk, Wv, Wu, bu):
        import jax, jax.numpy as jnp
        import numpy as np
        EMB, HEADS, K = (64, 8, 32)
        b, t, e = x.shape
        h, k = (HEADS, K)
        tp = t + k - 1
        scale = e ** 0.25
        xp = jnp.pad(x, ((0, 0), (k - 1, 0), (0, 0)))
        q = (x @ Wq.T).reshape(b, t, h, e) / scale
        kk = (xp @ Wk.T).reshape(b, tp, h, e) / scale
        v = (xp @ Wv.T).reshape(b, tp, h, e)
        idx = jnp.arange(t)[:, None] + jnp.arange(k)[None, :]
        kw = kk[:, idx]
        vw = v[:, idx]
        dot = jnp.einsum('bthe,btkhe->bthk', q, kw)
        attn = jax.nn.softmax(dot, axis=-1)
        out = jnp.einsum('bthk,btkhe->bthe', attn, vw)
        out = out.reshape(b, t, h * e)
        return out @ Wu.T + bu

    def _L2_ffn_ref(x, sigma, phi, M_u, M_phi_plus, M_phi_minus, log_weights, gumbel):
        import jax, jax.numpy as jnp
        import numpy as np
        PADDED_SL = 4096
        TEMPERATURE = 1.0
        SIGMA_POW = 0.25

        def _stu_conv(phi, u, n):
            b, sl, d = u.shape
            sgn = jnp.where(jnp.arange(sl) % 2 == 0, 1.0, -1.0).astype(u.dtype)
            sgn3 = sgn[None, :, None]
            Vf = jnp.fft.rfft(phi, n=n, axis=0)
            Uf_p = jnp.fft.rfft(u, n=n, axis=1)
            Uf_m = jnp.fft.rfft(u * sgn3, n=n, axis=1)
            U_plus = jnp.fft.irfft(Vf[None, :, :, None] * Uf_p[:, :, None, :], n=n, axis=1)[:, :sl]
            U_minus = jnp.fft.irfft(Vf[None, :, :, None] * Uf_m[:, :, None, :], n=n, axis=1)[:, :sl]
            U_minus = U_minus * sgn[None, :, None, None]
            return (U_plus, U_minus)

        def _compute_spectral(u, sigma, phi, Mpp, Mpm):
            U_plus, U_minus = _stu_conv(phi, u, PADDED_SL)
            s = sigma ** SIGMA_POW
            out = jnp.einsum('btkd,k,kde->bte', U_plus, s, Mpp)
            out = out + jnp.einsum('btkd,k,kde->bte', U_minus, s, Mpm)
            return out

        def _compute_ar_u(Mu, u):
            sl = u.shape[1]
            out = jnp.zeros(u.shape[:2] + (Mu.shape[-1],), dtype=u.dtype)
            for i in range(Mu.shape[0]):
                ui = jnp.pad(u, ((0, 0), (i, 0), (0, 0)))[:, :sl]
                out = out + jnp.einsum('btd,de->bte', ui, Mu[i])
            return out

        def _stu(u, sigma, phi, Mu, Mpp, Mpm):
            return _compute_spectral(u, sigma, phi, Mpp, Mpm) + _compute_ar_u(Mu, u)
        T = x.shape[1]
        outs = []
        for i, frac in enumerate((1, 2, 4, 8)):
            xi = x[:, :T // frac]
            si = _stu(xi, sigma, phi, M_u[i], M_phi_plus[i], M_phi_minus[i])
            si = jnp.pad(si, ((0, 0), (0, T - si.shape[1]), (0, 0)))
            outs.append(si)
        y_soft = jax.nn.softmax((log_weights + gumbel) / TEMPERATURE)
        y_hard = jax.nn.one_hot(jnp.argmax(y_soft), 4, dtype=y_soft.dtype)
        weights = y_hard - jax.lax.stop_gradient(y_soft) + y_soft
        stacked = jnp.stack(outs, axis=-1)
        return jnp.sum(stacked * weights, axis=-1)

    def _L3_attn_ref(Q, Wq, bq, Wk, bk, Wv, bv, Wo, bo):
        import jax, jax.numpy as jnp
        import numpy as np
        BS, L, D_MODEL, N_HEADS = (8, 8192, 64, 8)
        HEAD_DIM = D_MODEL // N_HEADS
        EPS = 1e-05
        bs, seq, _ = Q.shape
        q = (Q @ Wq + bq).reshape(bs, seq, N_HEADS, HEAD_DIM)
        k = (Q @ Wk + bk).reshape(bs, seq, N_HEADS, HEAD_DIM)
        v = (Q @ Wv + bv).reshape(bs, seq, N_HEADS, HEAD_DIM)
        phi_q = jax.nn.elu(q) + 1.0
        phi_k = jax.nn.elu(k) + 1.0
        KV = jnp.einsum('blhd,blhm->bhdm', phi_k, v)
        K_sum = phi_k.sum(axis=1)
        Z = 1.0 / (jnp.einsum('blhd,bhd->blh', phi_q, K_sum) + EPS)
        V_new = jnp.einsum('blhd,bhdm->blhm', phi_q, KV) * Z[..., None]
        out = V_new.reshape(bs, seq, N_HEADS * HEAD_DIM) @ Wo + bo
        return out

    def _L3_ffn_ref(x, gate_w, gate_b, weight1, weight2):
        import jax, jax.numpy as jnp
        import numpy as np
        B, S, D, E, H, O, K = (256, 1024, 64, 32, 256, 64, 8)
        Bn, Sn, Dn = x.shape
        logits = jnp.einsum('bsd,ed->bse', x, gate_w) + gate_b
        probs = jax.nn.softmax(logits, axis=1)
        vals, idx = jax.lax.top_k(probs.transpose(0, 2, 1), K)
        topv = vals.transpose(0, 2, 1)
        topi = idx.transpose(0, 2, 1)
        flat_idx = topi.reshape(Bn, K * E)
        gathered = jnp.take_along_axis(x, flat_idx[:, :, None], axis=1)
        gathered = gathered.reshape(Bn, K, E, Dn)
        pooled = jnp.einsum('bked,bke->bed', gathered, topv)
        ones = jnp.ones((E, Bn, 1), dtype=x.dtype)
        h = jnp.concatenate([pooled.transpose(1, 0, 2), ones], axis=-1)
        h = jax.nn.gelu(jnp.einsum('ebd,edh->ebh', h, weight1), approximate=False)
        h = jnp.concatenate([h, ones], axis=-1)
        out = jnp.einsum('ebh,eho->ebo', h, weight2)
        out = out.transpose(1, 0, 2)
        weighted = jnp.einsum('beo,bke->bkeo', out, topv).reshape(Bn, K * E, O)
        outputs = jnp.zeros((Bn, Sn, O), dtype=x.dtype)
        outputs = outputs.at[jnp.arange(Bn)[:, None], flat_idx].add(weighted)
        return outputs

    def _gn(v, G=32, eps=1e-05):
        B_, C_, H_, W_ = v.shape
        g = v.reshape(B_, G, C_ // G, H_, W_)
        m = jnp.mean(g, axis=(2, 3, 4), keepdims=True)
        s = jnp.var(g, axis=(2, 3, 4), keepdims=True)
        return ((g - m) / jnp.sqrt(s + eps)).reshape(v.shape)

    def _ln_c(v, eps=1e-06):
        m = jnp.mean(v, axis=1, keepdims=True)
        s = jnp.var(v, axis=1, keepdims=True)
        return (v - m) / jnp.sqrt(s + eps)

    def _ln_t(v, eps=1e-05):
        m = jnp.mean(v, axis=-1, keepdims=True)
        s = jnp.var(v, axis=-1, keepdims=True)
        return (v - m) / jnp.sqrt(s + eps)

    def _to_tokens(v):
        B_, C_, H_, W_ = v.shape
        return v.reshape(B_, C_, H_ * W_).transpose(0, 2, 1)

    def _from_tokens(t, like):
        B_, C_, H_, W_ = like.shape
        return t.transpose(0, 2, 1).reshape(B_, C_, H_, W_)
    x = _L0_conv_ref(x, L0_conv_w_theta, L0_conv_w_phi, L0_conv_w_g, L0_conv_w_last)
    x = _L1_conv_ref(x, L1_conv_w_d, L1_conv_b_d, L1_conv_w_u, L1_conv_b_u, L1_conv_w_r, L1_conv_b_r, L1_conv_w_l, L1_conv_b_l)
    t = _to_tokens(x)
    t = t + _L2_attn_ref(_ln_t(t), L2_attn_Wq, L2_attn_Wk, L2_attn_Wv, L2_attn_Wu, L2_attn_bu)
    t = t + _L2_ffn_ref(_ln_t(t), L2_ffn_sigma, L2_ffn_phi, L2_ffn_M_u, L2_ffn_M_phi_plus, L2_ffn_M_phi_minus, L2_ffn_log_weights, L2_ffn_gumbel)
    t = t + _L3_attn_ref(_ln_t(t), L3_attn_Wq, L3_attn_bq, L3_attn_Wk, L3_attn_bk, L3_attn_Wv, L3_attn_bv, L3_attn_Wo, L3_attn_bo)
    t = t + _L3_ffn_ref(_ln_t(t), L3_ffn_gate_w, L3_ffn_gate_b, L3_ffn_weight1, L3_ffn_weight2)
    x = _from_tokens(t, x)
    return x

_drawn_inputs = setup_inputs


def setup_inputs(seed=0):
    import zlib

    import numpy as np

    out = dict(_drawn_inputs(seed))
    spreads = {'L2_attn_bu': (0.0, 0.1), 'L2_ffn_log_weights': (1.0, 0.2), 'L3_ffn_gate_b': (0.0, 2.0)}
    factors = {'L1_conv_b_d': 3.847,
     'L1_conv_b_u': 4.194,
     'L1_conv_b_r': 3.713,
     'L1_conv_b_l': 3.869,
     'L3_attn_Wq': 4.287,
     'L3_attn_bq': 200.0,
     'L3_attn_bk': 200.0,
     'L3_attn_bv': 7.553,
     'L3_attn_bo': 8.0,
     'L3_ffn_gate_w': 8.0,
     'L3_ffn_weight1': 8.0,
     'L3_ffn_weight2': 8.0}
    for name, (base, spread) in spreads.items():
        noise = np.random.default_rng([zlib.crc32(name.encode()), seed]).standard_normal(out[name].shape)
        drawn = base * np.exp(spread * noise) if base else spread * noise
        out[name] = jnp.asarray(drawn.astype(out[name].dtype))
    for name, factor in factors.items():
        out[name] = (out[name] * factor).astype(out[name].dtype)
    return out
```

```python
import numpy as np
from contextlib import ExitStack

import concourse.bass as bass
from concourse import mybir
from concourse.alu_op_type import AluOpType as ALU

F32 = mybir.dt.float32
BF16 = mybir.dt.bfloat16
ACT = mybir.ActivationFunctionType
AX = mybir.AxisListType
ds = bass.ds

B, C, H, W = 8, 64, 32, 32
T = H * W
P = 2 * C
G = B // 2
HALF = (slice(0, C), slice(C, P))
BANK = 512

TAPS = 9
PAIRS = W // 2
PADP = 2
ROWP = PAIRS + 2 * PADP
SHIFTS = 2 * PADP + 1


class Memory:
    pass


def open_pools(nc, ctx):
    def sb(name, shape, dt=F32):
        return ctx.enter_context(nc.sbuf_tensor(name, shape, dt))

    def pb(name, shape, dt=F32):
        return ctx.enter_context(nc.psum_tensor(name, shape, dt))

    def sem(name):
        return nc.alloc_semaphore(name=name)

    return sb, pb, sem


def setup_stage(nc, m, ins):
    with ExitStack() as ctx:
        sb, pb, sem = open_pools(nc, ctx)
        NP = TAPS + 2
        raw = sb("conv_raw", [C, 4, C * TAPS])
        padded = sb("conv_padded", [C, 4, NP, C])
        turned = [pb(f"conv_turned{i}", [P, SHIFTS, 2, C]) for i in range(2)]
        x_in, w_in, ident_ok, zeroed = sem("x_in"), sem("w_in"), sem("ident_ok"), sem("pads_zeroed")
        pad_ok, turned_ok, taken = sem("taps_padded"), sem("taps_turned"), sem("taps_taken")
        const_ok = sem("const_ok")
        with nc.Block() as block:
            @block.sync
            def _(sp):
                for n, name in enumerate(("d", "u", "r", "l")):
                    sp.dma_start(raw[:, n, :], ins["L1_conv_w_" + name].rearrange("o i k -> o (i k)")).then_inc(w_in, 16)
                for p in range(2):
                    for g in range(G):
                        sp.dma_start(m.x[HALF[p], g, :], ins["x"][2 * g + p].rearrange("c h w -> c (h w)")).then_inc(x_in, 16)
                sp.wait_ge(x_in, 16 * B)

            @block.scalar
            def _(act):
                for n, name in enumerate(("d", "u", "r", "l")):
                    for p in range(2):
                        act.dma_start(m.conv_bias[HALF[p], n:n + 1], ins["L1_conv_b_" + name].rearrange("(c a) -> c a", a=1)).then_inc(w_in, 16)
                act.dma_start(m.w_theta[:, :], ins["L0_conv_w_theta"]).then_inc(w_in, 16)
                act.dma_start(m.w_phi[:, :], ins["L0_conv_w_phi"]).then_inc(w_in, 16)
                act.dma_start(m.w_g[:, :], ins["L0_conv_w_g"]).then_inc(w_in, 16)
                act.dma_start(m.w_last[:, :], ins["L0_conv_w_last"]).then_inc(w_in, 16)
                act.wait_ge(w_in, 16 * 16)

            @block.gpsimd
            def _(pool):
                nc.gpsimd.memset(m.ident[:, :], 0.0).then_inc(zeroed, 1)
                nc.gpsimd.memset(m.average[:, :], 0.0).then_inc(zeroed, 1)
                nc.gpsimd.memset(padded[:, :, 0, :], 0.0).then_inc(pad_ok, 1)
                nc.gpsimd.memset(padded[:, :, NP - 1, :], 0.0).then_inc(pad_ok, 1)
                pool.wait_ge(zeroed, 2)
                nc.gpsimd.affine_select(out=m.ident[:, :], in_=m.ident[:, :], compare_op=ALU.not_equal, fill=1.0,
                                        base=0, pattern=[[-1, P]], channel_multiplier=1).then_inc(ident_ok, 1)
                nc.gpsimd.memset(m.rows[:, :, :, :], 0.0).then_inc(zeroed, 1)
                nc.gpsimd.memset(m.cols[:, :, :, :], 0.0).then_inc(zeroed, 1)
                pool.wait_ge(zeroed, 4)
                for p in range(2):
                    nc.gpsimd.memset(m.average[HALF[p], p * C:(p + 1) * C], 1.0 / C).then_inc(const_ok, 1)

            @block.vector
            def _(dve):
                nc.vector.memset(m.eps[:, :], 1e-5)
                dve.wait_ge(w_in, 16 * 16)
                for n in range(4):
                    nc.vector.tensor_copy(padded[:, n, 1:NP - 1, :],
                                          raw[:, n, :].rearrange("o (i k) -> o k i", k=TAPS)).then_inc(pad_ok, 1)
                for n in range(4):
                    dve.wait_ge(turned_ok, n + 1)
                    nc.vector.tensor_copy(m.toeplitz[:, n, :, :], turned[n % 2][:, :, :, :].rearrange("p s a c -> p s (a c)")).then_inc(taken, 1)
                dve.wait_ge(ident_ok, 1)
                dve.wait_ge(const_ok, 2)
                nc.vector.tensor_tensor(m.centre[:, :], m.ident[:, :], m.average[:, :], ALU.subtract)
                nc.vector.tensor_copy(m.ident_bf[:, :], m.ident[:, :])

            @block.tensor
            def _(pe):
                pe.wait_ge(ident_ok, 1)
                pe.wait_ge(pad_ok, 6)
                for n in range(4):
                    if n >= 2:
                        pe.wait_ge(taken, n - 1)
                    for s in range(SHIFTS):
                        for po in range(2):
                            first = 2 * s - po + 1
                            last = nc.tensor.transpose(turned[n % 2][:, s, po, :],
                                                       padded[:, n, first:first + 2, :].rearrange("o t i -> o (t i)"),
                                                       m.ident[0:C, 0:C])
                    last.then_inc(turned_ok, 1)


def nonlocal_stage(nc, m):
    NB = 2 * (T // P)
    KT = T // P
    with ExitStack() as ctx:
        sb, pb, sem = open_pools(nc, ctx)
        last_t = sb("w_last_t", [C // 2, C])
        qk_w = sb("qk_w", [P, P])
        zo_w = sb("zo_w", [P, P])
        xg = sb("xg", [P, T])
        qg = sb("qg", [P, T])
        zg = sb("zg", [P, KT, P])
        probs = [sb(f"probs{i}", [P, T]) for i in range(2)]
        probs_t = [sb(f"probs_t{i}", [P, KT, P]) for i in range(2)]
        out_n = [sb(f"out_n{i}", [P, 2, C]) for i in range(2)]
        nmax = sb("nmax", [P, 4])
        rsum = sb("rsum", [P, 4])
        rinv = sb("rinv", [P, 4])
        scores = [pb(f"scores{i}", [P, T]) for i in range(2)]
        turned = pb("turned", [P, KT, P])
        out_ps = pb("out_ps", [P, BANK])[:, 0:P].rearrange("p (a c) -> p a c", a=2)
        out_t = pb("out_t", [P, BANK])[:, 0:P]
        wl_t, wl_c, fused, fused_c = sem("wl_t"), sem("wl_c"), sem("fused"), sem("fused_c")
        placed = sem("x_placed")
        xg_ok, proj_ok, qa, qd = sem("xg_ok"), sem("proj_ok"), sem("q_taken"), sem("z_taken")
        s_score, s_max, s_exp, s_tr = sem("score_ready"), sem("max_ready"), sem("probs_ready"), sem("turned_ready")
        s_ta, s_td, s_pv, s_inv = sem("turned_taken_act"), sem("turned_taken_dve"), sem("out_ready"), sem("inv_ready")
        s_norm, s_ot, s_add = sem("out_normed"), sem("out_turned"), sem("out_added")
        HK = KT // 2

        with nc.Block() as block:
            @block.gpsimd
            def _(pool):
                def place(par, p):
                    nc.gpsimd.tensor_copy(
                        m.rows[HALF[par], :, p::2, PADP:PADP + PAIRS].rearrange("c h g q -> c g h q"),
                        m.x[HALF[p], :, :].rearrange("c g (h q a) -> c g h q a", h=H, a=2)[:, :, :, :, par]).then_inc(placed, 1)
                nc.gpsimd.memset(qk_w[:, :], 0.0).then_inc(fused_c, 1)
                nc.gpsimd.memset(zo_w[:, :], 0.0).then_inc(fused_c, 1)
                nc.gpsimd.tensor_copy(xg[:, :], m.x[:, 0, :]).then_inc(xg_ok, 1)
                pool.wait_ge(xg_ok, 1)
                for par in range(2):
                    for p in range(2):
                        place(par, p)
                        pool.wait_ge(placed, 2 * par + p + 1)
                with pool.Fori(1, G) as g:
                    pool.wait_ge(s_score, g * NB)
                    nc.gpsimd.tensor_copy(xg[:, :], m.x[:, ds(g, 1), :].rearrange("p a t -> p (a t)")).then_inc(xg_ok, 1)

            @block.tensor
            def _(pe):
                nc.tensor.transpose(out_t[0:C // 2, 0:C], m.w_last[:, :], m.ident[0:C, 0:C]).then_inc(wl_t, 1)
                for p in range(2):
                    nc.tensor.matmul(scores[0][HALF[p], 0:C], m.w_theta[:, :], m.w_phi[:, :], start=True, stop=True).then_inc(fused, 1)
                pe.wait_ge(wl_c, 1)
                for p in range(2):
                    nc.tensor.matmul(scores[1][HALF[p], 0:C], m.w_g[:, :], last_t[:, :], start=True, stop=True).then_inc(fused, 1)
                pe.wait_ge(fused_c, 6)
                with pe.Fori(0, G) as g:
                    pe.wait_ge(xg_ok, g + 1)
                    for c in range(T // BANK):
                        mm = nc.tensor.matmul(scores[0][:, c * BANK:(c + 1) * BANK], qk_w[:, :], xg[:, c * BANK:(c + 1) * BANK], start=True, stop=True)
                    mm.then_inc(proj_ok, 1)
                    for k in range(KT):
                        mm = nc.tensor.matmul(scores[1][:, k * P:(k + 1) * P], xg[:, k * P:(k + 1) * P], zo_w[:, :], start=True, stop=True)
                    mm.then_inc(proj_ok, 1)
                    pe.wait_ge(qa, g + 1)
                    pe.wait_ge(qd, g + 1)

                    def score(i):
                        if i >= 2:
                            pe.wait_ge(s_exp, g * NB + (i - 1))
                        p, j, par = i // 8, (i // 2) % 4, i % 2
                        q = qg[HALF[p], 256 * j + par:256 * (j + 1):2]
                        for c in range(T // BANK):
                            mm = nc.tensor.matmul(scores[i % 2][:, c * BANK:(c + 1) * BANK], q, xg[HALF[p], c * BANK:(c + 1) * BANK], start=True, stop=True)
                        mm.then_inc(s_score, 1)

                    def turn(i):
                        pe.wait_ge(s_exp, g * NB + (i + 1))
                        if i >= 1:
                            pe.wait_ge(s_ta, g * NB + i)
                            pe.wait_ge(s_td, g * NB + i)
                        for k in range(KT):
                            mm = nc.tensor.transpose(turned[:, k, :], probs[i % 2][:, k * P:(k + 1) * P], m.ident[:, :])
                            if k == HK - 1 or k == KT - 1:
                                mm.then_inc(s_tr, 1)

                    def attend(i):
                        p, par = i // 8, i % 2
                        pe.wait_ge(s_ta, g * NB + (i + 1))
                        pe.wait_ge(s_td, g * NB + (i + 1))
                        if i >= 1:
                            pe.wait_ge(s_norm, g * NB + i)
                        for k in range(KT):
                            mm = nc.tensor.matmul(out_ps[:, par, :], probs_t[i % 2][:, k, :], zg[:, k, p * C:(p + 1) * C], start=(k == 0), stop=(k == KT - 1))
                        mm.then_inc(s_pv, 1)

                    def turn_out(n):
                        pe.wait_ge(s_norm, g * NB + (2 * n + 2))
                        if n >= 1:
                            pe.wait_ge(s_add, g * (NB // 2) + n)
                        nc.tensor.transpose(out_t[:, :], out_n[n % 2][:, :, :].rearrange("p a c -> p (a c)"), m.ident[:, :]).then_inc(s_ot, 1)

                    score(0)
                    score(1)
                    for i in range(NB):
                        turn(i)
                        if i + 2 < NB:
                            score(i + 2)
                        attend(i)
                        if i >= 2 and i % 2 == 0:
                            turn_out(i // 2 - 1)
                    turn_out(NB // 2 - 1)
                    pe.wait_ge(s_add, (g + 1) * (NB // 2))

            @block.scalar
            def _(act):
                act.wait_ge(fused, 2)
                act.wait_ge(fused_c, 2)
                for p in range(2):
                    nc.scalar.activation(qk_w[HALF[p], p * C:(p + 1) * C], scores[0][HALF[p], 0:C], ACT.Copy).then_inc(fused_c, 1)
                with act.Fori(0, G) as g:
                    act.wait_ge(proj_ok, 2 * g + 1)
                    nc.scalar.activation(qg[:, :], scores[0][:, :], ACT.Copy).then_inc(qa, 1)

                    def exp(i):
                        act.wait_ge(s_max, g * NB + (i + 1))
                        if i >= 2:
                            act.wait_ge(s_tr, 2 * (g * NB) + 2 * (i - 1))
                        nc.scalar.activation(probs[i % 2][:, :], scores[i % 2][:, :], ACT.Exp, bias=nmax[:, i % 4:i % 4 + 1],
                                             accum_out=rsum[:, i % 4:i % 4 + 1]).then_inc(s_exp, 1)

                    def take(i):
                        act.wait_ge(s_tr, 2 * (g * NB) + 2 * (i + 1))
                        if i >= 2:
                            act.wait_ge(s_pv, g * NB + (i - 1))
                        nc.scalar.activation(probs_t[i % 2][:, HK:KT, :], turned[:, HK:KT, :], ACT.Copy).then_inc(s_ta, 1)

                    exp(0)
                    exp(1)
                    for i in range(NB):
                        take(i)
                        if i + 2 < NB:
                            exp(i + 2)

            @block.vector
            def _(dve):
                dve.wait_ge(wl_t, 1)
                nc.vector.tensor_copy(last_t[:, :], out_t[0:C // 2, 0:C]).then_inc(wl_c, 1)
                dve.wait_ge(fused, 4)
                dve.wait_ge(fused_c, 2)
                for p in range(2):
                    nc.vector.tensor_copy(zo_w[HALF[p], p * C:(p + 1) * C], scores[1][HALF[p], 0:C]).then_inc(fused_c, 1)
                dve.wait_ge(placed, 4)
                with dve.Fori(0, G) as g:
                    dve.wait_ge(proj_ok, 2 * g + 2)
                    nc.vector.tensor_copy(zg[:, :, :].rearrange("p k c -> p (k c)"), scores[1][:, :]).then_inc(qd, 1)

                    def row_max(i):
                        dve.wait_ge(s_score, g * NB + (i + 1))
                        nc.vector.tensor_reduce(nmax[:, i % 4:i % 4 + 1], scores[i % 2][:, :], axis=AX.X, op=ALU.max, negate=True).then_inc(s_max, 1)

                    def take(i):
                        dve.wait_ge(s_tr, 2 * (g * NB) + (2 * i + 1))
                        if i >= 2:
                            dve.wait_ge(s_pv, g * NB + (i - 1))
                        nc.vector.tensor_copy(probs_t[i % 2][:, 0:HK, :], turned[:, 0:HK, :]).then_inc(s_td, 1)

                    def norm(i):
                        n, par = i // 2, i % 2
                        dve.wait_ge(s_exp, g * NB + (i + 1))
                        nc.vector.reciprocal(rinv[:, i % 4:i % 4 + 1], rsum[:, i % 4:i % 4 + 1]).then_inc(s_inv, 1)
                        dve.wait_ge(s_inv, g * NB + (i + 1))
                        dve.wait_ge(s_pv, g * NB + (i + 1))
                        if n >= 2:
                            dve.wait_ge(s_ot, g * (NB // 2) + (n - 1))
                        nc.vector.tensor_scalar(out_n[n % 2][:, par, :], out_ps[:, par, :], rinv[:, i % 4:i % 4 + 1], None, ALU.mult).then_inc(s_norm, 1)

                    def add(n):
                        p, j = n // 4, n % 4
                        dve.wait_ge(s_ot, g * (NB // 2) + (n + 1))
                        dst = m.rows[:, 8 * j:8 * j + 8, ds(2 * g + p, 1), PADP:PADP + PAIRS]
                        nc.vector.tensor_tensor(dst, out_t[:, :].rearrange("p (h a q) -> p h a q", h=8, a=1), dst, ALU.add).then_inc(s_add, 1)

                    row_max(0)
                    row_max(1)
                    for i in range(NB):
                        take(i)
                        if i + 2 < NB:
                            row_max(i + 2)
                        norm(i)
                        if i >= 2 and i % 2 == 0:
                            add(i // 2 - 1)
                    add(NB // 2 - 1)


def conv_passes(nc, m, grid, first, tag):
    LINES = H
    FWD, BWD = LINES - 1, LINES - 2
    with ExitStack() as ctx:
        sb, pb, sem = open_pools(nc, ctx)
        conv = [pb(f"conv{tag}{k}", [P, BANK])[:, 0:B * PAIRS].rearrange("p (b q) -> p b q", q=PAIRS) for k in range(2)]
        running = [sb(f"running{tag}{k}", [P, B, ROWP]) for k in range(2)]
        line_ok, conv_ok, saved, padded = sem("line_ready" + tag), sem("conv_ready" + tag), sem("line_saved" + tag), sem("running_padded" + tag)

        def steps(eng, step):
            step(1, 1, first, 1)
            with eng.Fori(1, (FWD + 1) // 2) as k:
                for odd in range(2):
                    step(k * 2 + odd, odd, first, k * 2 + odd)
            with eng.Fori((FWD + 1) // 2, (FWD + BWD + 1) // 2) as k:
                for odd in range(2):
                    step(k * 2 + odd, odd, first + 1, k * (-2) + (2 * FWD - odd))

        def at(line):
            return grid[:, ds(line, 1), :, PADP:PADP + PAIRS].rearrange("p l b q -> p (l b) q")

        with nc.Block() as block:
            @block.tensor
            def _(pe):
                def step(n, odd, wn, line):
                    if not isinstance(n, int):
                        pe.wait_ge(saved, n - 1)
                    nc.tensor.matmul(conv[odd][:, :, :], m.ident[:, :], at(line), start=True, stop=False)
                    pe.wait_ge(line_ok, n)
                    for s in range(SHIFTS):
                        mm = nc.tensor.matmul(conv[odd][:, :, :], m.toeplitz[:, wn, s, :], running[1 - odd][:, :, s:s + PAIRS],
                                              start=False, stop=(s == SHIFTS - 1))
                    mm.then_inc(conv_ok, 1)
                steps(pe, step)

            @block.vector
            def _(dve):
                for k in range(2):
                    nc.vector.memset(running[k][:, :, :], 0.0).then_inc(padded, 1)
                dve.wait_ge(padded, 2)
                nc.vector.tensor_copy(running[0][:, :, :], grid[:, 0, :, :]).then_inc(line_ok, 1)

                def step(n, odd, wn, line):
                    if not isinstance(n, int):
                        dve.wait_ge(saved, n - 1)
                    dve.wait_ge(conv_ok, n)
                    nc.vector.scalar_tensor_tensor(out=running[odd][:, :, PADP:PADP + PAIRS], in0=conv[odd][:, :, :], scalar=m.conv_bias[:, wn:wn + 1],
                                                   in1=at(line), op0=ALU.add, op1=ALU.max).then_inc(line_ok, 1)
                steps(dve, step)

            @block.scalar
            def _(act):
                act.sem_inc(saved, 1)

                def step(n, odd, wn, line):
                    act.wait_ge(line_ok, n + 1)
                    nc.scalar.copy(at(line), running[odd][:, :, PADP:PADP + PAIRS]).then_inc(saved, 1)
                steps(act, step)


def rows_to_cols_stage(nc, m):
    def move(copy, hp, wp):
        src = m.rows[HALF[wp], hp::2, :, PADP:PADP + PAIRS].rearrange("c r b q -> c b q r")
        dst = m.cols[HALF[hp], wp::2, :, PADP:PADP + PAIRS].rearrange("c q b r -> c b q r")
        copy(dst, src)

    with nc.Block() as block:
        @block.vector
        def _(dve):
            move(nc.vector.tensor_copy, 0, 1)
            move(nc.vector.tensor_copy, 1, 0)

        @block.scalar
        def _(act):
            move(nc.scalar.copy, 0, 0)

        @block.gpsimd
        def _(pool):
            move(nc.gpsimd.tensor_copy, 1, 1)


def cols_to_tokens_stage(nc, m):
    def move(copy, hp, p):
        src = m.cols[HALF[hp], :, p::2, PADP:PADP + PAIRS].rearrange("c w g r -> c g r w")
        dst = m.x[HALF[p], :, :].rearrange("c g (r a w) -> c g r a w", a=2, w=W)[:, :, :, hp, :]
        copy(dst, src)

    with nc.Block() as block:
        @block.vector
        def _(dve):
            move(nc.vector.tensor_copy, 0, 1)
            move(nc.vector.tensor_copy, 1, 0)

        @block.scalar
        def _(act):
            move(nc.scalar.copy, 0, 0)

        @block.gpsimd
        def _(pool):
            move(nc.gpsimd.tensor_copy, 1, 1)


def layernorm_stage(nc, m, out_piece, tag, extra=None):
    N = G * T // BANK
    with ExitStack() as ctx:
        sb, pb, sem = open_pools(nc, ctx)
        square = [sb(f"square{tag}{k}", [P, BANK]) for k in range(2)]
        inv = [sb(f"inv{tag}{k}", [P, BANK]) for k in range(2)]
        centred = [pb(f"centred{tag}{k}", [P, BANK]) for k in range(2)]
        var = [pb(f"var{tag}{k}", [P, BANK]) for k in range(2)]
        cen_ok, sq_ok, var_ok, sd_ok, inv_ok, out_ok = (sem(n + tag) for n in ("centred_ready", "square_ready", "var_ready", "sd_ready", "inv_ready", "normed_ready"))
        with nc.Block() as block:
            @block.tensor
            def _(pe):
                with pe.Fori(0, N // 2) as t:
                    for k in range(2):
                        nc.tensor.matmul(centred[k][:, :], m.centre[:, :], m.x_flat[:, ds(t * (2 * BANK) + k * BANK, BANK)], start=True, stop=True).then_inc(cen_ok, 1)
                    for k in range(2):
                        pe.wait_ge(sq_ok, t * 2 + (k + 1))
                        nc.tensor.matmul(var[k][:, :], m.average[:, :], square[k][:, :], start=True, stop=True).then_inc(var_ok, 1)
                    pe.wait_ge(out_ok, t * 2 + 2)

            @block.scalar
            def _(act):
                with act.Fori(0, N // 2) as t:
                    for k in range(2):
                        act.wait_ge(cen_ok, t * 2 + (k + 1))
                        nc.scalar.activation(square[k][:, :], centred[k][:, :], ACT.Square).then_inc(sq_ok, 1)
                    for k in range(2):
                        act.wait_ge(var_ok, t * 2 + (k + 1))
                        nc.scalar.activation(square[k][:, :], var[k][:, :], ACT.Sqrt, bias=m.eps[:, 0:1]).then_inc(sd_ok, 1)
                    act.wait_ge(out_ok, t * 2 + 2)

            @block.vector
            def _(dve):
                with dve.Fori(0, N // 2) as t:
                    for k in range(2):
                        dve.wait_ge(sd_ok, t * 2 + (k + 1))
                        nc.vector.reciprocal(inv[k][:, :], square[k][:, :]).then_inc(inv_ok, 1)
                        dve.wait_ge(inv_ok, t * 2 + (k + 1))
                        nc.vector.tensor_tensor(out_piece(t, k), centred[k][:, :].rearrange("p (c n) -> p c n", n=128),
                                                inv[k][:, :].rearrange("p (c n) -> p c n", n=128), ALU.mult).then_inc(out_ok, 1)

            if extra is not None:
                extra(block, out_ok, N)


HEADS = 8
WINDOW = 32
CHUNK = 128
NW = CHUNK // WINDOW
KEYS = 2 * WINDOW
PIECE = WINDOW + CHUNK
CHUNKS = G * T // CHUNK
MASKED = -1e30


def window_setup(nc, m, ins):
    with ExitStack() as ctx:
        sb, pb, sem = open_pools(nc, ctx)
        wq, wk, wv = (sb(n, [C, HEADS, C]) for n in ("win_wq", "win_wk", "win_wv"))
        wu = sb("win_wu", [C, HEADS * C])
        wut = sb("win_wut", [C, HEADS, C])
        mask = sb("win_mask", [P, KEYS])
        qk_ps, vo_ps, t_ps = (pb(n, [P, HEADS, C]) for n in ("qk_ps", "vo_ps", "wut_ps"))
        w_in, t_ok, t_c, qk_ok, vo_ok, zeroed, mk = (sem(n) for n in ("win_w_in", "wut_ready", "wut_taken", "qk_ready", "vo_ready", "win_zeroed", "mask_step"))
        with nc.Block() as block:
            @block.sync
            def _(sp):
                for dst, n in ((wq, "Wq"), (wk, "Wk"), (wv, "Wv")):
                    sp.dma_start(dst[:, :, :], ins["L2_attn_" + n].rearrange("(h e) c -> e h c", h=HEADS)).then_inc(w_in, 16)
                sp.dma_start(wu[:, :], ins["L2_attn_Wu"]).then_inc(w_in, 16)
                for p in range(2):
                    sp.dma_start(m.win_bias[HALF[p], 0:1], ins["L2_attn_bu"].rearrange("(c a) -> c a", a=1)).then_inc(w_in, 16)
                sp.wait_ge(w_in, 96)

            @block.gpsimd
            def _(pool):
                nc.gpsimd.memset(m.win_qk[:, :, :], 0.0).then_inc(zeroed, 1)
                nc.gpsimd.memset(m.win_vo[:, :, :], 0.0).then_inc(zeroed, 1)
                nc.gpsimd.memset(m.win_x[:, :, :, :], 0.0)
                nc.gpsimd.memset(mask[:, :], 0.0).then_inc(mk, 1)
                pool.wait_ge(mk, 1)
                for q in range(P // WINDOW):
                    rows = mask[q * WINDOW:(q + 1) * WINDOW, :]
                    nc.gpsimd.affine_select(out=rows, in_=rows, compare_op=ALU.is_ge, fill=MASKED, base=-1,
                                            pattern=[[1, KEYS]], channel_multiplier=-1).then_inc(mk, 1)
                    pool.wait_ge(mk, 2 * q + 2)
                    nc.gpsimd.affine_select(out=rows, in_=rows, compare_op=ALU.is_ge, fill=MASKED, base=WINDOW,
                                            pattern=[[-1, KEYS]], channel_multiplier=1).then_inc(mk, 1)
                    pool.wait_ge(mk, 2 * q + 3)
                for n in range(BANK // KEYS):
                    nc.gpsimd.tensor_copy(m.win_mask[:, n * KEYS:(n + 1) * KEYS], mask[:, :])
                nc.gpsimd.memset(m.pieces[:, ::T // CHUNK, 0:WINDOW], 0.0)

            @block.tensor
            def _(pe):
                pe.wait_ge(w_in, 96)
                for h in range(HEADS):
                    mm = nc.tensor.transpose(t_ps[0:C, h, :], wu[:, h * C:(h + 1) * C], m.ident[0:C, 0:C])
                mm.then_inc(t_ok, 1)
                for p in range(2):
                    for h in range(HEADS):
                        mm = nc.tensor.matmul(qk_ps[HALF[p], h, :], wq[:, h, :], wk[:, h, :], start=True, stop=True)
                mm.then_inc(qk_ok, 1)
                pe.wait_ge(t_c, 1)
                for p in range(2):
                    for h in range(HEADS):
                        mm = nc.tensor.matmul(vo_ps[HALF[p], h, :], wv[:, h, :], wut[:, h, :], start=True, stop=True)
                mm.then_inc(vo_ok, 1)

            @block.vector
            def _(dve):
                dve.wait_ge(t_ok, 1)
                nc.vector.tensor_copy(wut[:, :, :], t_ps[0:C, :, :]).then_inc(t_c, 1)
                dve.wait_ge(zeroed, 2)
                dve.wait_ge(qk_ok, 1)
                for p in range(2):
                    nc.vector.tensor_scalar(m.win_qk[HALF[p], :, p * C:(p + 1) * C], qk_ps[HALF[p], :, :], C ** -0.5, None, ALU.mult)
                dve.wait_ge(vo_ok, 1)
                for p in range(2):
                    nc.vector.tensor_copy(m.win_vo[HALF[p], :, p * C:(p + 1) * C], vo_ps[HALF[p], :, :])


def window_norm_stage(nc, m):
    def piece(t, k):
        return m.pieces[:, ds(t * (2 * NW) + k * NW, NW), WINDOW:PIECE]

    def history(block, out_ok, n):
        @block.gpsimd
        def _(pool):
            pool.wait_ge(out_ok, n)
            per = T // CHUNK
            for g in range(G):
                nc.gpsimd.tensor_copy(m.pieces[:, g * per + 1:(g + 1) * per, 0:WINDOW], m.pieces[:, g * per:(g + 1) * per - 1, CHUNK:PIECE])

    layernorm_stage(nc, m, piece, "w", history)


def window_attention_stage(nc, m):
    HG = HEADS // 4
    NT = HG * NW * 2
    with ExitStack() as ctx:
        sb, pb, sem = open_pools(nc, ctx)
        queries = sb("queries", [P, NW, HEADS, WINDOW])
        xt = sb("win_xt", [P, NW, P])
        shifted = sb("shifted", [P, HG, NW, P])
        probs = sb("win_probs", [P, HG, NW, P])
        probs_t = sb("win_probs_t", [P, HG, NW, P])
        heads = sb("win_heads", [P, HG, NW, P])
        heads_t = sb("win_heads_t", [P, HG, NW, P])
        rmax, rsum, rinv = (sb(n, [P, NT]) for n in ("win_max", "win_sum", "win_inv"))
        q_ps = pb("q_ps", [P, HEADS, CHUNK])
        s_ps = pb("s_ps", [P, HG, NW, P])
        t_ps = pb("t_ps", [P, HG, NW, P])
        z_ps = pb("z_ps", [P, HG, NW, P])
        xt_ps, o_ps = q_ps[:, 0:NW, :], z_ps[:, 0, 0, :]
        (win_ok, q_ok, q_act, q_dve, s_ok, xt_ok, xt_c, sub_ok, p_ok, pt_ok, pt_act, pt_dve, z_ok, max_ok, sum_ok, inv_ok, n_ok,
         zt_ok, zt_c, o_ok, o_c) = (sem("w_" + n) for n in (
             "windows", "queries", "queries_act", "queries_dve", "scores", "xt", "xt_taken", "shifted", "probs", "probs_turned", "pt_act", "pt_dve",
             "heads", "max", "sum", "inv", "normed", "heads_turned", "heads_taken", "out", "added"))
        LAST = CHUNKS - 1

        def pipeline(eng, body):
            body(0)
            with eng.Fori(1, LAST - 1) as i:
                body(i)
            body(LAST - 1)
            body(LAST)

        def loops(i, d=0):
            return not isinstance(i, int) or 0 <= i + d <= LAST

        with nc.Block() as block:
            @block.gpsimd
            def _(pool):
                def window(i):
                    if not (isinstance(i, int) and i == 0):
                        pool.wait_ge(s_ok, i)
                        pool.wait_ge(xt_ok, i)
                    for p in range(2):
                        c = m.pieces[HALF[p], ds(i, 1), 0:PIECE]
                        for k in range(2):
                            nc.gpsimd.tensor_copy(m.win_x[HALF[p], k::2, p, :],
                                                  c[:, :, k * WINDOW:k * WINDOW + 2 * KEYS].rearrange("p a (w n) -> p (a w) n", n=KEYS)).then_inc(win_ok, 1)
                window(0)
                with pool.Fori(1, CHUNKS) as i:
                    window(i)

            @block.tensor
            def _(pe):
                def query(i):
                    if not (isinstance(i, int) and i == 0):
                        pe.wait_ge(q_dve, i)
                        pe.wait_ge(q_act, i)
                    x = m.pieces[:, ds(i, 1), WINDOW:PIECE].rearrange("p a n -> p (a n)")
                    for h in range(4, HEADS):
                        mm = nc.tensor.matmul(q_ps[:, h, :], m.win_qk[:, h, :], x, start=True, stop=True)
                    mm.then_inc(q_ok, 1)
                    if not (isinstance(i, int) and i <= 1):
                        pe.wait_ge(xt_c, i)
                    elif i == 1:
                        pe.wait_ge(xt_c, 1)
                    for h in range(4):
                        mm = nc.tensor.matmul(q_ps[:, h, :], m.win_qk[:, h, :], x, start=True, stop=True)
                    mm.then_inc(q_ok, 1)

                def windows_turned(i):
                    pe.wait_ge(q_act, i + 1)
                    pe.wait_ge(win_ok, i * 4 + 4)
                    for w in range(NW):
                        mm = nc.tensor.transpose(xt_ps[:, w, :], m.win_x[:, w, :, :].rearrange("p a n -> p (a n)"), m.ident[:, :])
                    mm.then_inc(xt_ok, 1)

                def scores(i):
                    pe.wait_ge(win_ok, i * 4 + 4)
                    pe.wait_ge(q_act, i + 1)
                    pe.wait_ge(q_dve, i + 1)
                    if not (isinstance(i, int) and i == 0):
                        pe.wait_ge(sub_ok, i * HG)
                    for hg in range(HG):
                        nc.tensor.matmul(s_ps[:, hg, :, :].rearrange("p w n -> p (w n)"), m.ident_bf[:, :], m.win_mask[:, :], start=True, stop=False)
                        for w in range(NW):
                            mm = nc.tensor.matmul(s_ps[:, hg, w, :], queries[:, w, 4 * hg:4 * hg + 4, :].rearrange("p h n -> p (h n)"),
                                                  m.win_x[:, w, :, :].rearrange("p a n -> p (a n)"), start=False, stop=(w == NW - 1))
                    mm.then_inc(s_ok, 1)

                def turn_probs(i):
                    pe.wait_ge(p_ok, i + 1)
                    if not (isinstance(i, int) and i == 0):
                        pe.wait_ge(zt_c, i)
                    for hg in range(HG):
                        for w in range(NW):
                            mm = nc.tensor.transpose(t_ps[:, hg, w, :], probs[:, hg, w, :], m.ident[:, :])
                    mm.then_inc(pt_ok, 1)

                def output(i):
                    pe.wait_ge(zt_c, i + 1)
                    for h in range(HEADS):
                        mm = nc.tensor.matmul(o_ps, m.win_vo[:, h, :], heads_t[:, h // 4, :, (h % 4) * WINDOW:(h % 4 + 1) * WINDOW],
                                              start=(h == 0), stop=(h == HEADS - 1))
                    mm.then_inc(o_ok, 1)

                def attend(i):
                    pe.wait_ge(pt_act, i + 1)
                    pe.wait_ge(pt_dve, i + 1)
                    pe.wait_ge(xt_c, i + 1)
                    if not (isinstance(i, int) and i == 0):
                        pe.wait_ge(o_c, i)
                    for hg in range(HG):
                        for w in range(NW):
                            mm = nc.tensor.matmul(z_ps[:, hg, w, :], probs_t[:, hg, w, :], xt[:, w, :], start=True, stop=True)
                    mm.then_inc(z_ok, 1)

                def turn_heads(i):
                    pe.wait_ge(n_ok, i + 1)
                    for hg in range(HG):
                        for w in range(NW):
                            mm = nc.tensor.transpose(t_ps[:, hg, w, :], heads[:, hg, w, :], m.ident[:, :])
                    mm.then_inc(zt_ok, 1)

                def body(i):
                    if loops(i, 1):
                        scores(i + 1)
                    turn_probs(i)
                    if loops(i, -1):
                        output(i - 1)
                    attend(i)
                    if loops(i, 1):
                        windows_turned(i + 1)
                    if loops(i, 2):
                        query(i + 2)
                    turn_heads(i)

                query(0)
                scores(0)
                windows_turned(0)
                query(1)
                pipeline(pe, body)
                output(LAST)

            @block.scalar
            def _(act):
                def take_queries(i):
                    act.wait_ge(q_ok, i * 2 + 2)
                    if not (isinstance(i, int) and i == 0):
                        act.wait_ge(s_ok, i)
                    nc.scalar.activation(queries[:, :, 0:4, :], q_ps[:, 0:4, :].rearrange("p h (w n) -> p w h n", w=NW), ACT.Copy).then_inc(q_act, 1)

                def take_windows(i):
                    act.wait_ge(xt_ok, i + 1)
                    if not (isinstance(i, int) and i == 0):
                        act.wait_ge(z_ok, i)
                    nc.scalar.activation(xt[:, :, :], xt_ps, ACT.Copy).then_inc(xt_c, 1)

                def exps(i):
                    act.wait_ge(sub_ok, (i + 1) * HG)
                    if not (isinstance(i, int) and i == 0):
                        act.wait_ge(pt_ok, i)
                        act.wait_ge(sum_ok, i)
                    nc.scalar.activation(probs[:, :, :, :], shifted[:, :, :, :], ACT.Exp).then_inc(p_ok, 1)

                def take_probs(i):
                    act.wait_ge(pt_ok, i + 1)
                    nc.scalar.activation(probs_t[:, 0, :, :], t_ps[:, 0, :, :], ACT.Copy).then_inc(pt_act, 1)

                def take_heads(i):
                    act.wait_ge(zt_ok, i + 1)
                    if not (isinstance(i, int) and i == 0):
                        act.wait_ge(o_ok, i)
                    nc.scalar.activation(heads_t[:, :, :, :], t_ps[:, :, :, :], ACT.Copy).then_inc(zt_c, 1)

                def body(i):
                    take_probs(i)
                    if loops(i, 1):
                        exps(i + 1)
                        take_windows(i + 1)
                    if loops(i, 2):
                        take_queries(i + 2)
                    take_heads(i)

                take_queries(0)
                exps(0)
                take_windows(0)
                take_queries(1)
                pipeline(act, body)

            @block.vector
            def _(dve):
                def take_queries(i):
                    dve.wait_ge(q_ok, i * 2 + 1)
                    if not (isinstance(i, int) and i == 0):
                        dve.wait_ge(s_ok, i)
                    nc.vector.tensor_copy(queries[:, :, 4:HEADS, :], q_ps[:, 4:HEADS, :].rearrange("p h (w n) -> p w h n", w=NW)).then_inc(q_dve, 1)

                def shift(i):
                    dve.wait_ge(s_ok, i + 1)
                    nc.vector.tensor_reduce(rmax[:, :], s_ps[:, :, :, :].rearrange("p g w (a n) -> p (g w a) n", a=2), axis=AX.X, op=ALU.max).then_inc(max_ok, 1)
                    dve.wait_ge(max_ok, i + 1)
                    if not (isinstance(i, int) and i == 0):
                        dve.wait_ge(p_ok, i)
                    for hg in range(HG):
                        half = rmax[:, hg * (NT // HG):(hg + 1) * (NT // HG)]
                        nc.vector.tensor_tensor(shifted[:, hg, :, :].rearrange("p w (a n) -> p (w a) n", a=2),
                                                s_ps[:, hg, :, :].rearrange("p w (a n) -> p (w a) n", a=2),
                                                half.to_broadcast([P, NT // HG, KEYS]), ALU.subtract).then_inc(sub_ok, 1)

                def sums(i):
                    dve.wait_ge(p_ok, i + 1)
                    nc.vector.tensor_reduce(rsum[:, :], probs[:, :, :, :].rearrange("p g w (a n) -> p (g w a) n", a=2), axis=AX.X, op=ALU.add).then_inc(sum_ok, 1)
                    dve.wait_ge(sum_ok, i + 1)
                    nc.vector.reciprocal(rinv[:, :], rsum[:, :]).then_inc(inv_ok, 1)

                def take_probs(i):
                    dve.wait_ge(pt_ok, i + 1)
                    nc.vector.tensor_copy(probs_t[:, 1, :, :], t_ps[:, 1, :, :]).then_inc(pt_dve, 1)

                def normalise(i):
                    dve.wait_ge(z_ok, i + 1)
                    dve.wait_ge(inv_ok, i + 1)
                    nc.vector.tensor_tensor(heads[:, :, :, :].rearrange("p g w (a n) -> p (g w a) n", a=2),
                                            z_ps[:, :, :, :].rearrange("p g w (a n) -> p (g w a) n", a=2),
                                            rinv[:, :].to_broadcast([P, NT, C]), ALU.mult).then_inc(n_ok, 1)

                def add(i):
                    dve.wait_ge(o_ok, i + 1)
                    x = m.x_flat[:, ds(i * CHUNK, CHUNK)]
                    nc.vector.scalar_tensor_tensor(out=x, in0=o_ps, scalar=m.win_bias[:, 0:1], in1=x, op0=ALU.add, op1=ALU.add).then_inc(o_c, 1)

                def body(i):
                    sums(i)
                    take_probs(i)
                    if loops(i, 1):
                        shift(i + 1)
                    if loops(i, -1):
                        add(i - 1)
                    normalise(i)
                    if loops(i, 2):
                        take_queries(i + 2)

                take_queries(0)
                shift(0)
                take_queries(1)
                pipeline(dve, body)
                add(LAST)


FILTERS = 16
SCALES = 4
AR = 3
SPAN = 2 * P
SPANS = T // SPAN
PHI_ROW = SPAN + T
SEGMENTS = [(0, T >> 3), (T >> 3, T >> 3), (T >> 2, T >> 2), (T >> 1, T >> 1)]


def spectral_setup(nc, m, ins, phi_rows):
    with ExitStack() as ctx:
        sb, pb, sem = open_pools(nc, ctx)
        phi = sb("phi_in", [P, T // P, FILTERS])
        phi_t = sb("phi_t", [FILTERS, PHI_ROW])
        sigma = sb("sigma", [FILTERS, 2])
        plus, minus = (sb("m_" + n, [P, SCALES, FILTERS * C]) for n in ("plus", "minus"))
        ar = sb("ar_in", [P, SCALES, AR * C])
        cum_p, cum_m = (sb("cum_" + n, [P, SCALES, FILTERS * C]) for n in ("plus", "minus"))
        logits, soft, hard, weight, signed = (sb("pick_" + n, [P, SCALES]) for n in ("logits", "soft", "hard", "weight", "signed"))
        gumbel, free = sb("pick_gumbel", [P, SCALES]), sb("pick_free", [P, SCALES])
        col = sb("pick_col", [P, 4])
        t_ps = pb("phi_t_ps", [FILTERS, T])
        (phi_in, mats_in, small_in, t_ok, sig_ok, row_ok, row_out, exp_ok, step, cum_ok) = (sem("sp_" + n) for n in (
            "phi_in", "mats_in", "small_in", "turned", "sigma", "rows", "rows_out", "exp", "step", "cum"))
        table_in = sem("sp_table")
        with nc.Block() as block:
            @block.sync
            def _(sp):
                sp.dma_start(phi[:, :, :], ins["L2_ffn_phi"][0:T, :].rearrange("(n p) k -> p n k", p=P)).then_inc(phi_in, 16)
                for p in range(2):
                    sp.dma_start(plus[HALF[p], :, :].rearrange("d i (k e) -> d (i k) e", e=C), ins["L2_ffn_M_phi_plus"].rearrange("i k d e -> d (i k) e")).then_inc(mats_in, 16)
                    sp.dma_start(minus[HALF[p], :, :].rearrange("d i (k e) -> d (i k) e", e=C), ins["L2_ffn_M_phi_minus"].rearrange("i k d e -> d (i k) e")).then_inc(mats_in, 16)
                    sp.dma_start(ar[HALF[p], :, :].rearrange("d i (k e) -> d (i k) e", e=C), ins["L2_ffn_M_u"].rearrange("i k d e -> d (i k) e")).then_inc(mats_in, 16)
                sp.wait_ge(row_ok, 2)
                sp.dma_start(phi_rows, phi_t[:, :]).then_inc(row_out, 16)
                sp.wait_ge(row_out, 16)
                for k in range(FILTERS):
                    src = bass.AP(phi_rows.tensor, k * PHI_ROW + SPAN - 2 * (P - 1), [[2, P], [1, T]])
                    sp.dma_start(m.hankel[:, k, :], src).then_inc(table_in, 16)
                sp.wait_ge(table_in, 16 * FILTERS)
                sp.wait_ge(mats_in, 96)

            @block.scalar
            def _(act):
                act.dma_start(sigma[:, 0:1], ins["L2_ffn_sigma"].rearrange("(k a) -> k a", a=1)).then_inc(small_in, 16)
                act.dma_start(logits[:, :], ins["L2_ffn_log_weights"].rearrange("(a k) -> a k", a=1).to_broadcast([P, SCALES])).then_inc(small_in, 16)
                act.dma_start(gumbel[:, :], ins["L2_ffn_gumbel"].rearrange("(a k) -> a k", a=1).to_broadcast([P, SCALES])).then_inc(small_in, 16)
                act.wait_ge(small_in, 48)
                nc.scalar.activation(sigma[:, 1:2], sigma[:, 0:1], ACT.Sqrt).then_inc(sig_ok, 1)
                act.wait_ge(sig_ok, 1)
                nc.scalar.activation(sigma[:, 0:1], sigma[:, 1:2], ACT.Sqrt).then_inc(sig_ok, 1)
                act.wait_ge(sig_ok, 2)
                act.wait_ge(t_ok, 1)
                nc.scalar.activation(phi_t[:, SPAN:PHI_ROW], t_ps[:, :], ACT.Copy, scale=sigma[:, 0:1]).then_inc(row_ok, 1)
                act.wait_ge(step, 2)
                nc.scalar.activation(soft[:, :], logits[:, :], ACT.Exp, bias=col[:, 0:1], accum_out=col[:, 1:2]).then_inc(exp_ok, 1)

            @block.tensor
            def _(pe):
                pe.wait_ge(phi_in, 16)
                for n in range(T // P):
                    mm = nc.tensor.transpose(t_ps[:, n * P:(n + 1) * P], phi[:, n, :], m.ident[:, :])
                mm.then_inc(t_ok, 1)

            @block.vector
            def _(dve):
                nc.vector.memset(phi_t[:, 0:SPAN], 0.0).then_inc(row_ok, 1)
                done = [0]

                def link(ins_):
                    done[0] += 1
                    ins_.then_inc(step, 1)
                    dve.wait_ge(step, done[0])
                dve.wait_ge(small_in, 48)
                link(nc.vector.tensor_tensor(logits[:, :], logits[:, :], gumbel[:, :], ALU.add))
                link(nc.vector.tensor_reduce(col[:, 0:1], logits[:, :], axis=AX.X, op=ALU.max, negate=True))
                dve.wait_ge(exp_ok, 1)
                link(nc.vector.reciprocal(col[:, 2:3], col[:, 1:2]))
                link(nc.vector.tensor_scalar(soft[:, :], soft[:, :], col[:, 2:3], None, ALU.mult))
                link(nc.vector.tensor_reduce(col[:, 3:4], soft[:, :], axis=AX.X, op=ALU.max))
                link(nc.vector.tensor_scalar(hard[:, :], soft[:, :], col[:, 3:4], None, ALU.is_equal))
                link(nc.vector.tensor_scalar(free[:, :], hard[:, :], -1.0, 1.0, ALU.mult, ALU.add))
                for i in range(1, SCALES):
                    for j in range(i):
                        link(nc.vector.tensor_tensor(hard[:, i:i + 1], hard[:, i:i + 1], free[:, j:j + 1], ALU.mult))
                link(nc.vector.tensor_tensor(weight[:, :], hard[:, :], soft[:, :], ALU.subtract))
                link(nc.vector.tensor_tensor(weight[:, :], weight[:, :], soft[:, :], ALU.add))
                link(nc.vector.tensor_copy(signed[HALF[0], :], weight[HALF[0], :]))
                link(nc.vector.tensor_scalar(signed[HALF[1], :], weight[HALF[1], :], -1.0, None, ALU.mult))
                dve.wait_ge(mats_in, 96)
                for cum, mats, w in ((cum_p, plus, weight), (cum_m, minus, signed), (m.ar, ar, weight)):
                    for i in range(SCALES):
                        if i == 0:
                            link(nc.vector.tensor_scalar(cum[:, i, :], mats[:, i, :], w[:, i:i + 1], None, ALU.mult))
                        else:
                            link(nc.vector.scalar_tensor_tensor(out=cum[:, i, :], in0=mats[:, i, :], scalar=w[:, i:i + 1], in1=cum[:, i - 1, :], op0=ALU.mult, op1=ALU.add))
                for i in range(SCALES):
                    for par, op in ((0, ALU.add), (1, ALU.subtract)):
                        nc.vector.tensor_tensor(m.mix[:, :, i, par, :], cum_p[:, i, :].rearrange("p (k e) -> p k e", e=C),
                                                cum_m[:, i, :].rearrange("p (k e) -> p k e", e=C), op)


def spectral_norm_stage(nc, m):
    def piece(t, k):
        return m.normed[:, ds(t * 8 + k * 4, 4), :]
    layernorm_stage(nc, m, piece, "s")


def spectral_stage(nc, m):
    KP = FILTERS // 2
    with ExitStack() as ctx:
        sb, pb, sem = open_pools(nc, ctx)
        u = sb("sp_u", [P, T])
        apart = sb("sp_apart", [P, 2, AR - 1 + T])
        ut = sb("sp_ut", [P, 2, SPANS, 2, C])
        sums = [sb(f"sp_sums{k}", [P, 2, T]) for k in range(2)]
        mixk = [sb(f"sp_mix{k}", [P, SCALES, 2, C]) for k in range(2)]
        f_ps = [pb(f"sp_f{b}", [P, T]) for b in range(2)]
        o_ps = pb("sp_o", [C, 4, BANK])
        (u_ok, ut_ok, ut_c, f_ok, f_act, f_dve, mk_ok, mix_ok, o_ok, o_c, zero, first_ok) = (sem("st_" + n) for n in (
            "u", "ut", "ut_taken", "filtered", "taken_act", "taken_dve", "mix_in", "mixed", "out", "added", "zeroed", "first"))

        def out_of(seg, par):
            if seg == 3:
                return o_ps[:, par, :].rearrange("c (b n) -> c b n", b=2)
            if seg == 2:
                return o_ps[:, 2, :].rearrange("c (a b n) -> c a b n", a=2, b=2)[:, par, :, :]
            return o_ps[:, 3, :].rearrange("c (s a b n) -> c s a b n", s=2, a=2, b=2)[:, seg, par, :, :]

        with nc.Block() as block:
            @block.gpsimd
            def _(pool):
                nc.gpsimd.memset(apart[:, :, :], 0.0).then_inc(zero, 1)

            @block.tensor
            def _(pe):
                pe.sem_inc(mix_ok, 2)
                pe.wait_ge(first_ok, 1)
                with pe.Fori(0, G) as g:
                    pe.wait_ge(u_ok, g * 3 + 3)
                    for i in range(SPANS):
                        for par in range(2):
                            first = SPAN * (SPANS - 1 - i) + 1 - par
                            mm = nc.tensor.transpose(f_ps[i // 2][:, (i % 2) * SPAN + par * P:(i % 2) * SPAN + (par + 1) * P],
                                                     u[:, first:first + SPAN - 1:2], m.ident[:, :])
                        mm.then_inc(ut_ok, 1)
                    pe.wait_ge(ut_c, g * 2 + 2)
                    opened = set()
                    for tap in range(AR):
                        for seg, (lo, n) in enumerate(SEGMENTS):
                            for par in range(2):
                                first = AR - 1 - tap + lo + par
                                bank = par if seg == 3 else 2 if seg == 2 else 3
                                nc.tensor.matmul(out_of(seg, par), m.ar[:, SCALES - 1 - seg, tap * C:(tap + 1) * C],
                                                 apart[:, :, first:first + n - 1:2], start=bank not in opened, stop=False, skip_group_check=True)
                                opened.add(bank)

                    def filtered(j, n):
                        for b in range(2):
                            pe.wait_ge(f_act, g * (2 * FILTERS) + j * 4 + (2 * n + b + 1))
                            pe.wait_ge(f_dve, g * (2 * FILTERS) + j * 4 + (2 * n + b + 1))
                            for half in range(2):
                                spans = [i for i in range(SPANS) if i * SPAN < (half + 1) * BANK]
                                for i in spans:
                                    lo = max(half * BANK, i * SPAN)
                                    mm = nc.tensor.matmul(f_ps[b][:, lo:(half + 1) * BANK], ut[:, b, i, :, :].rearrange("p a c -> p (a c)"),
                                                          m.hankel[:, ds(j * 2 + n, 1), lo - i * SPAN:(half + 1) * BANK - i * SPAN].rearrange("p k t -> p (k t)"),
                                                          start=(i == 0), stop=(i == spans[-1]))
                            mm.then_inc(f_ok, 1)

                    def mixed(j, n):
                        pe.wait_ge(mk_ok, g * FILTERS + j * 2 + (n + 1))
                        pe.wait_ge(f_act, g * (2 * FILTERS) + j * 4 + (2 * n + 2 + 2))
                        pe.wait_ge(f_dve, g * (2 * FILTERS) + j * 4 + (2 * n + 2 + 2))
                        for seg, (lo, cnt) in enumerate(SEGMENTS):
                            for par in range(2):
                                mm = nc.tensor.matmul(out_of(seg, par), mixk[n][:, SCALES - 1 - seg, par, :], sums[n][:, :, lo + par:lo + cnt:2],
                                                      start=False, stop=False, skip_group_check=True)
                        mm.then_inc(mix_ok, 1)

                    with pe.Fori(0, KP) as j:
                        filtered(j, 0)
                        filtered(j, 1)
                        mixed(j, 0)
                        mixed(j, 1)
                    pe.wait_ge(o_c, g + 1)

            @block.scalar
            def _(act):
                act.sem_inc(f_act, 2)
                act.wait_ge(zero, 1)
                with act.Fori(0, G) as g:
                    act.wait_ge(mix_ok, g * FILTERS + 2)
                    source = m.normed[:, ds(g * (T // 128), T // 128), :].rearrange("p n t -> p (n t)")
                    nc.scalar.copy(u[:, ::-1], source).then_inc(u_ok, 1)
                    for b in range(2):
                        nc.scalar.copy(apart[HALF[b], b, AR - 1:], source[HALF[b], :]).then_inc(u_ok, 1)
                    act.wait_ge(ut_ok, g * 4 + 4)
                    nc.scalar.copy(ut[:, :, 2:4, :, :].rearrange("p b i a c -> p b (i a) c"), f_ps[1][:, 0:BANK].rearrange("p (i b c) -> p b i c", b=2, c=C)).then_inc(ut_c, 1)
                    with act.Fori(0, KP) as j:
                        for n in range(2):
                            for b in range(2):
                                act.wait_ge(f_ok, g * (2 * FILTERS) + j * 4 + (2 * n + b + 1))
                                if b == 0:
                                    act.wait_ge(mix_ok, g * FILTERS + j * 2 + (n + 1))
                                nc.scalar.copy(sums[n][HALF[1], b, 1:T], f_ps[b][HALF[1], 0:T - 1]).then_inc(f_act, 1)

            @block.vector
            def _(dve):
                for n in range(2):
                    last = nc.vector.memset(sums[n][HALF[1], :, 0:1], 0.0)
                last.then_inc(first_ok, 1)
                dve.sem_inc(f_dve, 2)
                with dve.Fori(0, G) as g:
                    dve.wait_ge(ut_ok, g * 4 + 2)
                    nc.vector.tensor_copy(ut[:, :, 0:2, :, :].rearrange("p b i a c -> p b (i a) c"), f_ps[0][:, 0:BANK].rearrange("p (i b c) -> p b i c", b=2, c=C)).then_inc(ut_c, 1)
                    with dve.Fori(0, KP) as j:
                        for n in range(2):
                            for b in range(2):
                                dve.wait_ge(f_ok, g * (2 * FILTERS) + j * 4 + (2 * n + b + 1))
                                if b == 0:
                                    dve.wait_ge(mix_ok, g * FILTERS + j * 2 + (n + 1))
                                    nc.vector.tensor_copy(mixk[n][:, :, :, :].rearrange("p s a e -> p (s a e)"),
                                                          m.mix[:, ds(j * 2 + n, 1), :, :, :].rearrange("p k s a e -> p (k s a e)")).then_inc(mk_ok, 1)
                                nc.vector.tensor_copy(sums[n][HALF[0], b, :], f_ps[b][HALF[0], :]).then_inc(f_dve, 1)
                    dve.wait_ge(mix_ok, g * FILTERS + (FILTERS + 2))
                    for b in range(2):
                        for seg, (lo, cnt) in enumerate(SEGMENTS):
                            for par in range(2):
                                x = m.x[HALF[b], ds(g, 1), lo + par:lo + cnt:2].rearrange("c g n -> c (g n)")
                                last = nc.vector.tensor_tensor(x, out_of(seg, par)[:, b, :], x, ALU.add)
                    last.then_inc(o_c, 1)


HEAD_DIM = C // HEADS
TILES = T // P


def linear_setup(nc, m, ins):
    with ExitStack() as ctx:
        sb, pb, sem = open_pools(nc, ctx)
        w_in, zeroed, step = sem("lin_w_in"), sem("lin_zeroed"), sem("lin_mask_step")
        with nc.Block() as block:
            @block.sync
            def _(sp):
                sp.wait_ge(zeroed, 3)
                for p in range(2):
                    cols = slice(p * C, (p + 1) * C)
                    sp.dma_start(m.lin_q[HALF[p], cols], ins["L3_attn_Wq"]).then_inc(w_in, 16)
                    sp.dma_start(m.lin_kv[HALF[p], 0, cols], ins["L3_attn_Wk"]).then_inc(w_in, 16)
                    sp.dma_start(m.lin_kv[HALF[p], 1, cols], ins["L3_attn_Wv"]).then_inc(w_in, 16)
                    sp.dma_start(m.lin_o[HALF[p], cols], ins["L3_attn_Wo"]).then_inc(w_in, 16)
                    sp.dma_start(m.lin_bias[HALF[p], 0:1], ins["L3_attn_bq"].rearrange("(c a) -> c a", a=1)).then_inc(w_in, 16)
                    sp.dma_start(m.lin_bias[HALF[p], 1:2], ins["L3_attn_bo"].rearrange("(c a) -> c a", a=1)).then_inc(w_in, 16)
                    sp.dma_start(m.lin_rows[:, 0, cols], ins["L3_attn_bk"].rearrange("(a c) -> a c", a=1).to_broadcast([P, C])).then_inc(w_in, 16)
                    sp.dma_start(m.lin_rows[:, 1, cols], ins["L3_attn_bv"].rearrange("(a c) -> a c", a=1).to_broadcast([P, C])).then_inc(w_in, 16)
                sp.wait_ge(w_in, 256)

            @block.gpsimd
            def _(pool):
                for t in (m.lin_q[:, :], m.lin_kv[:, :, :], m.lin_o[:, :]):
                    nc.gpsimd.memset(t, 0.0).then_inc(zeroed, 1)
                blocks = m.lin_mask[:, :].rearrange("p (h d) -> p h d", d=HEAD_DIM)
                nc.gpsimd.memset(m.lin_mask[:, :], 1.0).then_inc(step, 1)
                pool.wait_ge(step, 1)
                nc.gpsimd.affine_select(out=blocks, in_=blocks, compare_op=ALU.is_ge, fill=0.0, base=0,
                                        pattern=[[-HEAD_DIM, P // HEAD_DIM], [0, HEAD_DIM]], channel_multiplier=1).then_inc(step, 1)
                pool.wait_ge(step, 2)
                nc.gpsimd.affine_select(out=blocks, in_=blocks, compare_op=ALU.is_ge, fill=0.0, base=HEAD_DIM - 1,
                                        pattern=[[HEAD_DIM, P // HEAD_DIM], [0, HEAD_DIM]], channel_multiplier=-1).then_inc(step, 1)


def norm_stage(nc, m, tag):
    def piece(t, k):
        return m.normed[:, ds(t * 8 + k * 4, 4), :]
    layernorm_stage(nc, m, piece, tag)


def linear_attention_stage(nc, m):
    NH = P // HEAD_DIM
    with ExitStack() as ctx:
        sb, pb, sem = open_pools(nc, ctx)
        xg = sb("lin_xg", [P, T])
        kv = sb("lin_kvb", [P, TILES, 2 * P + 1])
        key_e = sb("lin_key_e", [P, TILES, P])
        q_e, q_r = sb("lin_q_e", [P, T]), sb("lin_q_r", [P, T])
        sums = sb("lin_sums", [P, P + NH])
        inv = sb("lin_inv", [P, TILES, NH])
        heads = sb("lin_heads", [P, TILES, P])
        heads_t = sb("lin_heads_t", [P, T])
        big = [pb(f"lin_big{k}", [P, 4, 2 * P]) for k in range(2)]
        q_ps = pb("lin_qps", [P, T])
        s_ps = pb("lin_sps", [P, BANK])
        (x_ok, kv_ok, kv_c, ke_ok, phi_ok, q_ok, qe_ok, qr_ok, pq_ok, s_ok, s_c, v_ok, d_ok, i_ok, h_ok, t_ok, t_c, o_ok, o_c, ones_ok, ksum) = (
            sem("l_" + n) for n in ("x", "kv", "kv_taken", "key_exp", "phi_k", "q", "q_exp", "q_relu", "phi_q", "sums", "sums_masked", "heads", "den",
                                    "inv", "normed", "turned", "turned_taken", "out", "added", "ones", "ksum"))
        with nc.Block() as block:
            @block.tensor
            def _(pe):
                with pe.Fori(0, G) as g:
                    pe.wait_ge(x_ok, g + 1)
                    for half in range(2):
                        for t in range(4):
                            tile = half * 4 + t
                            mm = nc.tensor.matmul(big[half][:, t, :], xg[:, tile * P:(tile + 1) * P], m.lin_kv[:, :, :].rearrange("p a c -> p (a c)"), start=True, stop=True)
                        mm.then_inc(kv_ok, 1)
                    for c in range(2):
                        mm = nc.tensor.matmul(q_ps[:, c * BANK:(c + 1) * BANK], m.lin_q[:, :], xg[:, c * BANK:(c + 1) * BANK], start=True, stop=True)
                    mm.then_inc(q_ok, 1)
                    pe.wait_ge(phi_ok, g + 1)
                    for t in range(TILES):
                        mm = nc.tensor.matmul(s_ps[:, 0:P + 1], kv[:, t, 0:P], kv[:, t, P:2 * P + 1], start=(t == 0), stop=(t == TILES - 1))
                    mm.then_inc(s_ok, 1)
                    pe.wait_ge(pq_ok, g + 1)
                    pe.wait_ge(s_c, g + 1)
                    for half in range(2):
                        for t in range(4):
                            tile = half * 4 + t
                            mm = nc.tensor.matmul(big[half][:, t, 0:P + NH], q_e[:, tile * P:(tile + 1) * P], sums[:, :], start=True, stop=True)
                        mm.then_inc(v_ok, 1)
                    for half in range(2):
                        pe.wait_ge(h_ok, g * 2 + (half + 1))
                        for t in range(4):
                            tile = half * 4 + t
                            mm = nc.tensor.transpose(q_ps[:, tile * P:(tile + 1) * P], heads[:, tile, :], m.ident[:, :])
                        mm.then_inc(t_ok, 1)
                    for c in range(2):
                        pe.wait_ge(t_c, g * 2 + (c + 1))
                        out = big[0][:, 2 * c:2 * c + 2, :].rearrange("p a c -> p (a c)")
                        nc.tensor.matmul(out, m.lin_o[:, :], heads_t[:, c * BANK:(c + 1) * BANK], start=True, stop=True).then_inc(o_ok, 1)
                    pe.wait_ge(o_c, g * 2 + 2)

            @block.scalar
            def _(act):
                nc.scalar.activation(kv[:, :, 2 * P:2 * P + 1], m.ident[:, 0:TILES].rearrange("p (t a) -> p t a", a=1), ACT.Exp, scale=0.0).then_inc(ones_ok, 1)
                with act.Fori(0, G) as g:
                    act.wait_ge(o_c, g * 2 + 2)
                    nc.scalar.copy(xg[:, :], m.normed[:, ds(g * (T // 128), T // 128), :].rearrange("p n t -> p (n t)")).then_inc(x_ok, 1)
                    for half in range(2):
                        act.wait_ge(kv_c, g * 2 + (half + 1))
                        nc.scalar.activation(key_e[:, half * 4:half * 4 + 4, :], kv[:, half * 4:half * 4 + 4, 0:P], ACT.Exp).then_inc(ke_ok, 1)
                    act.wait_ge(q_ok, g + 1)
                    nc.scalar.activation(q_e[:, :], q_ps[:, :], ACT.Exp, bias=m.lin_bias[:, 0:1]).then_inc(qe_ok, 1)
                    for half in range(2):
                        act.wait_ge(t_ok, g * 2 + (half + 1))
                        nc.scalar.copy(heads_t[:, half * BANK:(half + 1) * BANK], q_ps[:, half * BANK:(half + 1) * BANK]).then_inc(t_c, 1)

            @block.vector
            def _(dve):
                dve.sem_inc(o_c, 2)
                with dve.Fori(0, G) as g:
                    for half in range(2):
                        dve.wait_ge(kv_ok, g * 2 + (half + 1))
                        nc.vector.tensor_tensor(kv[:, half * 4:half * 4 + 4, 0:2 * P], big[half][:, :, :],
                                                m.lin_rows[:, :, :].rearrange("p a (b c) -> p b (a c)", b=1).to_broadcast([P, 4, 2 * P]), ALU.add).then_inc(kv_c, 1)
                    dve.wait_ge(qe_ok, g + 1)
                    nc.vector.tensor_scalar(q_r[:, :], q_ps[:, :], m.lin_bias[:, 0:1], 0.0, ALU.add, ALU.max).then_inc(qr_ok, 1)
                    dve.wait_ge(ke_ok, g * 2 + 2)
                    nc.vector.tensor_scalar(key_e[:, :, :], key_e[:, :, :], 1.0, None, ALU.min).then_inc(i_ok, 1)
                    dve.wait_ge(i_ok, g + 1)
                    nc.vector.scalar_tensor_tensor(out=kv[:, :, 0:P], in0=kv[:, :, 0:P], scalar=0.0, in1=key_e[:, :, :], op0=ALU.max, op1=ALU.add).then_inc(phi_ok, 1)
                    dve.wait_ge(qr_ok, g + 1)
                    nc.vector.scalar_tensor_tensor(out=q_e[:, :], in0=q_e[:, :], scalar=1.0, in1=q_r[:, :], op0=ALU.min, op1=ALU.add).then_inc(pq_ok, 1)
                    dve.wait_ge(s_ok, g + 1)
                    nc.vector.tensor_tensor(sums[:, 0:P], s_ps[:, 0:P], m.lin_mask[:, :], ALU.mult).then_inc(ksum, 1)
                    nc.vector.tensor_scalar(sums[:, P:P + NH], m.lin_mask[:, ::HEAD_DIM], s_ps[:, P:P + 1], None, ALU.mult).then_inc(s_c, 1)
                    for half in range(2):
                        part = inv[:, half * 4:half * 4 + 4, :]
                        dve.wait_ge(v_ok, g * 2 + (half + 1))
                        nc.vector.tensor_scalar(part, big[half][:, :, P:P + NH], m.eps[:, 0:1], None, ALU.add).then_inc(d_ok, 1)
                        dve.wait_ge(d_ok, g * 4 + (2 * half + 1))
                        nc.vector.reciprocal(part, part).then_inc(d_ok, 1)
                        dve.wait_ge(d_ok, g * 4 + (2 * half + 2))
                        for t in range(4):
                            tile = half * 4 + t
                            last = nc.vector.tensor_tensor(heads[:, tile, :].rearrange("p (h d) -> p h d", d=HEAD_DIM),
                                                           big[half][:, t, 0:P].rearrange("p (h d) -> p h d", d=HEAD_DIM),
                                                           inv[:, tile, :].to_broadcast([P, NH, HEAD_DIM]), ALU.mult)
                        last.then_inc(h_ok, 1)
                    for c in range(2):
                        dve.wait_ge(o_ok, g * 2 + (c + 1))
                        x = m.x_flat[:, ds(g * T + c * BANK, BANK)]
                        nc.vector.scalar_tensor_tensor(out=x, in0=big[0][:, 2 * c:2 * c + 2, :].rearrange("p a c -> p (a c)"), scalar=m.lin_bias[:, 1:2], in1=x,
                                                       op0=ALU.add, op1=ALU.add).then_inc(o_c, 1)


EXPERTS = 32
HIDDEN = 256
HT = HIDDEN // P
TOP = 8
QUADS = B // 4


def expert_stage(nc, m, ins, out):
    with ExitStack() as ctx:
        sb, pb, sem = open_pools(nc, ctx)
        gate = sb("gate_w", [EXPERTS, C])
        gate_t = sb("gate_t", [P, 2 * EXPERTS])
        gate_b = sb("gate_b", [P, 1])
        b2 = sb("ex_b2", [EXPERTS, C])
        b2_t = sb("ex_b2_t", [C, EXPERTS])
        logits = [sb(f"ex_logits{q}", [P, T]) for q in range(QUADS)]
        probs = [sb(f"ex_probs{q}", [P, T]) for q in range(QUADS)]
        kept_t = [sb(f"ex_kept_t{q}", [P, TILES, P]) for q in range(QUADS)]
        xt = sb("ex_xt", [P, G, TILES, P])
        top = [sb(f"ex_top{q}", [P, TOP]) for q in range(QUADS)]
        stat = sb("ex_stat", [P, QUADS, 4])
        pooled = sb("ex_pooled", [C + 1, EXPERTS, B])
        hidden = sb("ex_hidden", [P, EXPERTS, HT, B])
        made = sb("ex_made", [C, B, EXPERTS])
        spread = sb("ex_spread", [P, G, P])
        l_ps = [pb(f"ex_l{q}", [P, T]) for q in range(QUADS)]
        t_ps = [pb(f"ex_t{q}", [P, BANK]) for q in range(2)]
        a_ps, b_ps = pb("ex_a", [P, BANK]), pb("ex_b", [P, BANK])
        kept = logits
        (w_in, g_t, g_c, zeroed, l_ok, x_t, x_c, lg_ok, mx_ok, e_ok, step, keep_ok, k_t, k_c, p_ok, p_c, h_ok, h_c, m_ok, m_c, s_t, s_c, o_ok, o_c, done, b_c) = (
            sem("e_" + n) for n in ("w_in", "gate_turned", "gate_taken", "zeroed", "logits", "x_turned", "x_taken", "lg", "max", "exp", "step", "kept", "kept_turned",
                                    "kept_taken", "pooled", "pooled_taken", "hidden", "gelu", "made", "made_taken", "spread_turned", "spread", "out", "added", "stored", "b2"))
        with nc.Block() as block:
            @block.sync
            def _(sp):
                sp.dma_start(gate[:, :], ins["L3_ffn_gate_w"]).then_inc(w_in, 16)
                for q in range(4):
                    sp.dma_start(gate_b[q * EXPERTS:(q + 1) * EXPERTS, :], ins["L3_ffn_gate_b"].rearrange("(e a) -> e a", a=1)).then_inc(w_in, 16)
                sp.dma_start(b2[:, :], ins["L3_ffn_weight2"][:, HIDDEN, :]).then_inc(w_in, 16)
                for g in range(G):
                    sp.wait_ge(o_c, 2 * g + 2)
                    for p in range(2):
                        sp.dma_start(out[2 * g + p].rearrange("c h w -> c (h w)"), m.x[HALF[p], g, :]).then_inc(done, 16)
                sp.wait_ge(done, 16 * B)

            @block.gpsimd
            def _(pool):
                nc.gpsimd.memset(gate_t[:, :], 0.0).then_inc(zeroed, 1)
                nc.gpsimd.memset(spread[:, :, :], 0.0).then_inc(zeroed, 1)
                pool.wait_ge(zeroed, 2)
                nc.gpsimd.memset(pooled[C:C + 1, :, :], 1.0).then_inc(zeroed, 1)

            @block.tensor
            def _(pe):
                pe.wait_ge(w_in, 96)
                for p in range(2):
                    mm = nc.tensor.transpose(a_ps[0:C, p * EXPERTS:(p + 1) * EXPERTS], (gate, b2)[p][:, :], m.ident[0:EXPERTS, 0:EXPERTS])
                mm.then_inc(g_t, 1)
                for n in range(G * 2):
                    g, half = n // 2, n % 2
                    if n == 1:
                        pe.wait_ge(g_c, 2)
                        for gg in range(G):
                            for c in range(2):
                                mm = nc.tensor.matmul(l_ps[gg // 2][(gg % 2) * C:(gg % 2 + 1) * C, c * BANK:(c + 1) * BANK], gate_t[:, :],
                                                      m.normed[:, gg * 8 + c * 4:gg * 8 + c * 4 + 4, :].rearrange("p n t -> p (n t)"), start=True, stop=True)
                            mm.then_inc(l_ok, 1)
                    if n >= 2:
                        pe.wait_ge(x_c, n - 1)
                    for t in range(4):
                        mm = nc.tensor.transpose(t_ps[n % 2][:, t * P:(t + 1) * P], m.normed[:, g * 8 + half * 4 + t, :], m.ident[:, :])
                    mm.then_inc(x_t, 1)
                pe.wait_ge(x_c, 2 * G)
                for q in range(QUADS):
                    pe.wait_ge(keep_ok, q + 1)
                    for half in range(2):
                        if q:
                            pe.wait_ge(k_c, half + 1)
                        for t in range(4):
                            tile = half * 4 + t
                            mm = nc.tensor.transpose(t_ps[half][:, t * P:(t + 1) * P], kept[q][:, tile * P:(tile + 1) * P], m.ident[:, :])
                        mm.then_inc(k_t, 1)
                for g in range(G):
                    if g % 2 == 0:
                        pe.wait_ge(k_c, g + 2)
                    for t in range(TILES):
                        mm = nc.tensor.matmul(b_ps[:, g * P:(g + 1) * P], xt[:, g, t, :], kept_t[g // 2][:, t, :], start=(t == 0), stop=(t == TILES - 1))
                    mm.then_inc(p_ok, 1)
                pe.wait_ge(p_c, B)
                pe.wait_ge(m.ex_in, 16 * 3)
                for e in range(EXPERTS):
                    for t in range(HT):
                        mm = nc.tensor.matmul(a_ps[:, :].rearrange("p (e t b) -> p e t b", e=EXPERTS, t=HT)[:, e, t, :], m.ex_w1[:, e, t * P:(t + 1) * P],
                                              pooled[:, e, :], start=True, stop=True)
                mm.then_inc(h_ok, 1)
                pe.wait_ge(h_c, 1)
                for e in range(EXPERTS):
                    for t in range(HT):
                        mm = nc.tensor.matmul(b_ps[0:C, e * B:(e + 1) * B], m.ex_w2[:, e, t, :], hidden[:, e, t, :], start=(t == 0), stop=(t == HT - 1))
                mm.then_inc(m_ok, 1)
                pe.wait_ge(m_c, 1)
                for q in range(QUADS):
                    mm = nc.tensor.transpose(a_ps[:, q * C:(q + 1) * C], made[:, 4 * q:4 * q + 4, :].rearrange("c b e -> c (b e)"), m.ident[0:C, 0:C])
                mm.then_inc(s_t, 1)
                pe.wait_ge(s_c, B)
                for g in range(G):
                    for c in range(2):
                        n = 2 * g + c
                        if n >= 2:
                            pe.wait_ge(o_c, n - 1)
                        nc.tensor.matmul(t_ps[n % 2][:, :], spread[:, g, :], kept[g // 2][:, c * BANK:(c + 1) * BANK], start=True, stop=True).then_inc(o_ok, 1)

            @block.scalar
            def _(act):
                for n in range(2 * G):
                    g, half = n // 2, n % 2
                    act.wait_ge(x_t, n + 1)
                    nc.scalar.copy(xt[:, g, half * 4:half * 4 + 4, :], t_ps[n % 2][:, :].rearrange("p (t c) -> p t c", c=P)).then_inc(x_c, 1)
                for q in range(QUADS):
                    act.wait_ge(mx_ok, q + 1)
                    nc.scalar.activation(probs[q][:, :], logits[q][:, :], ACT.Exp, bias=stat[:, q, 0:1], accum_out=stat[:, q, 1:2]).then_inc(e_ok, 1)
                for q in range(QUADS):
                    for half in range(2):
                        act.wait_ge(k_t, 2 * q + half + 1)
                        nc.scalar.copy(kept_t[q][:, half * 4:half * 4 + 4, :], t_ps[half][:, :].rearrange("p (t c) -> p t c", c=P)).then_inc(k_c, 1)
                act.wait_ge(h_ok, 1)
                nc.scalar.activation(hidden[:, :, :, :], a_ps[:, :].rearrange("p (e t b) -> p e t b", e=EXPERTS, t=HT), ACT.Gelu).then_inc(h_c, 1)

            @block.vector
            def _(dve):
                dve.wait_ge(g_t, 1)
                dve.wait_ge(zeroed, 3)
                for p in range(2):
                    nc.vector.tensor_copy(gate_t[HALF[p], p * EXPERTS:(p + 1) * EXPERTS], a_ps[0:C, 0:EXPERTS]).then_inc(g_c, 1)
                nc.vector.tensor_copy(b2_t[:, :], a_ps[0:C, EXPERTS:2 * EXPERTS]).then_inc(b_c, 1)
                dve.wait_ge(w_in, 96)
                for q in range(QUADS):
                    dve.wait_ge(l_ok, 2 * q + 2)
                    nc.vector.tensor_scalar(logits[q][:, :], l_ps[q][:, :], gate_b[:, 0:1], None, ALU.add).then_inc(lg_ok, 1)
                    dve.wait_ge(lg_ok, q + 1)
                    nc.vector.tensor_reduce(stat[:, q, 0:1], logits[q][:, :], axis=AX.X, op=ALU.max, negate=True).then_inc(mx_ok, 1)
                n = 0
                for q in range(QUADS):
                    def link(ins_):
                        nonlocal n
                        n += 1
                        ins_.then_inc(step, 1)
                        dve.wait_ge(step, n)
                    dve.wait_ge(e_ok, q + 1)
                    link(nc.vector.reciprocal(stat[:, q, 2:3], stat[:, q, 1:2]))
                    link(nc.vector.tensor_scalar(probs[q][:, :], probs[q][:, :], stat[:, q, 2:3], None, ALU.mult))
                    link(nc.vector.max(top[q][:, :], probs[q][:, :]))
                    link(nc.vector.match_replace(kept[q][:, :], top[q][:, :], probs[q][:, :], 0.0))
                    nc.vector.tensor_tensor(kept[q][:, :], probs[q][:, :], kept[q][:, :], ALU.subtract).then_inc(keep_ok, 1)
                dve.wait_ge(p_ok, G)
                for g in range(G):
                    for p in range(2):
                        b = 2 * g + p
                        src = b_ps[HALF[p], g * P + (b % 4) * EXPERTS:g * P + (b % 4 + 1) * EXPERTS]
                        nc.vector.tensor_copy(pooled[0:C, :, b], src).then_inc(p_c, 1)
                dve.wait_ge(m_ok, 1)
                nc.vector.tensor_tensor(made[:, :, :].rearrange("c b e -> c e b"), b_ps[0:C, 0:B * EXPERTS].rearrange("c (e b) -> c e b", b=B),
                                        b2_t[:, :].to_broadcast([C, EXPERTS, B]), ALU.add).then_inc(m_c, 1)
                dve.wait_ge(s_t, 1)
                for b in range(B):
                    rows = slice((b % 4) * EXPERTS, (b % 4 + 1) * EXPERTS)
                    nc.vector.tensor_copy(spread[rows, b // 2, (b % 2) * C:(b % 2 + 1) * C], a_ps[rows, (b // 4) * C:(b // 4 + 1) * C]).then_inc(s_c, 1)
                for n in range(2 * G):
                    dve.wait_ge(o_ok, n + 1)
                    x = m.x_flat[:, n * BANK:(n + 1) * BANK]
                    nc.vector.tensor_tensor(x, t_ps[n % 2][:, :], x, ALU.add).then_inc(o_c, 1)


def expert_load(nc, m, ins, eng):
    eng.dma_start(m.ex_w1[:, :, :], ins["L3_ffn_weight1"].rearrange("e d h -> d e h")).then_inc(m.ex_in, 16)
    for t in range(HT):
        eng.dma_start(m.ex_w2[:, :, t, :], ins["L3_ffn_weight2"][:, t * P:(t + 1) * P, :].rearrange("e h o -> h e o")).then_inc(m.ex_in, 16)


def hybrid_program(nc, ins, out):
    with ExitStack() as whole:
        sb, pb, sem = open_pools(nc, whole)
        m = Memory()
        m.x = sb("x", [P, G, T])
        m.x_flat = m.x[:, :, :].rearrange("p g t -> p (g t)")
        m.ident, m.ident_bf = sb("ident", [P, P]), sb("ident_bf", [P, P], BF16)
        m.average, m.centre, m.eps = sb("average", [P, P]), sb("centre", [P, P]), sb("eps", [P, 1])
        phi_rows = nc.dram_tensor("phi_rows", (FILTERS, PHI_ROW), F32).ap()

        with nc.cleanup_on_exit(), ExitStack() as ctx:
            sb, pb, sem = open_pools(nc, ctx)
            m.rows, m.cols = sb("rows", [P, H, B, ROWP]), sb("cols", [P, W, B, ROWP])
            m.toeplitz, m.conv_bias = sb("toeplitz", [P, 4, SHIFTS, P]), sb("conv_bias", [P, 4])
            m.w_theta, m.w_phi, m.w_g = sb("w_theta", [C // 2, C]), sb("w_phi", [C // 2, C]), sb("w_g", [C // 2, C])
            m.w_last = sb("w_last", [C, C // 2])
            setup_stage(nc, m, ins)
            nonlocal_stage(nc, m)
            conv_passes(nc, m, m.rows, 0, "v")
            rows_to_cols_stage(nc, m)
            conv_passes(nc, m, m.cols, 2, "h")
            cols_to_tokens_stage(nc, m)

        with nc.cleanup_on_exit(), ExitStack() as ctx:
            sb, pb, sem = open_pools(nc, ctx)
            m.pieces = sb("pieces", [P, CHUNKS, PIECE])
            m.win_qk, m.win_vo = sb("win_qk", [P, HEADS, P]), sb("win_vo", [P, HEADS, P])
            m.win_x, m.win_mask, m.win_bias = sb("win_x", [P, NW, 2, KEYS]), sb("win_maskb", [P, BANK], BF16), sb("win_bias", [P, 1])
            window_setup(nc, m, ins)
            window_norm_stage(nc, m)
            window_attention_stage(nc, m)

        m.normed = whole.enter_context(nc.sbuf_tensor("normed", [P, G * T // 128, 128], F32))

        with nc.cleanup_on_exit(), ExitStack() as ctx:
            sb, pb, sem = open_pools(nc, ctx)
            m.hankel, m.mix, m.ar = sb("hankel", [P, FILTERS, T]), sb("mix", [P, FILTERS, SCALES, 2, C]), sb("ar", [P, SCALES, AR * C])
            spectral_setup(nc, m, ins, phi_rows)
            spectral_norm_stage(nc, m)
            spectral_stage(nc, m)

        with nc.cleanup_on_exit(), ExitStack() as ctx:
            sb, pb, sem = open_pools(nc, ctx)
            m.lin_q, m.lin_o, m.lin_kv = sb("lin_q", [P, P]), sb("lin_o", [P, P]), sb("lin_kv", [P, 2, P])
            m.lin_bias, m.lin_rows, m.lin_mask = sb("lin_bias", [P, 2]), sb("lin_rows", [P, 2, P]), sb("lin_mask", [P, P])
            m.ex_w1, m.ex_w2 = sb("ex_w1", [C + 1, EXPERTS, HIDDEN]), sb("ex_w2", [P, EXPERTS, HT, C])
            m.ex_in = sem("ex_in")
            linear_setup(nc, m, ins)
            with nc.Block() as block:
                @block.sync
                def _(sp):
                    expert_load(nc, m, ins, sp)
            norm_stage(nc, m, "l")
            linear_attention_stage(nc, m)
            norm_stage(nc, m, "e")
            expert_stage(nc, m, ins, out)


def kernel(**inputs):
    import concourse.bacc as bacc
    from concourse.bass_utils import run_bass_kernel_spmd

    nc = bacc.Bacc("TRN2", target_bir_lowering=False, num_devices=1)
    arrays, ins = {}, {}
    for name in inputs:
        a = np.ascontiguousarray(inputs[name])
        arrays["in_" + name] = a
        ins[name] = nc.dram_tensor("in_" + name, a.shape, mybir.dt.from_np(a.dtype), kind="ExternalInput").ap()
    out = nc.dram_tensor("out_0", (B, C, H, W), F32, kind="ExternalOutput").ap()
    hybrid_program(nc, ins, out)
    r = run_bass_kernel_spmd(nc, [arrays], core_ids=[0])
    return r.results[0]["out_0"]
```

```python
import numpy as np
from contextlib import ExitStack

import concourse.bass as bass
from concourse import mybir
from concourse.alu_op_type import AluOpType as ALU

F32 = mybir.dt.float32
BF16 = mybir.dt.bfloat16
F16 = mybir.dt.float16
ACT = mybir.ActivationFunctionType
AX = mybir.AxisListType
ds = bass.ds

B, C, H, W = 8, 64, 32, 32
T = H * W
P = 2 * C
G = B // 2
HALF = (slice(0, C), slice(C, P))
BANK = 512

TAPS = 9
PAIRS = W // 2
PADP = 2
ROWP = PAIRS + 2 * PADP
SHIFTS = 2 * PADP + 1


class Memory:
    pass


def open_pools(nc, ctx):
    def sb(name, shape, dt=F32):
        return ctx.enter_context(nc.sbuf_tensor(name, shape, dt))

    def pb(name, shape, dt=F32):
        return ctx.enter_context(nc.psum_tensor(name, shape, dt))

    def sem(name):
        return nc.alloc_semaphore(name=name)

    return sb, pb, sem


def setup_stage(nc, m, ins):
    with ExitStack() as ctx:
        sb, pb, sem = open_pools(nc, ctx)
        NP = TAPS + 2
        raw = sb("conv_raw", [C, 4, C * TAPS])
        padded = sb("conv_padded", [C, 4, NP, C])
        turned = [pb(f"conv_turned{i}", [P, SHIFTS, 2, C]) for i in range(2)]
        x_in, w_in, ident_ok, zeroed = sem("x_in"), sem("w_in"), sem("ident_ok"), sem("pads_zeroed")
        pad_ok, turned_ok, taken = sem("taps_padded"), sem("taps_turned"), sem("taps_taken")
        const_ok = sem("const_ok")
        with nc.Block() as block:
            @block.sync
            def _(sp):
                for n, name in enumerate(("d", "u", "r", "l")):
                    sp.dma_start(raw[:, n, :], ins["L1_conv_w_" + name].rearrange("o i k -> o (i k)")).then_inc(w_in, 16)
                for p in range(2):
                    for g in range(G):
                        sp.dma_start(m.x[HALF[p], g, :], ins["x"][2 * g + p].rearrange("c h w -> c (h w)")).then_inc(x_in, 16)
                sp.wait_ge(x_in, 16 * B)

            @block.scalar
            def _(act):
                for n, name in enumerate(("d", "u", "r", "l")):
                    for p in range(2):
                        act.dma_start(m.conv_bias[HALF[p], n:n + 1], ins["L1_conv_b_" + name].rearrange("(c a) -> c a", a=1)).then_inc(w_in, 16)
                act.dma_start(m.w_theta[:, :], ins["L0_conv_w_theta"]).then_inc(w_in, 16)
                act.dma_start(m.w_phi[:, :], ins["L0_conv_w_phi"]).then_inc(w_in, 16)
                act.dma_start(m.w_g[:, :], ins["L0_conv_w_g"]).then_inc(w_in, 16)
                act.dma_start(m.w_last[:, :], ins["L0_conv_w_last"]).then_inc(w_in, 16)
                act.wait_ge(w_in, 16 * 16)

            @block.gpsimd
            def _(pool):
                nc.gpsimd.memset(m.ident[:, :], 0.0).then_inc(zeroed, 1)
                nc.gpsimd.memset(m.average[:, :], 0.0).then_inc(zeroed, 1)
                nc.gpsimd.memset(padded[:, :, 0, :], 0.0).then_inc(pad_ok, 1)
                nc.gpsimd.memset(padded[:, :, NP - 1, :], 0.0).then_inc(pad_ok, 1)
                pool.wait_ge(zeroed, 2)
                nc.gpsimd.affine_select(out=m.ident[:, :], in_=m.ident[:, :], compare_op=ALU.not_equal, fill=1.0,
                                        base=0, pattern=[[-1, P]], channel_multiplier=1).then_inc(ident_ok, 1)
                nc.gpsimd.memset(m.rows[:, :, :, :], 0.0).then_inc(zeroed, 1)
                nc.gpsimd.memset(m.cols[:, :, :, :], 0.0).then_inc(zeroed, 1)
                pool.wait_ge(zeroed, 4)
                for p in range(2):
                    nc.gpsimd.memset(m.average[HALF[p], p * C:(p + 1) * C], 1.0 / C).then_inc(const_ok, 1)

            @block.vector
            def _(dve):
                nc.vector.memset(m.eps[:, :], 1e-5)
                dve.wait_ge(w_in, 16 * 16)
                for n in range(4):
                    nc.vector.tensor_copy(padded[:, n, 1:NP - 1, :],
                                          raw[:, n, :].rearrange("o (i k) -> o k i", k=TAPS)).then_inc(pad_ok, 1)
                for n in range(4):
                    dve.wait_ge(turned_ok, n + 1)
                    nc.vector.tensor_copy(m.toeplitz[:, n, :, :], turned[n % 2][:, :, :, :].rearrange("p s a c -> p s (a c)")).then_inc(taken, 1)
                dve.wait_ge(ident_ok, 1)
                dve.wait_ge(const_ok, 2)
                nc.vector.tensor_tensor(m.centre[:, :], m.ident[:, :], m.average[:, :], ALU.subtract)
                nc.vector.tensor_copy(m.ident_bf[:, :], m.ident[:, :])

            @block.tensor
            def _(pe):
                pe.wait_ge(ident_ok, 1)
                pe.wait_ge(pad_ok, 6)
                for n in range(4):
                    if n >= 2:
                        pe.wait_ge(taken, n - 1)
                    for s in range(SHIFTS):
                        for po in range(2):
                            first = 2 * s - po + 1
                            last = nc.tensor.transpose(turned[n % 2][:, s, po, :],
                                                       padded[:, n, first:first + 2, :].rearrange("o t i -> o (t i)"),
                                                       m.ident[0:C, 0:C])
                    last.then_inc(turned_ok, 1)


def nonlocal_stage(nc, m):
    NB = 2 * (T // P)
    KT = T // P
    with ExitStack() as ctx:
        sb, pb, sem = open_pools(nc, ctx)
        last_t = sb("w_last_t", [C // 2, C])
        qk_w = sb("qk_w", [P, P])
        zo_w = sb("zo_w", [P, P])
        xg = sb("xg", [P, T])
        qg = sb("qg", [P, T])
        zg = sb("zg", [P, KT, P])
        probs = [sb(f"probs{i}", [P, T]) for i in range(2)]
        probs_t = [sb(f"probs_t{i}", [P, KT, P]) for i in range(2)]
        out_n = [sb(f"out_n{i}", [P, 2, C]) for i in range(2)]
        nmax = sb("nmax", [P, 4])
        rsum = sb("rsum", [P, 4])
        rinv = sb("rinv", [P, 4])
        scores = [pb(f"scores{i}", [P, T]) for i in range(2)]
        turned = pb("turned", [P, KT, P])
        out_ps = pb("out_ps", [P, BANK])[:, 0:P].rearrange("p (a c) -> p a c", a=2)
        out_t = pb("out_t", [P, BANK])[:, 0:P]
        wl_t, wl_c, fused, fused_c = sem("wl_t"), sem("wl_c"), sem("fused"), sem("fused_c")
        placed = sem("x_placed")
        xg_ok, proj_ok, qa, qd = sem("xg_ok"), sem("proj_ok"), sem("q_taken"), sem("z_taken")
        s_score, s_max, s_exp, s_tr = sem("score_ready"), sem("max_ready"), sem("probs_ready"), sem("turned_ready")
        s_ta, s_td, s_pv, s_inv = sem("turned_taken_act"), sem("turned_taken_dve"), sem("out_ready"), sem("inv_ready")
        s_norm, s_ot, s_add = sem("out_normed"), sem("out_turned"), sem("out_added")
        HK = KT // 2

        with nc.Block() as block:
            @block.gpsimd
            def _(pool):
                def place(par, p):
                    nc.gpsimd.tensor_copy(
                        m.rows[HALF[par], :, p::2, PADP:PADP + PAIRS].rearrange("c h g q -> c g h q"),
                        m.x[HALF[p], :, :].rearrange("c g (h q a) -> c g h q a", h=H, a=2)[:, :, :, :, par]).then_inc(placed, 1)
                nc.gpsimd.memset(qk_w[:, :], 0.0).then_inc(fused_c, 1)
                nc.gpsimd.memset(zo_w[:, :], 0.0).then_inc(fused_c, 1)
                nc.gpsimd.tensor_copy(xg[:, :], m.x[:, 0, :]).then_inc(xg_ok, 1)
                pool.wait_ge(xg_ok, 1)
                for par in range(2):
                    for p in range(2):
                        place(par, p)
                        pool.wait_ge(placed, 2 * par + p + 1)
                with pool.Fori(1, G) as g:
                    pool.wait_ge(s_score, g * NB)
                    nc.gpsimd.tensor_copy(xg[:, :], m.x[:, ds(g, 1), :].rearrange("p a t -> p (a t)")).then_inc(xg_ok, 1)

            @block.tensor
            def _(pe):
                nc.tensor.transpose(out_t[0:C // 2, 0:C], m.w_last[:, :], m.ident[0:C, 0:C]).then_inc(wl_t, 1)
                for p in range(2):
                    nc.tensor.matmul(scores[0][HALF[p], 0:C], m.w_theta[:, :], m.w_phi[:, :], start=True, stop=True).then_inc(fused, 1)
                pe.wait_ge(wl_c, 1)
                for p in range(2):
                    nc.tensor.matmul(scores[1][HALF[p], 0:C], m.w_g[:, :], last_t[:, :], start=True, stop=True).then_inc(fused, 1)
                pe.wait_ge(fused_c, 6)
                with pe.Fori(0, G) as g:
                    pe.wait_ge(xg_ok, g + 1)
                    for c in range(T // BANK):
                        mm = nc.tensor.matmul(scores[0][:, c * BANK:(c + 1) * BANK], qk_w[:, :], xg[:, c * BANK:(c + 1) * BANK], start=True, stop=True)
                    mm.then_inc(proj_ok, 1)
                    for k in range(KT):
                        mm = nc.tensor.matmul(scores[1][:, k * P:(k + 1) * P], xg[:, k * P:(k + 1) * P], zo_w[:, :], start=True, stop=True)
                    mm.then_inc(proj_ok, 1)
                    pe.wait_ge(qa, g + 1)
                    pe.wait_ge(qd, g + 1)

                    def score(i):
                        if i >= 2:
                            pe.wait_ge(s_exp, g * NB + (i - 1))
                        p, j, par = i // 8, (i // 2) % 4, i % 2
                        q = qg[HALF[p], 256 * j + par:256 * (j + 1):2]
                        for c in range(T // BANK):
                            mm = nc.tensor.matmul(scores[i % 2][:, c * BANK:(c + 1) * BANK], q, xg[HALF[p], c * BANK:(c + 1) * BANK], start=True, stop=True)
                        mm.then_inc(s_score, 1)

                    def turn(i):
                        pe.wait_ge(s_exp, g * NB + (i + 1))
                        if i >= 1:
                            pe.wait_ge(s_ta, g * NB + i)
                            pe.wait_ge(s_td, g * NB + i)
                        for k in range(KT):
                            mm = nc.tensor.transpose(turned[:, k, :], probs[i % 2][:, k * P:(k + 1) * P], m.ident[:, :])
                            if k == HK - 1 or k == KT - 1:
                                mm.then_inc(s_tr, 1)

                    def attend(i):
                        p, par = i // 8, i % 2
                        pe.wait_ge(s_ta, g * NB + (i + 1))
                        pe.wait_ge(s_td, g * NB + (i + 1))
                        if i >= 1:
                            pe.wait_ge(s_norm, g * NB + i)
                        for k in range(KT):
                            mm = nc.tensor.matmul(out_ps[:, par, :], probs_t[i % 2][:, k, :], zg[:, k, p * C:(p + 1) * C], start=(k == 0), stop=(k == KT - 1))
                        mm.then_inc(s_pv, 1)

                    def turn_out(n):
                        pe.wait_ge(s_norm, g * NB + (2 * n + 2))
                        if n >= 1:
                            pe.wait_ge(s_add, g * (NB // 2) + n)
                        nc.tensor.transpose(out_t[:, :], out_n[n % 2][:, :, :].rearrange("p a c -> p (a c)"), m.ident[:, :]).then_inc(s_ot, 1)

                    score(0)
                    score(1)
                    for i in range(NB):
                        turn(i)
                        if i + 2 < NB:
                            score(i + 2)
                        attend(i)
                        if i >= 2 and i % 2 == 0:
                            turn_out(i // 2 - 1)
                    turn_out(NB // 2 - 1)
                    pe.wait_ge(s_add, (g + 1) * (NB // 2))

            @block.scalar
            def _(act):
                act.wait_ge(fused, 2)
                act.wait_ge(fused_c, 2)
                for p in range(2):
                    nc.scalar.activation(qk_w[HALF[p], p * C:(p + 1) * C], scores[0][HALF[p], 0:C], ACT.Copy).then_inc(fused_c, 1)
                with act.Fori(0, G) as g:
                    act.wait_ge(proj_ok, 2 * g + 1)
                    nc.scalar.activation(qg[:, :], scores[0][:, :], ACT.Copy).then_inc(qa, 1)

                    def exp(i):
                        act.wait_ge(s_max, g * NB + (i + 1))
                        if i >= 2:
                            act.wait_ge(s_tr, 2 * (g * NB) + 2 * (i - 1))
                        nc.scalar.activation(probs[i % 2][:, :], scores[i % 2][:, :], ACT.Exp, bias=nmax[:, i % 4:i % 4 + 1],
                                             accum_out=rsum[:, i % 4:i % 4 + 1]).then_inc(s_exp, 1)

                    def take(i):
                        act.wait_ge(s_tr, 2 * (g * NB) + 2 * (i + 1))
                        if i >= 2:
                            act.wait_ge(s_pv, g * NB + (i - 1))
                        nc.scalar.activation(probs_t[i % 2][:, HK:KT, :], turned[:, HK:KT, :], ACT.Copy).then_inc(s_ta, 1)

                    exp(0)
                    exp(1)
                    for i in range(NB):
                        take(i)
                        if i + 2 < NB:
                            exp(i + 2)

            @block.vector
            def _(dve):
                dve.wait_ge(wl_t, 1)
                nc.vector.tensor_copy(last_t[:, :], out_t[0:C // 2, 0:C]).then_inc(wl_c, 1)
                dve.wait_ge(fused, 4)
                dve.wait_ge(fused_c, 2)
                for p in range(2):
                    nc.vector.tensor_copy(zo_w[HALF[p], p * C:(p + 1) * C], scores[1][HALF[p], 0:C]).then_inc(fused_c, 1)
                dve.wait_ge(placed, 4)
                with dve.Fori(0, G) as g:
                    dve.wait_ge(proj_ok, 2 * g + 2)
                    nc.vector.tensor_copy(zg[:, :, :].rearrange("p k c -> p (k c)"), scores[1][:, :]).then_inc(qd, 1)

                    def row_max(i):
                        dve.wait_ge(s_score, g * NB + (i + 1))
                        nc.vector.tensor_reduce(nmax[:, i % 4:i % 4 + 1], scores[i % 2][:, :], axis=AX.X, op=ALU.max, negate=True).then_inc(s_max, 1)

                    def take(i):
                        dve.wait_ge(s_tr, 2 * (g * NB) + (2 * i + 1))
                        if i >= 2:
                            dve.wait_ge(s_pv, g * NB + (i - 1))
                        nc.vector.tensor_copy(probs_t[i % 2][:, 0:HK, :], turned[:, 0:HK, :]).then_inc(s_td, 1)

                    def norm(i):
                        n, par = i // 2, i % 2
                        dve.wait_ge(s_exp, g * NB + (i + 1))
                        nc.vector.reciprocal(rinv[:, i % 4:i % 4 + 1], rsum[:, i % 4:i % 4 + 1]).then_inc(s_inv, 1)
                        dve.wait_ge(s_inv, g * NB + (i + 1))
                        dve.wait_ge(s_pv, g * NB + (i + 1))
                        if n >= 2:
                            dve.wait_ge(s_ot, g * (NB // 2) + (n - 1))
                        nc.vector.tensor_scalar(out_n[n % 2][:, par, :], out_ps[:, par, :], rinv[:, i % 4:i % 4 + 1], None, ALU.mult).then_inc(s_norm, 1)

                    def add(n):
                        p, j = n // 4, n % 4
                        dve.wait_ge(s_ot, g * (NB // 2) + (n + 1))
                        dst = m.rows[:, 8 * j:8 * j + 8, ds(2 * g + p, 1), PADP:PADP + PAIRS]
                        nc.vector.tensor_tensor(dst, out_t[:, :].rearrange("p (h a q) -> p h a q", h=8, a=1), dst, ALU.add).then_inc(s_add, 1)

                    row_max(0)
                    row_max(1)
                    for i in range(NB):
                        take(i)
                        if i + 2 < NB:
                            row_max(i + 2)
                        norm(i)
                        if i >= 2 and i % 2 == 0:
                            add(i // 2 - 1)
                    add(NB // 2 - 1)


def conv_passes(nc, m, grid, first, tag, extra=None):
    LINES = H
    FWD, BWD = LINES - 1, LINES - 2
    with ExitStack() as ctx:
        sb, pb, sem = open_pools(nc, ctx)
        conv = [pb(f"conv{tag}{k}", [P, BANK])[:, 0:B * PAIRS].rearrange("p (b q) -> p b q", q=PAIRS) for k in range(2)]
        running = [sb(f"running{tag}{k}", [P, B, ROWP]) for k in range(2)]
        line_ok, conv_ok, saved, padded = sem("line_ready" + tag), sem("conv_ready" + tag), sem("line_saved" + tag), sem("running_padded" + tag)

        def steps(eng, step):
            step(1, 1, first, 1)
            with eng.Fori(1, (FWD + 1) // 2) as k:
                for odd in range(2):
                    step(k * 2 + odd, odd, first, k * 2 + odd)
            with eng.Fori((FWD + 1) // 2, (FWD + BWD + 1) // 2) as k:
                for odd in range(2):
                    step(k * 2 + odd, odd, first + 1, k * (-2) + (2 * FWD - odd))

        def at(line):
            return grid[:, ds(line, 1), :, PADP:PADP + PAIRS].rearrange("p l b q -> p (l b) q")

        with nc.Block() as block:
            @block.tensor
            def _(pe):
                def step(n, odd, wn, line):
                    if not isinstance(n, int):
                        pe.wait_ge(saved, n - 1)
                    nc.tensor.matmul(conv[odd][:, :, :], m.ident[:, :], at(line), start=True, stop=False)
                    pe.wait_ge(line_ok, n)
                    for s in range(SHIFTS):
                        mm = nc.tensor.matmul(conv[odd][:, :, :], m.toeplitz[:, wn, s, :], running[1 - odd][:, :, s:s + PAIRS],
                                              start=False, stop=(s == SHIFTS - 1))
                    mm.then_inc(conv_ok, 1)
                steps(pe, step)

            @block.vector
            def _(dve):
                for k in range(2):
                    nc.vector.memset(running[k][:, :, :], 0.0).then_inc(padded, 1)
                dve.wait_ge(padded, 2)
                nc.vector.tensor_copy(running[0][:, :, :], grid[:, 0, :, :]).then_inc(line_ok, 1)

                def step(n, odd, wn, line):
                    if not isinstance(n, int):
                        dve.wait_ge(saved, n - 1)
                    dve.wait_ge(conv_ok, n)
                    nc.vector.scalar_tensor_tensor(out=running[odd][:, :, PADP:PADP + PAIRS], in0=conv[odd][:, :, :], scalar=m.conv_bias[:, wn:wn + 1],
                                                   in1=at(line), op0=ALU.add, op1=ALU.max).then_inc(line_ok, 1)
                steps(dve, step)

            @block.scalar
            def _(act):
                act.sem_inc(saved, 1)

                def step(n, odd, wn, line):
                    act.wait_ge(line_ok, n + 1)
                    nc.scalar.copy(at(line), running[odd][:, :, PADP:PADP + PAIRS]).then_inc(saved, 1)
                steps(act, step)

            if extra is not None:
                extra(block)


def rows_to_cols_stage(nc, m):
    def move(copy, hp, wp):
        src = m.rows[HALF[wp], hp::2, :, PADP:PADP + PAIRS].rearrange("c r b q -> c b q r")
        dst = m.cols[HALF[hp], wp::2, :, PADP:PADP + PAIRS].rearrange("c q b r -> c b q r")
        copy(dst, src)

    with nc.Block() as block:
        @block.vector
        def _(dve):
            move(nc.vector.tensor_copy, 0, 1)
            move(nc.vector.tensor_copy, 1, 0)

        @block.scalar
        def _(act):
            move(nc.scalar.copy, 0, 0)

        @block.gpsimd
        def _(pool):
            move(nc.gpsimd.tensor_copy, 1, 1)


def cols_to_tokens_stage(nc, m):
    def move(copy, hp, p):
        src = m.cols[HALF[hp], :, p::2, PADP:PADP + PAIRS].rearrange("c w g r -> c g r w")
        dst = m.x[HALF[p], :, :].rearrange("c g (r a w) -> c g r a w", a=2, w=W)[:, :, :, hp, :]
        copy(dst, src)

    with nc.Block() as block:
        @block.vector
        def _(dve):
            move(nc.vector.tensor_copy, 0, 1)
            move(nc.vector.tensor_copy, 1, 0)

        @block.scalar
        def _(act):
            move(nc.scalar.copy, 0, 0)

        @block.gpsimd
        def _(pool):
            move(nc.gpsimd.tensor_copy, 1, 1)


def layernorm_stage(nc, m, out_piece, tag, extra=None):
    N = G * T // BANK
    TP = BANK // P
    with ExitStack() as ctx:
        sb, pb, sem = open_pools(nc, ctx)
        square = [sb(f"square{tag}{k}", [P, BANK]) for k in range(2)]
        dev = sb(f"dev{tag}", [P, 2 * TP * N])
        inv = sb(f"inv{tag}", [P, 2 * TP * N])
        wide = [sb(f"wide{tag}{k}", [P, 2 * TP, C]) for k in range(2)]
        centred = [pb(f"centred{tag}{k}", [P, BANK]) for k in range(2)]
        scale = [pb(f"scale{tag}{k}", [P, BANK]) for k in range(2)]
        var = pb(f"var{tag}", [P, BANK])
        cen_ok, sq_ok, kept_ok, var_ok, sd_ok, inv_ok, wide_ok, scale_ok, out_ok = (sem(n + tag) for n in (
            "centred_ready", "square_ready", "centred_kept", "var_ready", "sd_ready", "inv_ready", "wide_ready", "scale_ready", "normed_ready"))
        with nc.Block() as block:
            @block.tensor
            def _(pe):
                with pe.Fori(0, N // 2) as t:
                    for k in range(2):
                        pe.wait_ge(kept_ok, t * 2 + (k + 1))
                        nc.tensor.matmul(centred[k][:, :], m.centre[:, :], m.x_flat[:, ds(t * (2 * BANK) + k * BANK, BANK)], start=True, stop=True).then_inc(cen_ok, 1)
                    for k in range(2):
                        pe.wait_ge(sq_ok, t * 2 + (k + 1))
                        for j in range(TP):
                            mm = nc.tensor.matmul(var[:, ds(t * (4 * TP) + (k * TP + j) * 2, 2)], square[k][:, j * P:(j + 1) * P], m.average[:, ::C], start=True, stop=True)
                        mm.then_inc(var_ok, 1)
                with pe.Fori(0, N // 2) as t:
                    for k in range(2):
                        pe.wait_ge(wide_ok, t * 2 + (k + 1))
                        pe.wait_ge(out_ok, t * 2 + (k + 1))
                        for j in range(TP):
                            mm = nc.tensor.matmul(scale[k][:, j * P:(j + 1) * P], wide[k][:, 2 * j:2 * j + 2, :].rearrange("p a c -> p (a c)"), m.ident[:, :], start=True, stop=True)
                        mm.then_inc(scale_ok, 1)

            @block.scalar
            def _(act):
                with act.Fori(0, N // 2) as t:
                    for k in range(2):
                        act.wait_ge(cen_ok, t * 2 + (k + 1))
                        nc.scalar.activation(square[k][:, :], centred[k][:, :], ACT.Square).then_inc(sq_ok, 1)
                act.wait_ge(var_ok, N)
                nc.scalar.activation(dev[:, :], var[:, 0:2 * TP * N], ACT.Sqrt, bias=m.eps[:, 0:1]).then_inc(sd_ok, 1)
                act.wait_ge(inv_ok, 1)
                with act.Fori(0, N // 2) as t:
                    for k in range(2):
                        act.wait_ge(out_ok, t * 2 + (k + 1))
                        nc.scalar.activation(wide[k][:, :, :], inv[:, ds(t * (4 * TP) + k * (2 * TP), 2 * TP)].to_broadcast([P, 2 * TP, C]), ACT.Copy).then_inc(wide_ok, 1)

            @block.vector
            def _(dve):
                dve.sem_inc(kept_ok, 2)
                dve.sem_inc(out_ok, 2)
                with dve.Fori(0, N // 2) as t:
                    for k in range(2):
                        dve.wait_ge(sq_ok, t * 2 + (k + 1))
                        nc.vector.tensor_copy(out_piece(t, k), centred[k][:, :].rearrange("p (c n) -> p c n", n=P)).then_inc(kept_ok, 1)
                dve.wait_ge(sd_ok, 1)
                nc.vector.reciprocal(inv[:, :], dev[:, :]).then_inc(inv_ok, 1)
                dve.wait_ge(kept_ok, N + 2)
                with dve.Fori(0, N // 2) as t:
                    for k in range(2):
                        dve.wait_ge(scale_ok, t * 2 + (k + 1))
                        nc.vector.tensor_tensor(out_piece(t, k), scale[k][:, :].rearrange("p (c n) -> p c n", n=P), out_piece(t, k), ALU.mult).then_inc(out_ok, 1)

            if extra is not None:
                extra(block, out_ok, N + 2)


HEADS = 8
WINDOW = 32
CHUNK = 128
NW = CHUNK // WINDOW
KEYS = 2 * WINDOW
PIECE = WINDOW + CHUNK
CHUNKS = G * T // CHUNK
MASKED = -1e30


def window_norm_stage(nc, m, hankel_load=None):
    def piece(t, k):
        return m.pieces[:, ds(t * (2 * NW) + k * NW, NW), WINDOW:PIECE]

    def history(block, out_ok, n):
        @block.gpsimd
        def _(pool):
            nc.gpsimd.memset(m.pieces[:, ::T // CHUNK, 0:WINDOW], 0.0)
            pool.wait_ge(out_ok, n)
            per = T // CHUNK
            for g in range(G):
                nc.gpsimd.tensor_copy(m.pieces[:, g * per + 1:(g + 1) * per, 0:WINDOW], m.pieces[:, g * per:(g + 1) * per - 1, CHUNK:PIECE])

        if hankel_load is not None:
            @block.sync
            def _(sp):
                hankel_load(nc, m, sp)

    layernorm_stage(nc, m, piece, "w", history)


def window_attention_stage(nc, m):
    HG = HEADS // 4
    NT = HG * NW * 2
    with ExitStack() as ctx:
        sb, pb, sem = open_pools(nc, ctx)
        queries = sb("queries", [P, NW, HEADS, WINDOW])
        xt = [sb(f"win_xt{k}", [P, NW, P]) for k in range(2)]
        shifted = sb("shifted", [P, HG, NW, P])
        probs = sb("win_probs", [P, HG, NW, P])
        probs_t = sb("win_probs_t", [P, HG, NW, P])
        heads = sb("win_heads", [P, HG, NW, P])
        heads_t = sb("win_heads_t", [P, HG, NW, P])
        rmax, rsum, rinv = (sb(n, [P, NT]) for n in ("win_max", "win_sum", "win_inv"))
        q_ps = pb("q_ps", [P, HEADS, CHUNK])
        s_ps = pb("s_ps", [P, HG, NW, P])
        t_ps = pb("t_ps", [P, HG, NW, P])
        z_ps = pb("z_ps", [P, HG, NW, P])
        xt_ps, o_ps = q_ps[:, 0:NW, :], z_ps[:, 0, 0, :]
        (win_ok, q_ok, q_act, q_dve, s_ok, xt_ok, xt_c, sub_ok, p_ok, pt_ok, pt_act, pt_dve, z_ok, max_ok, sum_ok, inv_ok, n_ok,
         zt_ok, zt_c, o_ok, o_c) = (sem("w_" + n) for n in (
             "windows", "queries", "queries_act", "queries_dve", "scores", "xt", "xt_taken", "shifted", "probs", "probs_turned", "pt_act", "pt_dve",
             "heads", "max", "sum", "inv", "normed", "heads_turned", "heads_taken", "out", "added"))
        LAST = CHUNKS - 1

        def pipeline(eng, body):
            body(0, 0)
            with eng.Fori(0, (LAST - 2) // 2) as k:
                for odd in (1, 0):
                    body(k * 2 + (2 - odd), odd)
            for i in range(LAST // 2 * 2 - 1, LAST + 1):
                body(i, i % 2)

        def loops(i, d=0):
            return not isinstance(i, int) or 0 <= i + d <= LAST

        with nc.Block() as block:
            @block.gpsimd
            def _(pool):
                def window(i):
                    if not (isinstance(i, int) and i == 0):
                        pool.wait_ge(s_ok, i)
                        pool.wait_ge(xt_ok, i)
                    for p in range(2):
                        c = m.pieces[HALF[p], ds(i, 1), 0:PIECE]
                        for k in range(2):
                            nc.gpsimd.tensor_copy(m.win_x[HALF[p], k::2, p, :],
                                                  c[:, :, k * WINDOW:k * WINDOW + 2 * KEYS].rearrange("p a (w n) -> p (a w) n", n=KEYS)).then_inc(win_ok, 1)
                window(0)
                with pool.Fori(1, CHUNKS) as i:
                    window(i)

            @block.tensor
            def _(pe):
                def query(i):
                    if not (isinstance(i, int) and i == 0):
                        pe.wait_ge(q_dve, i)
                        pe.wait_ge(q_act, i)
                    x = m.pieces[:, ds(i, 1), WINDOW:PIECE].rearrange("p a n -> p (a n)")
                    for h in range(4, HEADS):
                        mm = nc.tensor.matmul(q_ps[:, h, :], m.win_qk[:, h, :], x, start=True, stop=True)
                    mm.then_inc(q_ok, 1)
                    if not (isinstance(i, int) and i <= 1):
                        pe.wait_ge(xt_c, i)
                    elif i == 1:
                        pe.wait_ge(xt_c, 1)
                    for h in range(4):
                        mm = nc.tensor.matmul(q_ps[:, h, :], m.win_qk[:, h, :], x, start=True, stop=True)
                    mm.then_inc(q_ok, 1)

                def windows_turned(i):
                    pe.wait_ge(q_act, i + 1)
                    pe.wait_ge(win_ok, i * 4 + 4)
                    for w in range(NW):
                        mm = nc.tensor.transpose(xt_ps[:, w, :], m.win_x[:, w, :, :].rearrange("p a n -> p (a n)"), m.ident[:, :])
                    mm.then_inc(xt_ok, 1)

                def scores(i):
                    pe.wait_ge(win_ok, i * 4 + 4)
                    pe.wait_ge(q_act, i + 1)
                    pe.wait_ge(q_dve, i + 1)
                    if not (isinstance(i, int) and i == 0):
                        pe.wait_ge(sub_ok, i * HG)
                    for hg in range(HG):
                        nc.tensor.matmul(s_ps[:, hg, :, :].rearrange("p w n -> p (w n)"), m.ident_bf[:, :], m.win_mask[:, :], start=True, stop=False)
                        for w in range(NW):
                            mm = nc.tensor.matmul(s_ps[:, hg, w, :], queries[:, w, 4 * hg:4 * hg + 4, :].rearrange("p h n -> p (h n)"),
                                                  m.win_x[:, w, :, :].rearrange("p a n -> p (a n)"), start=False, stop=(w == NW - 1))
                    mm.then_inc(s_ok, 1)

                def turn_probs(i):
                    pe.wait_ge(p_ok, i + 1)
                    if not (isinstance(i, int) and i == 0):
                        pe.wait_ge(zt_c, i)
                    for hg in range(HG):
                        for w in range(NW):
                            mm = nc.tensor.transpose(t_ps[:, hg, w, :], probs[:, hg, w, :], m.ident[:, :])
                    mm.then_inc(pt_ok, 1)

                def output(i):
                    pe.wait_ge(zt_c, i + 1)
                    for h in range(HEADS):
                        mm = nc.tensor.matmul(o_ps, m.win_vo[:, h, :], heads_t[:, h // 4, :, (h % 4) * WINDOW:(h % 4 + 1) * WINDOW],
                                              start=(h == 0), stop=(h == HEADS - 1))
                    mm.then_inc(o_ok, 1)

                def attend(i, odd):
                    pe.wait_ge(pt_act, i + 1)
                    pe.wait_ge(pt_dve, i + 1)
                    pe.wait_ge(xt_c, i + 1)
                    if not (isinstance(i, int) and i == 0):
                        pe.wait_ge(o_c, i)
                    for hg in range(HG):
                        for w in range(NW):
                            mm = nc.tensor.matmul(z_ps[:, hg, w, :], probs_t[:, hg, w, :], xt[odd][:, w, :], start=True, stop=True)
                    mm.then_inc(z_ok, 1)

                def turn_heads(i):
                    pe.wait_ge(n_ok, i + 1)
                    for hg in range(HG):
                        for w in range(NW):
                            mm = nc.tensor.transpose(t_ps[:, hg, w, :], heads[:, hg, w, :], m.ident[:, :])
                    mm.then_inc(zt_ok, 1)

                def body(i, odd):
                    if loops(i, 1):
                        scores(i + 1)
                    if loops(i, -1):
                        output(i - 1)
                    turn_probs(i)
                    if loops(i, 1):
                        windows_turned(i + 1)
                    attend(i, odd)
                    if loops(i, 2):
                        query(i + 2)
                    turn_heads(i)

                query(0)
                scores(0)
                windows_turned(0)
                query(1)
                pipeline(pe, body)
                output(LAST)

            @block.scalar
            def _(act):
                def take_queries(i):
                    act.wait_ge(q_ok, i * 2 + 2)
                    if not (isinstance(i, int) and i == 0):
                        act.wait_ge(s_ok, i)
                    nc.scalar.activation(queries[:, :, 0:4, :], q_ps[:, 0:4, :].rearrange("p h (w n) -> p w h n", w=NW), ACT.Copy).then_inc(q_act, 1)

                def take_windows(i, odd):
                    act.wait_ge(xt_ok, i + 1)
                    if not (isinstance(i, int) and i <= 1):
                        act.wait_ge(z_ok, i - 1)
                    nc.scalar.activation(xt[odd][:, :, :], xt_ps, ACT.Copy).then_inc(xt_c, 1)

                def exps(i):
                    act.wait_ge(sub_ok, (i + 1) * HG)
                    if not (isinstance(i, int) and i == 0):
                        act.wait_ge(pt_ok, i)
                        act.wait_ge(sum_ok, i)
                    nc.scalar.activation(probs[:, :, :, :], shifted[:, :, :, :], ACT.Exp).then_inc(p_ok, 1)

                def take_probs(i):
                    act.wait_ge(pt_ok, i + 1)
                    nc.scalar.activation(probs_t[:, 0, :, :], t_ps[:, 0, :, :], ACT.Copy).then_inc(pt_act, 1)

                def take_heads(i):
                    act.wait_ge(zt_ok, i + 1)
                    if not (isinstance(i, int) and i == 0):
                        act.wait_ge(o_ok, i)
                    nc.scalar.activation(heads_t[:, :, :, :], t_ps[:, :, :, :], ACT.Copy).then_inc(zt_c, 1)

                def body(i, odd):
                    take_probs(i)
                    if loops(i, 1):
                        take_windows(i + 1, 1 - odd)
                        exps(i + 1)
                    if loops(i, 2):
                        take_queries(i + 2)
                    take_heads(i)

                take_queries(0)
                exps(0)
                take_windows(0, 0)
                take_queries(1)
                pipeline(act, body)

            @block.vector
            def _(dve):
                def take_queries(i):
                    dve.wait_ge(q_ok, i * 2 + 1)
                    if not (isinstance(i, int) and i == 0):
                        dve.wait_ge(s_ok, i)
                    nc.vector.tensor_copy(queries[:, :, 4:HEADS, :], q_ps[:, 4:HEADS, :].rearrange("p h (w n) -> p w h n", w=NW)).then_inc(q_dve, 1)

                def shift(i):
                    dve.wait_ge(s_ok, i + 1)
                    nc.vector.tensor_reduce(rmax[:, :], s_ps[:, :, :, :].rearrange("p g w (a n) -> p (g w a) n", a=2), axis=AX.X, op=ALU.max).then_inc(max_ok, 1)
                    dve.wait_ge(max_ok, i + 1)
                    if not (isinstance(i, int) and i == 0):
                        dve.wait_ge(p_ok, i)
                    for hg in range(HG):
                        half = rmax[:, hg * (NT // HG):(hg + 1) * (NT // HG)]
                        nc.vector.tensor_tensor(shifted[:, hg, :, :].rearrange("p w (a n) -> p (w a) n", a=2),
                                                s_ps[:, hg, :, :].rearrange("p w (a n) -> p (w a) n", a=2),
                                                half.to_broadcast([P, NT // HG, KEYS]), ALU.subtract).then_inc(sub_ok, 1)

                def sums(i):
                    dve.wait_ge(p_ok, i + 1)
                    nc.vector.tensor_reduce(rsum[:, :], probs[:, :, :, :].rearrange("p g w (a n) -> p (g w a) n", a=2), axis=AX.X, op=ALU.add).then_inc(sum_ok, 1)
                    dve.wait_ge(sum_ok, i + 1)
                    nc.vector.reciprocal(rinv[:, :], rsum[:, :]).then_inc(inv_ok, 1)

                def take_probs(i):
                    dve.wait_ge(pt_ok, i + 1)
                    nc.vector.tensor_copy(probs_t[:, 1, :, :], t_ps[:, 1, :, :]).then_inc(pt_dve, 1)

                def normalise(i):
                    dve.wait_ge(z_ok, i + 1)
                    dve.wait_ge(inv_ok, i + 1)
                    nc.vector.tensor_tensor(heads[:, :, :, :].rearrange("p g w (a n) -> p (g w a) n", a=2),
                                            z_ps[:, :, :, :].rearrange("p g w (a n) -> p (g w a) n", a=2),
                                            rinv[:, :].to_broadcast([P, NT, C]), ALU.mult).then_inc(n_ok, 1)

                def add(i):
                    dve.wait_ge(o_ok, i + 1)
                    x = m.x_flat[:, ds(i * CHUNK, CHUNK)]
                    nc.vector.scalar_tensor_tensor(out=x, in0=o_ps, scalar=m.win_bias[:, 0:1], in1=x, op0=ALU.add, op1=ALU.add).then_inc(o_c, 1)

                def body(i, odd):
                    sums(i)
                    if loops(i, -1):
                        add(i - 1)
                    take_probs(i)
                    if loops(i, 1):
                        shift(i + 1)
                    normalise(i)
                    if loops(i, 2):
                        take_queries(i + 2)

                take_queries(0)
                shift(0)
                take_queries(1)
                pipeline(dve, body)
                add(LAST)


FILTERS = 16
SCALES = 4
AR = 3
SPAN = 2 * P
SPANS = T // SPAN
PIECES16 = 2
PHI_ROW = SPAN + T
PRODUCTS = ((0, 0), (0, 1), (1, 0))
SEGMENTS = [(0, T >> 3), (T >> 3, T >> 3), (T >> 2, T >> 2), (T >> 1, T >> 1)]


def spectral_norm_stage(nc, m):
    def piece(t, k):
        return m.normed[:, ds(t * 8 + k * 4, 4), :]
    layernorm_stage(nc, m, piece, "s")


def spectral_stage(nc, m):
    KP = FILTERS // 2
    with ExitStack() as ctx:
        sb, pb, sem = open_pools(nc, ctx)
        u = sb("sp_u", [P, T])
        apart = sb("sp_apart", [P, 2, AR - 1 + T])
        ut = sb("sp_ut", [P, PIECES16, 2, SPANS, 2, C], F16)
        sums = [sb(f"sp_sums{k}", [P, 2, T]) for k in range(2)]
        mixk = [sb(f"sp_mix{k}", [P, SCALES, 2, C]) for k in range(2)]
        f_ps = [pb(f"sp_f{b}", [P, T]) for b in range(2)]
        o_ps = pb("sp_o", [P, 2, 2, T // 4])
        (u_ok, apart_ok, ut_hi, ut_ok, ut_c, f_ok, f_act, f_dve, mk_ok, mix_ok, ar_ok, o_c, zero, first_ok) = (sem("st_" + n) for n in (
            "u", "apart", "ut_high", "ut", "ut_taken", "filtered", "taken_act", "taken_dve", "mix_in", "mixed", "ar_done", "added", "zeroed", "first"))

        def out_of(lo, cnt, par):
            half, first = lo // (T // 2), lo % (T // 2) // 2
            return o_ps[HALF[par], half, :, first:first + cnt // 2]

        def tokens(piece, i):
            return ut[:, piece, :, 2 * i:2 * i + 2, :, :].rearrange("p b i a c -> p b (i a) c")

        def turned(i):
            return f_ps[i][:, 0:BANK].rearrange("p (i b c) -> p b i c", b=2, c=C)

        with nc.Block() as block:
            @block.gpsimd
            def _(pool):
                nc.gpsimd.memset(apart[:, :, :], 0.0).then_inc(zero, 1)
                pool.wait_ge(zero, 1)
                with pool.Fori(0, G) as g:
                    pool.wait_ge(ar_ok, g + 1)
                    nc.gpsimd.tensor_copy(u[:, ::-1], m.normed[:, ds(g * (T // 128), T // 128), :].rearrange("p n t -> p (n t)")).then_inc(u_ok, 1)

            @block.tensor
            def _(pe):
                pe.sem_inc(mix_ok, 2)
                pe.sem_inc(ar_ok, 1)
                pe.wait_ge(first_ok, 1)
                pe.wait_ge(m.table_in, 16 * PIECES16 * FILTERS)
                with pe.Fori(0, G) as g:
                    pe.wait_ge(u_ok, g + 1)
                    pe.wait_ge(f_act, g * (2 * FILTERS) + 2)
                    pe.wait_ge(f_dve, g * (2 * FILTERS) + 2)
                    for i in range(SPANS):
                        for par in range(2):
                            first = SPAN * (SPANS - 1 - i) + 1 - par
                            mm = nc.tensor.transpose(f_ps[i // 2][:, (i % 2) * SPAN + par * P:(i % 2) * SPAN + (par + 1) * P],
                                                     u[:, first:first + SPAN - 1:2], m.ident[:, :])
                        mm.then_inc(ut_ok, 1)
                    pe.wait_ge(ut_c, g * 2 + 2)
                    pe.wait_ge(apart_ok, g * 2 + 2)
                    pe.wait_ge(o_c, g + 1)
                    opened = set()
                    for tap in range(AR):
                        for seg, (lo, cnt) in enumerate(SEGMENTS):
                            for par in range(2):
                                first = AR - 1 - tap + lo + par
                                bank = (lo // (T // 2), par)
                                mm = nc.tensor.matmul(out_of(lo, cnt, par), m.ar[:, SCALES - 1 - seg, tap * C:(tap + 1) * C],
                                                      apart[:, :, first:first + cnt - 1:2], start=bank not in opened, stop=False, skip_group_check=True)
                                opened.add(bank)
                    mm.then_inc(ar_ok, 1)

                    def filtered(j, n):
                        for b in range(2):
                            pe.wait_ge(f_act, g * (2 * FILTERS) + j * 4 + (2 * n + b + 1))
                            pe.wait_ge(f_dve, g * (2 * FILTERS) + j * 4 + (2 * n + b + 1))
                            for half in range(2):
                                spans = [i for i in range(SPANS) if i * SPAN < (half + 1) * BANK]
                                for i in spans:
                                    lo = max(half * BANK, i * SPAN)
                                    for hu, hf in PRODUCTS:
                                        mm = nc.tensor.matmul(f_ps[b][:, lo:(half + 1) * BANK], ut[:, hu, b, i, :, :].rearrange("p a c -> p (a c)"),
                                                              m.hankel[:, hf, ds(j * 2 + n, 1), lo - i * SPAN:(half + 1) * BANK - i * SPAN].rearrange("p k t -> p (k t)"),
                                                              start=(i == 0 and (hu, hf) == PRODUCTS[0]), stop=(i == spans[-1] and (hu, hf) == PRODUCTS[-1]))
                            mm.then_inc(f_ok, 1)

                    def mixed(j, n):
                        pe.wait_ge(mk_ok, g * FILTERS + j * 2 + (n + 1))
                        pe.wait_ge(f_act, g * (2 * FILTERS) + j * 4 + (2 * n + 2 + 2))
                        pe.wait_ge(f_dve, g * (2 * FILTERS) + j * 4 + (2 * n + 2 + 2))
                        for seg, (lo, cnt) in enumerate(SEGMENTS):
                            for par in range(2):
                                mm = nc.tensor.matmul(out_of(lo, cnt, par), mixk[n][:, SCALES - 1 - seg, par, :], sums[n][:, :, lo + par:lo + cnt:2],
                                                      start=False, stop=False, skip_group_check=True)
                        mm.then_inc(mix_ok, 1)

                    with pe.Fori(0, KP) as j:
                        filtered(j, 0)
                        filtered(j, 1)
                        mixed(j, 0)
                        mixed(j, 1)

            @block.scalar
            def _(act):
                act.sem_inc(f_act, 2)
                act.wait_ge(zero, 1)
                with act.Fori(0, G) as g:
                    act.wait_ge(ar_ok, g + 1)
                    source = m.normed[:, ds(g * (T // 128), T // 128), :].rearrange("p n t -> p (n t)")
                    for b in range(2):
                        nc.scalar.copy(apart[HALF[b], b, AR - 1:], source[HALF[b], :]).then_inc(apart_ok, 1)
                    act.wait_ge(ut_ok, g * 4 + 4)
                    for i in range(2):
                        nc.scalar.copy(tokens(0, i), turned(i)).then_inc(ut_hi, 1)
                    with act.Fori(0, KP) as j:
                        for n in range(2):
                            for b in range(2):
                                act.wait_ge(f_ok, g * (2 * FILTERS) + j * 4 + (2 * n + b + 1))
                                if b == 0:
                                    act.wait_ge(mix_ok, g * FILTERS + j * 2 + (n + 1))
                                nc.scalar.copy(sums[n][HALF[1], b, 1:T], f_ps[b][HALF[1], 0:T - 1]).then_inc(f_act, 1)

            @block.vector
            def _(dve):
                for n in range(2):
                    last = nc.vector.memset(sums[n][HALF[1], :, 0:1], 0.0)
                last.then_inc(first_ok, 1)
                dve.sem_inc(f_dve, 2)
                dve.sem_inc(o_c, 1)
                with dve.Fori(0, G) as g:
                    for i in range(2):
                        dve.wait_ge(ut_hi, g * 2 + (i + 1))
                        nc.vector.tensor_tensor(tokens(1, i), turned(i), tokens(0, i), ALU.subtract).then_inc(ut_c, 1)
                    with dve.Fori(0, KP) as j:
                        for n in range(2):
                            for b in range(2):
                                dve.wait_ge(f_ok, g * (2 * FILTERS) + j * 4 + (2 * n + b + 1))
                                if b == 0:
                                    dve.wait_ge(mix_ok, g * FILTERS + j * 2 + (n + 1))
                                    nc.vector.tensor_copy(mixk[n][:, :, :, :].rearrange("p s a e -> p (s a e)"),
                                                          m.mix[:, ds(j * 2 + n, 1), :, :, :].rearrange("p k s a e -> p (k s a e)")).then_inc(mk_ok, 1)
                                nc.vector.tensor_copy(sums[n][HALF[0], b, :], f_ps[b][HALF[0], :]).then_inc(f_dve, 1)
                    dve.wait_ge(mix_ok, g * FILTERS + (FILTERS + 2))
                    for b in range(2):
                        for par in range(2):
                            x = m.x[HALF[b], ds(g, 1), par::2].rearrange("c g (h n) -> c (g h) n", h=2)
                            last = nc.vector.tensor_tensor(x, o_ps[HALF[par], :, b, :], x, ALU.add)
                    last.then_inc(o_c, 1)


HEAD_DIM = C // HEADS
TILES = T // P


def norm_stage(nc, m, tag):
    def piece(t, k):
        return m.normed[:, ds(t * 8 + k * 4, 4), :]
    layernorm_stage(nc, m, piece, tag)


def linear_attention_stage(nc, m):
    NH = P // HEAD_DIM
    with ExitStack() as ctx:
        sb, pb, sem = open_pools(nc, ctx)
        xg = sb("lin_xg", [P, T])
        kv = sb("lin_kvb", [P, TILES, 2 * P + 1])
        key_e = sb("lin_key_e", [P, TILES, P])
        q_e, q_r = sb("lin_q_e", [P, T]), sb("lin_q_r", [P, T])
        sums = sb("lin_sums", [P, P + NH])
        inv = sb("lin_inv", [P, TILES, NH])
        heads = sb("lin_heads", [P, TILES, P])
        heads_t = sb("lin_heads_t", [P, T])
        big = [pb(f"lin_big{k}", [P, 4, 2 * P]) for k in range(2)]
        q_ps = pb("lin_qps", [P, T])
        s_ps = pb("lin_sps", [P, BANK])
        (x_ok, kv_ok, kv_c, ke_ok, phi_ok, q_ok, qe_ok, qr_ok, pq_ok, s_ok, s_c, v_ok, d_ok, i_ok, h_ok, t_ok, t_c, o_ok, o_c, ones_ok, ksum) = (
            sem("l_" + n) for n in ("x", "kv", "kv_taken", "key_exp", "phi_k", "q", "q_exp", "q_relu", "phi_q", "sums", "sums_masked", "heads", "den",
                                    "inv", "normed", "turned", "turned_taken", "out", "added", "ones", "ksum"))
        with nc.Block() as block:
            @block.tensor
            def _(pe):
                with pe.Fori(0, G) as g:
                    pe.wait_ge(x_ok, g + 1)
                    for half in range(2):
                        for t in range(4):
                            tile = half * 4 + t
                            mm = nc.tensor.matmul(big[half][:, t, :], xg[:, tile * P:(tile + 1) * P], m.lin_kv[:, :, :].rearrange("p a c -> p (a c)"), start=True, stop=True)
                        mm.then_inc(kv_ok, 1)
                    for c in range(2):
                        mm = nc.tensor.matmul(q_ps[:, c * BANK:(c + 1) * BANK], m.lin_q[:, :], xg[:, c * BANK:(c + 1) * BANK], start=True, stop=True)
                    mm.then_inc(q_ok, 1)
                    pe.wait_ge(phi_ok, g + 1)
                    for t in range(TILES):
                        mm = nc.tensor.matmul(s_ps[:, 0:P + 1], kv[:, t, 0:P], kv[:, t, P:2 * P + 1], start=(t == 0), stop=(t == TILES - 1))
                    mm.then_inc(s_ok, 1)
                    pe.wait_ge(pq_ok, g + 1)
                    pe.wait_ge(s_c, g + 1)
                    for half in range(2):
                        for t in range(4):
                            tile = half * 4 + t
                            mm = nc.tensor.matmul(big[half][:, t, 0:P + NH], q_e[:, tile * P:(tile + 1) * P], sums[:, :], start=True, stop=True)
                        mm.then_inc(v_ok, 1)
                    for half in range(2):
                        pe.wait_ge(h_ok, g * 2 + (half + 1))
                        for t in range(4):
                            tile = half * 4 + t
                            mm = nc.tensor.transpose(q_ps[:, tile * P:(tile + 1) * P], heads[:, tile, :], m.ident[:, :])
                        mm.then_inc(t_ok, 1)
                    for c in range(2):
                        pe.wait_ge(t_c, g * 2 + (c + 1))
                        out = big[0][:, 2 * c:2 * c + 2, :].rearrange("p a c -> p (a c)")
                        nc.tensor.matmul(out, m.lin_o[:, :], heads_t[:, c * BANK:(c + 1) * BANK], start=True, stop=True).then_inc(o_ok, 1)
                    pe.wait_ge(o_c, g * 2 + 2)

            @block.scalar
            def _(act):
                nc.scalar.activation(kv[:, :, 2 * P:2 * P + 1], m.ident[:, 0:TILES].rearrange("p (t a) -> p t a", a=1), ACT.Exp, scale=0.0).then_inc(ones_ok, 1)
                with act.Fori(0, G) as g:
                    act.wait_ge(o_c, g * 2 + 2)
                    nc.scalar.copy(xg[:, :], m.normed[:, ds(g * (T // 128), T // 128), :].rearrange("p n t -> p (n t)")).then_inc(x_ok, 1)
                    for half in range(2):
                        act.wait_ge(kv_c, g * 2 + (half + 1))
                        nc.scalar.activation(key_e[:, half * 4:half * 4 + 4, :], kv[:, half * 4:half * 4 + 4, 0:P], ACT.Exp).then_inc(ke_ok, 1)
                    act.wait_ge(q_ok, g + 1)
                    nc.scalar.activation(q_e[:, :], q_ps[:, :], ACT.Exp, bias=m.lin_bias[:, 0:1]).then_inc(qe_ok, 1)
                    for half in range(2):
                        act.wait_ge(t_ok, g * 2 + (half + 1))
                        nc.scalar.copy(heads_t[:, half * BANK:(half + 1) * BANK], q_ps[:, half * BANK:(half + 1) * BANK]).then_inc(t_c, 1)

            @block.vector
            def _(dve):
                dve.sem_inc(o_c, 2)
                with dve.Fori(0, G) as g:
                    for half in range(2):
                        dve.wait_ge(kv_ok, g * 2 + (half + 1))
                        nc.vector.tensor_tensor(kv[:, half * 4:half * 4 + 4, 0:2 * P], big[half][:, :, :],
                                                m.lin_rows[:, :, :].rearrange("p a (b c) -> p b (a c)", b=1).to_broadcast([P, 4, 2 * P]), ALU.add).then_inc(kv_c, 1)
                    dve.wait_ge(qe_ok, g + 1)
                    nc.vector.tensor_scalar(q_r[:, :], q_ps[:, :], m.lin_bias[:, 0:1], 0.0, ALU.add, ALU.max).then_inc(qr_ok, 1)
                    dve.wait_ge(ke_ok, g * 2 + 2)
                    nc.vector.tensor_scalar(key_e[:, :, :], key_e[:, :, :], 1.0, None, ALU.min).then_inc(i_ok, 1)
                    dve.wait_ge(i_ok, g + 1)
                    nc.vector.scalar_tensor_tensor(out=kv[:, :, 0:P], in0=kv[:, :, 0:P], scalar=0.0, in1=key_e[:, :, :], op0=ALU.max, op1=ALU.add).then_inc(phi_ok, 1)
                    dve.wait_ge(qr_ok, g + 1)
                    nc.vector.scalar_tensor_tensor(out=q_e[:, :], in0=q_e[:, :], scalar=1.0, in1=q_r[:, :], op0=ALU.min, op1=ALU.add).then_inc(pq_ok, 1)
                    dve.wait_ge(s_ok, g + 1)
                    nc.vector.tensor_tensor(sums[:, 0:P], s_ps[:, 0:P], m.lin_mask[:, :], ALU.mult).then_inc(ksum, 1)
                    nc.vector.tensor_scalar(sums[:, P:P + NH], m.lin_mask[:, ::HEAD_DIM], s_ps[:, P:P + 1], None, ALU.mult).then_inc(s_c, 1)
                    for half in range(2):
                        part = inv[:, half * 4:half * 4 + 4, :]
                        dve.wait_ge(v_ok, g * 2 + (half + 1))
                        nc.vector.tensor_scalar(part, big[half][:, :, P:P + NH], m.eps[:, 0:1], None, ALU.add).then_inc(d_ok, 1)
                        dve.wait_ge(d_ok, g * 4 + (2 * half + 1))
                        nc.vector.reciprocal(part, part).then_inc(d_ok, 1)
                        dve.wait_ge(d_ok, g * 4 + (2 * half + 2))
                        for t in range(4):
                            tile = half * 4 + t
                            last = nc.vector.tensor_tensor(heads[:, tile, :].rearrange("p (h d) -> p h d", d=HEAD_DIM),
                                                           big[half][:, t, 0:P].rearrange("p (h d) -> p h d", d=HEAD_DIM),
                                                           inv[:, tile, :].to_broadcast([P, NH, HEAD_DIM]), ALU.mult)
                        last.then_inc(h_ok, 1)
                    for c in range(2):
                        dve.wait_ge(o_ok, g * 2 + (c + 1))
                        x = m.x_flat[:, ds(g * T + c * BANK, BANK)]
                        nc.vector.scalar_tensor_tensor(out=x, in0=big[0][:, 2 * c:2 * c + 2, :].rearrange("p a c -> p (a c)"), scalar=m.lin_bias[:, 1:2], in1=x,
                                                       op0=ALU.add, op1=ALU.add).then_inc(o_c, 1)


EXPERTS = 32
HIDDEN = 256
HT = HIDDEN // P
TOP = 8
QUADS = B // 4


def expert_stage(nc, m, ins, out):
    with ExitStack() as ctx:
        sb, pb, sem = open_pools(nc, ctx)
        gate = sb("gate_w", [EXPERTS, C])
        gate_t = sb("gate_t", [P, 2 * EXPERTS])
        gate_b = sb("gate_b", [P, 1])
        b2 = sb("ex_b2", [EXPERTS, C])
        b2_t = sb("ex_b2_t", [C, EXPERTS])
        logits = [sb(f"ex_logits{q}", [P, T]) for q in range(QUADS)]
        probs = [sb(f"ex_probs{q}", [P, T]) for q in range(QUADS)]
        kept_t = [sb(f"ex_kept_t{q}", [P, TILES, P]) for q in range(QUADS)]
        xt = sb("ex_xt", [P, G, TILES, P])
        top = [sb(f"ex_top{q}", [P, TOP]) for q in range(QUADS)]
        stat = sb("ex_stat", [P, QUADS, 4])
        pooled = sb("ex_pooled", [C + 1, EXPERTS, B])
        hidden = sb("ex_hidden", [P, EXPERTS, HT, B])
        made = sb("ex_made", [C, B, EXPERTS])
        spread = sb("ex_spread", [P, G, P])
        l_ps = [pb(f"ex_l{q}", [P, T]) for q in range(QUADS)]
        t_ps = [pb(f"ex_t{q}", [P, BANK]) for q in range(2)]
        a_ps, b_ps = pb("ex_a", [P, BANK]), pb("ex_b", [P, BANK])
        kept = logits
        (w_in, g_t, g_c, zeroed, l_ok, x_t, x_c, lg_ok, mx_ok, e_ok, step, keep_ok, k_t, k_c, p_ok, p_c, h_ok, h_c, m_ok, m_c, s_t, s_c, o_ok, o_c, done, b_c) = (
            sem("e_" + n) for n in ("w_in", "gate_turned", "gate_taken", "zeroed", "logits", "x_turned", "x_taken", "lg", "max", "exp", "step", "kept", "kept_turned",
                                    "kept_taken", "pooled", "pooled_taken", "hidden", "gelu", "made", "made_taken", "spread_turned", "spread", "out", "added", "stored", "b2"))
        with nc.Block() as block:
            @block.sync
            def _(sp):
                sp.dma_start(gate[:, :], ins["L3_ffn_gate_w"]).then_inc(w_in, 16)
                for q in range(4):
                    sp.dma_start(gate_b[q * EXPERTS:(q + 1) * EXPERTS, :], ins["L3_ffn_gate_b"].rearrange("(e a) -> e a", a=1)).then_inc(w_in, 16)
                sp.dma_start(b2[:, :], ins["L3_ffn_weight2"][:, HIDDEN, :]).then_inc(w_in, 16)
                for g in range(G):
                    sp.wait_ge(o_c, 2 * g + 2)
                    for p in range(2):
                        sp.dma_start(out[2 * g + p].rearrange("c h w -> c (h w)"), m.x[HALF[p], g, :]).then_inc(done, 16)
                sp.wait_ge(done, 16 * B)

            @block.gpsimd
            def _(pool):
                nc.gpsimd.memset(gate_t[:, :], 0.0).then_inc(zeroed, 1)
                nc.gpsimd.memset(spread[:, :, :], 0.0).then_inc(zeroed, 1)
                pool.wait_ge(zeroed, 2)
                nc.gpsimd.memset(pooled[C:C + 1, :, :], 1.0).then_inc(zeroed, 1)

            @block.tensor
            def _(pe):
                pe.wait_ge(w_in, 96)
                for p in range(2):
                    mm = nc.tensor.transpose(a_ps[0:C, p * EXPERTS:(p + 1) * EXPERTS], (gate, b2)[p][:, :], m.ident[0:EXPERTS, 0:EXPERTS])
                mm.then_inc(g_t, 1)
                for n in range(G * 2):
                    g, half = n // 2, n % 2
                    if n == 1:
                        pe.wait_ge(g_c, 2)
                        for gg in range(G):
                            for c in range(2):
                                mm = nc.tensor.matmul(l_ps[gg // 2][(gg % 2) * C:(gg % 2 + 1) * C, c * BANK:(c + 1) * BANK], gate_t[:, :],
                                                      m.normed[:, gg * 8 + c * 4:gg * 8 + c * 4 + 4, :].rearrange("p n t -> p (n t)"), start=True, stop=True)
                            mm.then_inc(l_ok, 1)
                    if n >= 2:
                        pe.wait_ge(x_c, n - 1)
                    for t in range(4):
                        mm = nc.tensor.transpose(t_ps[n % 2][:, t * P:(t + 1) * P], m.normed[:, g * 8 + half * 4 + t, :], m.ident[:, :])
                    mm.then_inc(x_t, 1)
                pe.wait_ge(x_c, 2 * G)
                for q in range(QUADS):
                    pe.wait_ge(keep_ok, q + 1)
                    for half in range(2):
                        if q:
                            pe.wait_ge(k_c, half + 1)
                        for t in range(4):
                            tile = half * 4 + t
                            mm = nc.tensor.transpose(t_ps[half][:, t * P:(t + 1) * P], kept[q][:, tile * P:(tile + 1) * P], m.ident[:, :])
                        mm.then_inc(k_t, 1)
                for g in range(G):
                    if g % 2 == 0:
                        pe.wait_ge(k_c, g + 2)
                    for t in range(TILES):
                        mm = nc.tensor.matmul(b_ps[:, g * P:(g + 1) * P], xt[:, g, t, :], kept_t[g // 2][:, t, :], start=(t == 0), stop=(t == TILES - 1))
                    mm.then_inc(p_ok, 1)
                pe.wait_ge(p_c, B)
                pe.wait_ge(m.ex_in, 16 * 3)
                for e in range(EXPERTS):
                    for t in range(HT):
                        mm = nc.tensor.matmul(a_ps[:, :].rearrange("p (e t b) -> p e t b", e=EXPERTS, t=HT)[:, e, t, :], m.ex_w1[:, e, t * P:(t + 1) * P],
                                              pooled[:, e, :], start=True, stop=True)
                mm.then_inc(h_ok, 1)
                pe.wait_ge(h_c, 1)
                for e in range(EXPERTS):
                    for t in range(HT):
                        mm = nc.tensor.matmul(b_ps[0:C, e * B:(e + 1) * B], m.ex_w2[:, e, t, :], hidden[:, e, t, :], start=(t == 0), stop=(t == HT - 1))
                mm.then_inc(m_ok, 1)
                pe.wait_ge(m_c, 1)
                for q in range(QUADS):
                    mm = nc.tensor.transpose(a_ps[:, q * C:(q + 1) * C], made[:, 4 * q:4 * q + 4, :].rearrange("c b e -> c (b e)"), m.ident[0:C, 0:C])
                mm.then_inc(s_t, 1)
                pe.wait_ge(s_c, B)
                for g in range(G):
                    for c in range(2):
                        n = 2 * g + c
                        if n >= 2:
                            pe.wait_ge(o_c, n - 1)
                        nc.tensor.matmul(t_ps[n % 2][:, :], spread[:, g, :], kept[g // 2][:, c * BANK:(c + 1) * BANK], start=True, stop=True).then_inc(o_ok, 1)

            @block.scalar
            def _(act):
                for n in range(2 * G):
                    g, half = n // 2, n % 2
                    act.wait_ge(x_t, n + 1)
                    nc.scalar.copy(xt[:, g, half * 4:half * 4 + 4, :], t_ps[n % 2][:, :].rearrange("p (t c) -> p t c", c=P)).then_inc(x_c, 1)
                for q in range(QUADS):
                    act.wait_ge(mx_ok, q + 1)
                    nc.scalar.activation(probs[q][:, :], logits[q][:, :], ACT.Exp, bias=stat[:, q, 0:1], accum_out=stat[:, q, 1:2]).then_inc(e_ok, 1)
                for q in range(QUADS):
                    for half in range(2):
                        act.wait_ge(k_t, 2 * q + half + 1)
                        nc.scalar.copy(kept_t[q][:, half * 4:half * 4 + 4, :], t_ps[half][:, :].rearrange("p (t c) -> p t c", c=P)).then_inc(k_c, 1)
                act.wait_ge(h_ok, 1)
                nc.scalar.activation(hidden[:, :, :, :], a_ps[:, :].rearrange("p (e t b) -> p e t b", e=EXPERTS, t=HT), ACT.Gelu).then_inc(h_c, 1)

            @block.vector
            def _(dve):
                dve.wait_ge(g_t, 1)
                dve.wait_ge(zeroed, 3)
                for p in range(2):
                    nc.vector.tensor_copy(gate_t[HALF[p], p * EXPERTS:(p + 1) * EXPERTS], a_ps[0:C, 0:EXPERTS]).then_inc(g_c, 1)
                nc.vector.tensor_copy(b2_t[:, :], a_ps[0:C, EXPERTS:2 * EXPERTS]).then_inc(b_c, 1)
                dve.wait_ge(w_in, 96)
                for q in range(QUADS):
                    dve.wait_ge(l_ok, 2 * q + 2)
                    nc.vector.tensor_scalar(logits[q][:, :], l_ps[q][:, :], gate_b[:, 0:1], None, ALU.add).then_inc(lg_ok, 1)
                    dve.wait_ge(lg_ok, q + 1)
                    nc.vector.tensor_reduce(stat[:, q, 0:1], logits[q][:, :], axis=AX.X, op=ALU.max, negate=True).then_inc(mx_ok, 1)
                n = 0
                for q in range(QUADS):
                    def link(ins_):
                        nonlocal n
                        n += 1
                        ins_.then_inc(step, 1)
                        dve.wait_ge(step, n)
                    dve.wait_ge(e_ok, q + 1)
                    link(nc.vector.reciprocal(stat[:, q, 2:3], stat[:, q, 1:2]))
                    link(nc.vector.tensor_scalar(probs[q][:, :], probs[q][:, :], stat[:, q, 2:3], None, ALU.mult))
                    link(nc.vector.max(top[q][:, :], probs[q][:, :]))
                    link(nc.vector.match_replace(kept[q][:, :], top[q][:, :], probs[q][:, :], 0.0))
                    nc.vector.tensor_tensor(kept[q][:, :], probs[q][:, :], kept[q][:, :], ALU.subtract).then_inc(keep_ok, 1)
                dve.wait_ge(p_ok, G)
                for g in range(G):
                    for p in range(2):
                        b = 2 * g + p
                        src = b_ps[HALF[p], g * P + (b % 4) * EXPERTS:g * P + (b % 4 + 1) * EXPERTS]
                        nc.vector.tensor_copy(pooled[0:C, :, b], src).then_inc(p_c, 1)
                dve.wait_ge(m_ok, 1)
                nc.vector.tensor_tensor(made[:, :, :].rearrange("c b e -> c e b"), b_ps[0:C, 0:B * EXPERTS].rearrange("c (e b) -> c e b", b=B),
                                        b2_t[:, :].to_broadcast([C, EXPERTS, B]), ALU.add).then_inc(m_c, 1)
                dve.wait_ge(s_t, 1)
                for b in range(B):
                    rows = slice((b % 4) * EXPERTS, (b % 4 + 1) * EXPERTS)
                    nc.vector.tensor_copy(spread[rows, b // 2, (b % 2) * C:(b % 2 + 1) * C], a_ps[rows, (b // 4) * C:(b // 4 + 1) * C]).then_inc(s_c, 1)
                for n in range(2 * G):
                    dve.wait_ge(o_ok, n + 1)
                    x = m.x_flat[:, n * BANK:(n + 1) * BANK]
                    nc.vector.tensor_tensor(x, t_ps[n % 2][:, :], x, ALU.add).then_inc(o_c, 1)


def expert_load(nc, m, ins, eng):
    eng.dma_start(m.ex_w1[:, :, :], ins["L3_ffn_weight1"].rearrange("e d h -> d e h")).then_inc(m.ex_in, 16)
    for t in range(HT):
        eng.dma_start(m.ex_w2[:, :, t, :], ins["L3_ffn_weight2"][:, t * P:(t + 1) * P, :].rearrange("e h o -> h e o")).then_inc(m.ex_in, 16)


TINY = 1e-30


def weights_stage(nc, m, ins, phi_rows):
    with ExitStack() as ctx:
        sb, pb, sem = open_pools(nc, ctx)
        wq, wk, wv = (sb(n, [C, HEADS, C]) for n in ("win_wq", "win_wk", "win_wv"))
        wu = sb("win_wu", [C, HEADS * C])
        wut = sb("win_wut", [C, HEADS, C])
        mask = sb("win_mask", [P, KEYS])
        phi = sb("phi_in", [P, T // P, FILTERS])
        phi_n = sb("phi_n", [FILTERS, T])
        phi_t = sb("phi_t", [FILTERS, PIECES16, PHI_ROW], F16)
        sigma = sb("sigma", [FILTERS, 2])
        size = sb("phi_size", [FILTERS, 4])
        ones, diag = sb("phi_ones", [FILTERS, P]), sb("phi_diag", [FILTERS, FILTERS])
        logits, soft, hard, free = (sb("pick_" + n, [P, SCALES]) for n in ("logits", "soft", "hard", "free"))
        gumbel, weight, signed = sb("pick_gumbel", [P, SCALES]), sb("pick_weight", [P, SCALES]), sb("pick_signed", [P, SCALES])
        col = sb("pick_col", [P, 4])
        qk_ps, vo_ps, wut_ps = (pb(n, [P, HEADS, C]) for n in ("qk_ps", "vo_ps", "wut_ps"))
        phi_ps, gain_ps = pb("phi_t_ps", [FILTERS, T]), pb("gain_ps", [P, BANK])
        (win_in, t_ok, t_c, qk_ok, vo_ok, zeroed, mk, lin_in, phi_in, small_in, turned, sig_ok, high_ok, row_ok, exp_ok, step, pstep, diag_ok, gain_ok) = (sem("ws_" + n) for n in (
            "win_in", "wut", "wut_taken", "qk", "vo", "zeroed", "mask_step", "lin_in", "phi_in", "small_in", "phi_turned", "sigma", "high", "rows", "exp",
            "pick_step", "phi_step", "diag", "gain"))
        with nc.Block() as block:
            @block.sync
            def _(sp):
                sp.dma_start(phi[:, :, :], ins["L2_ffn_phi"][0:T, :].rearrange("(n p) k -> p n k", p=P)).then_inc(phi_in, 16)
                for dst, n in ((wq, "Wq"), (wk, "Wk"), (wv, "Wv")):
                    sp.dma_start(dst[:, :, :], ins["L2_attn_" + n].rearrange("(h e) c -> e h c", h=HEADS)).then_inc(win_in, 16)
                sp.dma_start(wu[:, :], ins["L2_attn_Wu"]).then_inc(win_in, 16)
                for p in range(2):
                    sp.dma_start(m.win_bias[HALF[p], 0:1], ins["L2_attn_bu"].rearrange("(c a) -> c a", a=1)).then_inc(win_in, 16)
                for p in range(2):
                    for dst, n in ((m.plus, "M_phi_plus"), (m.minus, "M_phi_minus")):
                        sp.dma_start(dst[HALF[p], :, :].rearrange("d i (k e) -> d (i k) e", e=C), ins["L2_ffn_" + n].rearrange("i k d e -> d (i k) e")).then_inc(m.mats_in, 16)
                sp.wait_ge(row_ok, 3)
                sp.dma_start(phi_rows, phi_t[:, :, :]).then_inc(m.rows_out, 16)
                sp.wait_ge(m.rows_out, 16)
                sp.wait_ge(win_in, 96)

            @block.scalar
            def _(act):
                act.dma_start(sigma[:, 0:1], ins["L2_ffn_sigma"].rearrange("(k a) -> k a", a=1)).then_inc(small_in, 16)
                act.dma_start(logits[:, :], ins["L2_ffn_log_weights"].rearrange("(a k) -> a k", a=1).to_broadcast([P, SCALES])).then_inc(small_in, 16)
                act.dma_start(gumbel[:, :], ins["L2_ffn_gumbel"].rearrange("(a k) -> a k", a=1).to_broadcast([P, SCALES])).then_inc(small_in, 16)
                for p in range(2):
                    act.dma_start(m.ar[HALF[p], :, :].rearrange("d i (k e) -> d (i k) e", e=C), ins["L2_ffn_M_u"].rearrange("i k d e -> d (i k) e")).then_inc(small_in, 16)
                act.wait_ge(small_in, 80)
                nc.scalar.activation(sigma[:, 1:2], sigma[:, 0:1], ACT.Sqrt).then_inc(sig_ok, 1)
                act.wait_ge(sig_ok, 1)
                nc.scalar.activation(sigma[:, 0:1], sigma[:, 1:2], ACT.Sqrt).then_inc(sig_ok, 1)
                act.wait_ge(step, 2)
                nc.scalar.activation(soft[:, :], logits[:, :], ACT.Exp, bias=col[:, 0:1], accum_out=col[:, 1:2]).then_inc(exp_ok, 1)
                act.wait_ge(zeroed, 3)
                for p in range(2):
                    cols = slice(p * C, (p + 1) * C)
                    act.dma_start(m.lin_q[HALF[p], cols], ins["L3_attn_Wq"]).then_inc(lin_in, 16)
                    act.dma_start(m.lin_kv[HALF[p], 0, cols], ins["L3_attn_Wk"]).then_inc(lin_in, 16)
                    act.dma_start(m.lin_kv[HALF[p], 1, cols], ins["L3_attn_Wv"]).then_inc(lin_in, 16)
                    act.dma_start(m.lin_o[HALF[p], cols], ins["L3_attn_Wo"]).then_inc(lin_in, 16)
                    act.dma_start(m.lin_bias[HALF[p], 0:1], ins["L3_attn_bq"].rearrange("(c a) -> c a", a=1)).then_inc(lin_in, 16)
                    act.dma_start(m.lin_bias[HALF[p], 1:2], ins["L3_attn_bo"].rearrange("(c a) -> c a", a=1)).then_inc(lin_in, 16)
                    act.dma_start(m.lin_rows[:, 0, cols], ins["L3_attn_bk"].rearrange("(a c) -> a c", a=1).to_broadcast([P, C])).then_inc(lin_in, 16)
                    act.dma_start(m.lin_rows[:, 1, cols], ins["L3_attn_bv"].rearrange("(a c) -> a c", a=1).to_broadcast([P, C])).then_inc(lin_in, 16)
                act.wait_ge(lin_in, 256)

            @block.gpsimd
            def _(pool):
                for t in (m.lin_q[:, :], m.lin_kv[:, :, :], m.lin_o[:, :], m.win_qk[:, :, :], m.win_vo[:, :, :]):
                    nc.gpsimd.memset(t, 0.0).then_inc(zeroed, 1)
                nc.gpsimd.memset(m.win_x[:, :, :, :], 0.0)
                blocks = m.lin_mask[:, :].rearrange("p (h d) -> p h d", d=HEAD_DIM)
                nc.gpsimd.memset(m.lin_mask[:, :], 1.0).then_inc(mk, 1)
                nc.gpsimd.memset(mask[:, :], 0.0).then_inc(mk, 1)
                pool.wait_ge(mk, 2)
                nc.gpsimd.affine_select(out=blocks, in_=blocks, compare_op=ALU.is_ge, fill=0.0, base=0,
                                        pattern=[[-HEAD_DIM, P // HEAD_DIM], [0, HEAD_DIM]], channel_multiplier=1).then_inc(mk, 1)
                pool.wait_ge(mk, 3)
                nc.gpsimd.affine_select(out=blocks, in_=blocks, compare_op=ALU.is_ge, fill=0.0, base=HEAD_DIM - 1,
                                        pattern=[[HEAD_DIM, P // HEAD_DIM], [0, HEAD_DIM]], channel_multiplier=-1).then_inc(mk, 1)
                pool.wait_ge(mk, 4)
                for q in range(P // WINDOW):
                    rows = mask[q * WINDOW:(q + 1) * WINDOW, :]
                    nc.gpsimd.affine_select(out=rows, in_=rows, compare_op=ALU.is_ge, fill=MASKED, base=-1,
                                            pattern=[[1, KEYS]], channel_multiplier=-1).then_inc(mk, 1)
                    pool.wait_ge(mk, 2 * q + 5)
                    nc.gpsimd.affine_select(out=rows, in_=rows, compare_op=ALU.is_ge, fill=MASKED, base=WINDOW,
                                            pattern=[[-1, KEYS]], channel_multiplier=1).then_inc(mk, 1)
                    pool.wait_ge(mk, 2 * q + 6)
                for n in range(BANK // KEYS):
                    nc.gpsimd.tensor_copy(m.win_mask[:, n * KEYS:(n + 1) * KEYS], mask[:, :])

            @block.tensor
            def _(pe):
                pe.wait_ge(phi_in, 16)
                for n in range(T // P):
                    mm = nc.tensor.transpose(phi_ps[:, n * P:(n + 1) * P], phi[:, n, :], m.ident[:, :])
                mm.then_inc(turned, 1)
                pe.wait_ge(win_in, 96)
                for h in range(HEADS):
                    mm = nc.tensor.transpose(wut_ps[0:C, h, :], wu[:, h * C:(h + 1) * C], m.ident[0:C, 0:C])
                mm.then_inc(t_ok, 1)
                for p in range(2):
                    for h in range(HEADS):
                        mm = nc.tensor.matmul(qk_ps[HALF[p], h, :], wq[:, h, :], wk[:, h, :], start=True, stop=True)
                mm.then_inc(qk_ok, 1)
                pe.wait_ge(t_c, 1)
                for p in range(2):
                    for h in range(HEADS):
                        mm = nc.tensor.matmul(vo_ps[HALF[p], h, :], wv[:, h, :], wut[:, h, :], start=True, stop=True)
                mm.then_inc(vo_ok, 1)
                pe.wait_ge(diag_ok, 2)
                nc.tensor.matmul(gain_ps[:, 0:FILTERS], ones[:, :], diag[:, :], start=True, stop=True).then_inc(gain_ok, 1)

            @block.vector
            def _(dve):
                nc.vector.memset(ones[:, :], 1.0).then_inc(diag_ok, 1)
                nc.vector.memset(phi_t[:, :, 0:SPAN], 0.0).then_inc(row_ok, 1)
                done, filters_done = [0], [0]

                def link(ins_):
                    done[0] += 1
                    ins_.then_inc(step, 1)
                    dve.wait_ge(step, done[0])

                def link_phi(ins_):
                    filters_done[0] += 1
                    ins_.then_inc(pstep, 1)
                    dve.wait_ge(pstep, filters_done[0])

                dve.wait_ge(small_in, 80)
                link(nc.vector.tensor_tensor(logits[:, :], logits[:, :], gumbel[:, :], ALU.add))
                link(nc.vector.tensor_reduce(col[:, 0:1], logits[:, :], axis=AX.X, op=ALU.max, negate=True))
                dve.wait_ge(turned, 1)
                link_phi(nc.vector.tensor_reduce(size[:, 0:1], phi_ps[:, :], axis=AX.X, op=ALU.max))
                link_phi(nc.vector.tensor_reduce(size[:, 1:2], phi_ps[:, :], axis=AX.X, op=ALU.min, negate=True))
                link_phi(nc.vector.tensor_tensor(size[:, 0:1], size[:, 0:1], size[:, 1:2], ALU.max))
                link_phi(nc.vector.tensor_scalar(size[:, 0:1], size[:, 0:1], TINY, None, ALU.max))
                link_phi(nc.vector.reciprocal(size[:, 2:3], size[:, 0:1]))
                link_phi(nc.vector.tensor_scalar(phi_n[:, :], phi_ps[:, :], size[:, 2:3], None, ALU.mult))
                nc.vector.tensor_copy(phi_t[:, 0, SPAN:], phi_n[:, :]).then_inc(row_ok, 1)
                dve.wait_ge(row_ok, 2)
                nc.vector.tensor_tensor(phi_t[:, 1, SPAN:], phi_n[:, :], phi_t[:, 0, SPAN:], ALU.subtract).then_inc(row_ok, 1)
                dve.wait_ge(sig_ok, 2)
                link_phi(nc.vector.tensor_tensor(size[:, 3:4], size[:, 0:1], sigma[:, 0:1], ALU.mult))
                nc.vector.tensor_scalar(diag[:, :], m.ident[0:FILTERS, 0:FILTERS], size[:, 3:4], None, ALU.mult).then_inc(diag_ok, 1)
                dve.wait_ge(t_ok, 1)
                nc.vector.tensor_copy(wut[:, :, :], wut_ps[0:C, :, :]).then_inc(t_c, 1)
                dve.wait_ge(zeroed, 5)
                dve.wait_ge(qk_ok, 1)
                for p in range(2):
                    nc.vector.tensor_scalar(m.win_qk[HALF[p], :, p * C:(p + 1) * C], qk_ps[HALF[p], :, :], C ** -0.5, None, ALU.mult)
                dve.wait_ge(vo_ok, 1)
                for p in range(2):
                    nc.vector.tensor_copy(m.win_vo[HALF[p], :, p * C:(p + 1) * C], vo_ps[HALF[p], :, :])
                dve.wait_ge(exp_ok, 1)
                link(nc.vector.reciprocal(col[:, 2:3], col[:, 1:2]))
                link(nc.vector.tensor_scalar(soft[:, :], soft[:, :], col[:, 2:3], None, ALU.mult))
                link(nc.vector.tensor_reduce(col[:, 3:4], soft[:, :], axis=AX.X, op=ALU.max))
                link(nc.vector.tensor_scalar(hard[:, :], soft[:, :], col[:, 3:4], None, ALU.is_equal))
                link(nc.vector.tensor_scalar(free[:, :], hard[:, :], -1.0, 1.0, ALU.mult, ALU.add))
                for i in range(1, SCALES):
                    for j in range(i):
                        link(nc.vector.tensor_tensor(hard[:, i:i + 1], hard[:, i:i + 1], free[:, j:j + 1], ALU.mult))
                link(nc.vector.tensor_tensor(weight[:, :], hard[:, :], soft[:, :], ALU.subtract))
                link(nc.vector.tensor_tensor(weight[:, :], weight[:, :], soft[:, :], ALU.add))
                link(nc.vector.tensor_copy(signed[HALF[0], :], weight[HALF[0], :]))
                link(nc.vector.tensor_scalar(signed[HALF[1], :], weight[HALF[1], :], -1.0, None, ALU.mult))
                dve.wait_ge(gain_ok, 1)
                for i in range(SCALES):
                    nc.vector.tensor_scalar(m.gain[:, 0, i, :], gain_ps[:, 0:FILTERS], weight[:, i:i + 1], None, ALU.mult)
                    nc.vector.tensor_scalar(m.gain[:, 1, i, :], gain_ps[:, 0:FILTERS], signed[:, i:i + 1], None, ALU.mult)
                    link(nc.vector.tensor_scalar(m.ar[:, i, :], m.ar[:, i, :], weight[:, i:i + 1], None, ALU.mult))
                    if i:
                        link(nc.vector.tensor_tensor(m.ar[:, i, :], m.ar[:, i, :], m.ar[:, i - 1, :], ALU.add))


def spectral_mixing(nc, m, block, step):
    @block.gpsimd
    def _(pool):
        done = 0
        pool.wait_ge(m.mats_in, 64)
        for sign, mats in ((0, m.plus), (1, m.minus)):
            for i in range(SCALES):
                by_filter = mats[:, i, :].rearrange("p (k e) -> p k e", e=C)
                nc.gpsimd.tensor_tensor(by_filter, by_filter, m.gain[:, sign, i, :].to_broadcast([P, FILTERS, C]), ALU.mult).then_inc(step, 1)
                done += 1
                pool.wait_ge(step, done)
                if i:
                    nc.gpsimd.tensor_tensor(mats[:, i, :], mats[:, i, :], mats[:, i - 1, :], ALU.add).then_inc(step, 1)
                    done += 1
                    pool.wait_ge(step, done)
        for i in range(SCALES):
            for par, op in ((0, ALU.add), (1, ALU.subtract)):
                nc.gpsimd.tensor_tensor(m.mix[:, :, i, par, :], m.plus[:, i, :].rearrange("p (k e) -> p k e", e=C),
                                        m.minus[:, i, :].rearrange("p (k e) -> p k e", e=C), op)


def hankel_load(nc, m, phi_rows, sp):
    for piece in range(PIECES16):
        for k in range(FILTERS):
            src = bass.AP(phi_rows.tensor, (k * PIECES16 + piece) * PHI_ROW + SPAN - 2 * (P - 1), [[2, P], [1, T]])
            sp.dma_start(m.hankel[:, piece, k, :], src).then_inc(m.table_in, 16)


def hybrid_program(nc, ins, out):
    with ExitStack() as whole:
        sb, pb, sem = open_pools(nc, whole)
        m = Memory()
        m.x = sb("x", [P, G, T])
        m.x_flat = m.x[:, :, :].rearrange("p g t -> p (g t)")
        m.ident, m.ident_bf = sb("ident", [P, P]), sb("ident_bf", [P, P], BF16)
        m.average, m.centre, m.eps = sb("average", [P, P]), sb("centre", [P, P]), sb("eps", [P, 1])
        m.win_qk, m.win_vo = sb("win_qk", [P, HEADS, P]), sb("win_vo", [P, HEADS, P])
        m.win_x, m.win_mask, m.win_bias = sb("win_x", [P, NW, 2, KEYS]), sb("win_maskb", [P, BANK], BF16), sb("win_bias", [P, 1])
        m.mix, m.ar, m.gain = sb("mix", [P, FILTERS, SCALES, 2, C]), sb("ar", [P, SCALES, AR * C]), sb("gain", [P, 2, SCALES, FILTERS])
        m.lin_q, m.lin_o, m.lin_kv = sb("lin_q", [P, P]), sb("lin_o", [P, P]), sb("lin_kv", [P, 2, P])
        m.lin_bias, m.lin_rows, m.lin_mask = sb("lin_bias", [P, 2]), sb("lin_rows", [P, 2, P]), sb("lin_mask", [P, P])
        m.mats_in, m.rows_out, m.table_in, m.ex_in = sem("mats_in"), sem("phi_rows_out"), sem("table_in"), sem("ex_in")
        phi_rows = nc.dram_tensor("phi_rows", (FILTERS, PIECES16, PHI_ROW), F16).ap()

        with nc.cleanup_on_exit(), ExitStack() as ctx:
            sb, pb, sem = open_pools(nc, ctx)
            m.rows, m.cols = sb("rows", [P, H, B, ROWP]), sb("cols", [P, W, B, ROWP])
            m.toeplitz, m.conv_bias = sb("toeplitz", [P, 4, SHIFTS, P]), sb("conv_bias", [P, 4])
            m.w_theta, m.w_phi, m.w_g = sb("w_theta", [C // 2, C]), sb("w_phi", [C // 2, C]), sb("w_g", [C // 2, C])
            m.w_last = sb("w_last", [C, C // 2])
            m.plus, m.minus = (sb("m_" + n, [P, SCALES, FILTERS * C]) for n in ("plus", "minus"))
            mixing_step = sem("mixing_step")
            setup_stage(nc, m, ins)
            weights_stage(nc, m, ins, phi_rows)
            nonlocal_stage(nc, m)
            conv_passes(nc, m, m.rows, 0, "v", lambda block: spectral_mixing(nc, m, block, mixing_step))
            rows_to_cols_stage(nc, m)
            conv_passes(nc, m, m.cols, 2, "h")
            cols_to_tokens_stage(nc, m)

        with ExitStack() as late:
            sb, pb, sem = open_pools(nc, late)
            m.normed = sb("normed", [P, G * T // 128, 128])
            with nc.cleanup_on_exit(), ExitStack() as filters:
                sb, pb, sem = open_pools(nc, filters)
                m.hankel = sb("hankel", [P, PIECES16, FILTERS, T], F16)

                with ExitStack() as ctx:
                    sb, pb, sem = open_pools(nc, ctx)
                    m.pieces = sb("pieces", [P, CHUNKS, PIECE])
                    window_norm_stage(nc, m, lambda nc, m, sp: hankel_load(nc, m, phi_rows, sp))
                    window_attention_stage(nc, m)

                spectral_norm_stage(nc, m)
                spectral_stage(nc, m)

            with nc.cleanup_on_exit(), ExitStack() as ctx:
                sb, pb, sem = open_pools(nc, ctx)
                m.ex_w1, m.ex_w2 = sb("ex_w1", [C + 1, EXPERTS, HIDDEN]), sb("ex_w2", [P, EXPERTS, HT, C])
                with nc.Block() as block:
                    @block.sync
                    def _(sp):
                        expert_load(nc, m, ins, sp)
                norm_stage(nc, m, "l")
                linear_attention_stage(nc, m)
                norm_stage(nc, m, "e")
                expert_stage(nc, m, ins, out)


def kernel(**inputs):
    import concourse.bacc as bacc
    from concourse.bass_utils import run_bass_kernel_spmd

    nc = bacc.Bacc("TRN2", target_bir_lowering=False, num_devices=1)
    arrays, ins = {}, {}
    for name in inputs:
        a = np.ascontiguousarray(inputs[name])
        arrays["in_" + name] = a
        ins[name] = nc.dram_tensor("in_" + name, a.shape, mybir.dt.from_np(a.dtype), kind="ExternalInput").ap()
    out = nc.dram_tensor("out_0", (B, C, H, W), F32, kind="ExternalOutput").ap()
    hybrid_program(nc, ins, out)
    r = run_bass_kernel_spmd(nc, [arrays], core_ids=[0])
    return r.results[0]["out_0"]
```

```python
import numpy as np
from contextlib import ExitStack

import concourse.bass as bass
from concourse import mybir
from concourse.alu_op_type import AluOpType as ALU

F32 = mybir.dt.float32
BF16 = mybir.dt.bfloat16
F16 = mybir.dt.float16
ACT = mybir.ActivationFunctionType
AX = mybir.AxisListType
ds = bass.ds

B, C, H, W = 8, 64, 32, 32
T = H * W
P = 2 * C
G = B // 2
HALF = (slice(0, C), slice(C, P))
BANK = 512

TAPS = 9
PAIRS = W // 2
PADP = 2
ROWP = PAIRS + 2 * PADP
SHIFTS = 2 * PADP + 1


class Memory:
    pass


def open_pools(nc, ctx):
    def sb(name, shape, dt=F32):
        return ctx.enter_context(nc.sbuf_tensor(name, shape, dt))

    def pb(name, shape, dt=F32):
        return ctx.enter_context(nc.psum_tensor(name, shape, dt))

    def sem(name):
        return nc.alloc_semaphore(name=name)

    return sb, pb, sem


def setup_stage(nc, m, ins):
    with ExitStack() as ctx:
        sb, pb, sem = open_pools(nc, ctx)
        x_in, w_in, ident_ok, zeroed, const_ok = sem("x_in"), sem("w_in"), sem("ident_ok"), sem("pads_zeroed"), sem("const_ok")
        with nc.Block() as block:
            def load_x(eng, p):
                eng.dma_start(m.x[HALF[p], :, :], ins["x"][p::2].rearrange("g c h w -> c g (h w)")).then_inc(x_in, 16)

            @block.sync
            def _(sp):
                load_x(sp, 0)
                sp.dma_start(m.w_g[:, :], ins["L0_conv_w_g"]).then_inc(w_in, 16)
                sp.dma_start(m.w_last[:, :], ins["L0_conv_w_last"]).then_inc(w_in, 16)
                sp.wait_ge(x_in, 32)

            @block.scalar
            def _(act):
                load_x(act, 1)
                act.dma_start(m.w_theta[:, :], ins["L0_conv_w_theta"]).then_inc(w_in, 16)
                act.dma_start(m.w_phi[:, :], ins["L0_conv_w_phi"]).then_inc(w_in, 16)
                act.wait_ge(w_in, 64)

            @block.gpsimd
            def _(pool):
                nc.gpsimd.memset(m.ident[:, :], 0.0).then_inc(zeroed, 1)
                nc.gpsimd.memset(m.average[:, :], 0.0).then_inc(zeroed, 1)
                pool.wait_ge(zeroed, 2)
                nc.gpsimd.affine_select(out=m.ident[:, :], in_=m.ident[:, :], compare_op=ALU.not_equal, fill=1.0,
                                        base=0, pattern=[[-1, P]], channel_multiplier=1).then_inc(ident_ok, 1)
                nc.gpsimd.memset(m.rows[:, :, :, :], 0.0).then_inc(zeroed, 1)
                for t in (m.lin_q[:, :], m.lin_kv[:, :, :], m.lin_o[:, :]):
                    nc.gpsimd.memset(t, 0.0).then_inc(zeroed, 1)
                pool.wait_ge(zeroed, 6)
                for p in range(2):
                    nc.gpsimd.memset(m.average[HALF[p], p * C:(p + 1) * C], 1.0 / C).then_inc(const_ok, 1)

            @block.vector
            def _(dve):
                nc.vector.memset(m.eps[:, :], 1e-5)
                nc.vector.memset(m.win_qk[:, :, :], 0.0)
                nc.vector.memset(m.win_vo[:, :, :], 0.0)
                dve.wait_ge(ident_ok, 1)
                dve.wait_ge(const_ok, 2)
                nc.vector.tensor_tensor(m.centre[:, :], m.ident[:, :], m.average[:, :], ALU.subtract)
                nc.vector.tensor_copy(m.ident_bf[:, :], m.ident[:, :])


def nonlocal_stage(nc, m, extra):
    NB = 2 * (T // P)
    NR = NB // 2
    KT = T // P
    HK = KT // 2
    with ExitStack() as ctx:
        sb, pb, sem = open_pools(nc, ctx)
        last_t = sb("w_last_t", [C // 2, C])
        qk_w = sb("qk_w", [P, P])
        zo_w = sb("zo_w", [P, P])
        later = m.mix[:, :, :, :, :].rearrange("p k s a e -> p (k s a e)")
        queries = later[:, 0:G * T].rearrange("p (g t) -> p g t", g=G)
        values = later[:, G * T:2 * G * T].rearrange("p (n c) -> p n c", c=P)
        xg = sb("xg", [P, T])
        qg = sb("qg", [P, T])
        vg = sb("vg", [P, KT, P])
        probs = [sb(f"probs{i}", [P, T]) for i in range(2)]
        probs_t = [sb(f"probs_t{i}", [P, KT, P]) for i in range(4)]
        wide = [sb(f"nl_wide{i}", [P, 2, C]) for i in range(2)]
        scaled = sb("nl_scaled", [P, P])
        nmax, rsum, rinv = sb("nmax", [P, 4]), sb("rsum", [P, 4]), sb("rinv", [P, 4])
        scores = [pb(f"scores{i}", [P, T]) for i in range(2)]
        turned = pb("turned", [P, KT, P])
        out_ps = pb("out_ps", [P, BANK])[:, 0:P]
        scale_ps = pb("scale_ps", [P, BANK])[:, 0:P]
        wl_t, wl_c, fused, fused_c, placed = sem("wl_t"), sem("wl_c"), sem("fused"), sem("fused_c"), sem("x_placed")
        q_ok, z_ok, q_c, z_c, xg_ok, qg_ok, vg_ok = (sem("nl_" + n) for n in ("queries", "values", "queries_taken", "values_taken", "xg", "qg", "vg"))
        s_score, s_max, s_exp, s_tr, s_ta, s_td, s_pv, s_inv, s_wide, s_scale, s_mul, s_add = (sem("nl_" + n) for n in (
            "scores", "max", "probs", "turned", "turned_act", "turned_dve", "out", "inv", "wide", "scale_taken", "scaled", "added"))

        def blocks(eng, body):
            with eng.Fori(0, G - 1) as g:
                body(g, True)
            body(G - 1, False)

        with nc.Block() as block:
            @block.gpsimd
            def _(pool):
                nc.gpsimd.memset(qk_w[:, :], 0.0).then_inc(fused_c, 1)
                nc.gpsimd.memset(zo_w[:, :], 0.0).then_inc(fused_c, 1)
                pool.wait_ge(fused_c, 2)
                for par in range(2):
                    for p in range(2):
                        nc.gpsimd.tensor_copy(
                            m.rows[HALF[par], :, p::2, PADP:PADP + PAIRS].rearrange("c h g q -> c g h q"),
                            m.x[HALF[p], :, :].rearrange("c g (h q a) -> c g h q a", h=H, a=2)[:, :, :, :, par]).then_inc(placed, 1)
                        pool.wait_ge(placed, 2 * par + p + 1)
                nc.gpsimd.memset(m.cols[:, :, :, :], 0.0)

            @block.tensor
            def _(pe):
                pe.sem_inc(s_tr, 4)
                pe.sem_inc(s_pv, 2)
                nc.tensor.transpose(turned[0:C // 2, 0, 0:C], m.w_last[:, :], m.ident[0:C, 0:C]).then_inc(wl_t, 1)
                for p in range(2):
                    nc.tensor.matmul(scores[0][HALF[p], 0:C], m.w_theta[:, :], m.w_phi[:, :], start=True, stop=True).then_inc(fused, 1)
                pe.wait_ge(wl_c, 1)
                for p in range(2):
                    nc.tensor.matmul(scores[1][HALF[p], 0:C], m.w_g[:, :], last_t[:, :], start=True, stop=True).then_inc(fused, 1)
                pe.wait_ge(fused_c, 6)
                for g in range(G):
                    if g:
                        pe.wait_ge(q_c, g)
                    for c in range(T // BANK):
                        mm = nc.tensor.matmul(scores[0][:, c * BANK:(c + 1) * BANK], qk_w[:, :], m.x[:, g, c * BANK:(c + 1) * BANK], start=True, stop=True)
                    mm.then_inc(q_ok, 1)
                    if g:
                        pe.wait_ge(z_c, g)
                    for k in range(KT):
                        mm = nc.tensor.matmul(scores[1][:, k * P:(k + 1) * P], m.x[:, g, k * P:(k + 1) * P], zo_w[:, :], start=True, stop=True)
                    mm.then_inc(z_ok, 1)
                pe.wait_ge(q_c, G)
                pe.wait_ge(z_c, G)

                def score(g, i):
                    pe.wait_ge(s_exp, g * NB + (i + 1))
                    p, j, par = i // 8, (i // 2) % 4, i % 2
                    q = qg[HALF[p], 256 * j + par:256 * (j + 1):2]
                    for c in range(T // BANK):
                        mm = nc.tensor.matmul(scores[i % 2][:, c * BANK:(c + 1) * BANK], q, xg[HALF[p], c * BANK:(c + 1) * BANK], start=True, stop=True)
                    mm.then_inc(s_score, 1)

                def turn(g, i):
                    pe.wait_ge(s_exp, g * NB + (i + 3))
                    pe.wait_ge(s_ta, g * NB + (i + 1))
                    pe.wait_ge(s_td, g * NB + (i + 1))
                    for k in range(KT):
                        mm = nc.tensor.transpose(turned[:, k, :], probs[i % 2][:, k * P:(k + 1) * P], m.ident[:, :])
                        if k == HK - 1 or k == KT - 1:
                            mm.then_inc(s_tr, 1)

                def attend(g, n):
                    p = n // 4
                    pe.wait_ge(s_ta, g * NB + (2 * n + 3))
                    pe.wait_ge(s_td, g * NB + (2 * n + 3))
                    pe.wait_ge(vg_ok, g + 1)
                    pe.wait_ge(s_mul, g * NR + (n + 1))
                    for k in range(KT):
                        for par in range(2):
                            nc.tensor.matmul(out_ps[HALF[par], :], vg[:, k, p * C:(p + 1) * C], probs_t[(2 * n + par) % 4][:, k, :], start=(k == 0), stop=(k == KT - 1),
                                             skip_group_check=True)
                    pe.wait_ge(s_wide, g * NR + (n + 1))
                    for par in range(2):
                        mm = nc.tensor.matmul(scale_ps[HALF[par], :], wide[n % 2][:, par, :], m.ident[:, :], start=True, stop=True)
                    mm.then_inc(s_pv, 1)

                def body(g, more):
                    for i in range(NB):
                        turn(g, i)
                        if i + 2 < NB:
                            score(g, i + 2)
                        elif more:
                            if i + 2 == NB:
                                pe.wait_ge(xg_ok, g + 2)
                                pe.wait_ge(qg_ok, g + 2)
                            score(g + 1, i + 2 - NB)
                        if i % 2:
                            attend(g, i // 2)

                pe.wait_ge(xg_ok, 1)
                pe.wait_ge(qg_ok, 1)
                score(0, 0)
                score(0, 1)
                blocks(pe, body)

            @block.scalar
            def _(act):
                act.wait_ge(fused, 2)
                act.wait_ge(fused_c, 2)
                for p in range(2):
                    nc.scalar.activation(qk_w[HALF[p], p * C:(p + 1) * C], scores[0][HALF[p], 0:C], ACT.Copy).then_inc(fused_c, 1)
                nc.scalar.copy(xg[:, :], m.x[:, 0, :]).then_inc(xg_ok, 1)
                for g in range(G):
                    act.wait_ge(q_ok, g + 1)
                    nc.scalar.activation(queries[:, g, :], scores[0][:, :], ACT.Copy).then_inc(q_c, 1)
                act.sem_inc(s_exp, 2)
                act.sem_inc(s_ta, 1)

                def exp(g, i):
                    act.wait_ge(s_max, g * NB + (i + 1))
                    act.wait_ge(s_tr, 2 * (g * NB) + (2 * i + 2))
                    nc.scalar.activation(probs[i % 2][:, :], scores[i % 2][:, :], ACT.Exp, bias=nmax[:, i % 4:i % 4 + 1],
                                         accum_out=rsum[:, i % 4:i % 4 + 1]).then_inc(s_exp, 1)

                def take(g, i):
                    act.wait_ge(s_tr, 2 * (g * NB) + (2 * i + 6))
                    act.wait_ge(s_pv, g * NR + (i // 2 + 1))
                    nc.scalar.activation(probs_t[i % 4][:, HK:KT, :], turned[:, HK:KT, :], ACT.Copy).then_inc(s_ta, 1)

                def body(g, more):
                    for i in range(NB):
                        take(g, i)
                        if i == 0:
                            act.wait_ge(s_pv, g * NR + 2)
                            nc.scalar.copy(vg[:, :, :], values[:, ds(g * KT, KT), :]).then_inc(vg_ok, 1)
                        for ahead in (i + 1, i + 2) if i % 2 else ():
                            if ahead == NB - 1 and more:
                                act.wait_ge(s_score, g * NB + NB)
                                nc.scalar.copy(xg[:, :], m.x_flat[:, ds(g * T + T, T)]).then_inc(xg_ok, 1)
                            if ahead < NB:
                                exp(g, ahead)
                            elif more:
                                exp(g + 1, ahead - NB)

                exp(0, 0)
                exp(0, 1)
                blocks(act, body)

            @block.vector
            def _(dve):
                dve.wait_ge(wl_t, 1)
                nc.vector.tensor_copy(last_t[:, :], turned[0:C // 2, 0, 0:C]).then_inc(wl_c, 1)
                dve.wait_ge(fused, 4)
                dve.wait_ge(fused_c, 2)
                for p in range(2):
                    nc.vector.tensor_copy(zo_w[HALF[p], p * C:(p + 1) * C], scores[1][HALF[p], 0:C]).then_inc(fused_c, 1)
                for g in range(G):
                    dve.wait_ge(z_ok, g + 1)
                    nc.vector.tensor_copy(values[:, g * KT:(g + 1) * KT, :].rearrange("p k c -> p (k c)"), scores[1][:, :]).then_inc(z_c, 1)
                    if g == 0:
                        dve.wait_ge(q_c, 1)
                        nc.vector.tensor_copy(qg[:, :], queries[:, 0, :]).then_inc(qg_ok, 1)
                dve.sem_inc(s_td, 1)
                dve.sem_inc(s_mul, 1)

                def row_max(g, i):
                    dve.wait_ge(s_score, g * NB + (i + 1))
                    nc.vector.tensor_reduce(nmax[:, i % 4:i % 4 + 1], scores[i % 2][:, :], axis=AX.X, op=ALU.max, negate=True).then_inc(s_max, 1)

                def take(g, i):
                    dve.wait_ge(s_tr, 2 * (g * NB) + (2 * i + 5))
                    dve.wait_ge(s_pv, g * NR + (i // 2 + 1))
                    nc.vector.tensor_copy(probs_t[i % 4][:, 0:HK, :], turned[:, 0:HK, :]).then_inc(s_td, 1)

                def spread(g, n):
                    two = slice(2 * n % 4, 2 * n % 4 + 2)
                    dve.wait_ge(s_exp, g * NB + (2 * n + 4))
                    nc.vector.reciprocal(rinv[:, two], rsum[:, two]).then_inc(s_inv, 1)
                    dve.wait_ge(s_inv, g * NR + (n + 1))
                    dve.wait_ge(s_pv, g * NR + (n + 1))
                    nc.vector.tensor_copy(wide[n % 2][:, :, :], rinv[:, two].to_broadcast([P, 2, C])).then_inc(s_wide, 1)

                def add(g, n):
                    p, j = n // 4, n % 4
                    dve.wait_ge(s_pv, g * NR + (n + 3))
                    dve.wait_ge(s_add, g * NR + (n + 1))
                    nc.vector.tensor_copy(scaled[:, :], scale_ps).then_inc(s_scale, 1)
                    dve.wait_ge(s_scale, g * NR + (n + 1))
                    nc.vector.tensor_tensor(scaled[:, :], out_ps, scaled[:, :], ALU.mult).then_inc(s_mul, 1)
                    dve.wait_ge(s_mul, g * NR + (n + 2))
                    dst = m.rows[:, 8 * j:8 * j + 8, ds(2 * g + p, 1), PADP:PADP + PAIRS]
                    nc.vector.tensor_tensor(dst, scaled[:, :].rearrange("p (h a q) -> p h a q", h=8, a=1), dst, ALU.add).then_inc(s_add, 1)

                def body(g, more):
                    for i in range(NB):
                        take(g, i)
                        if i % 2:
                            spread(g, i // 2)
                        if i + 2 < NB:
                            row_max(g, i + 2)
                            if more and i + 3 == NB:
                                nc.vector.tensor_copy(qg[:, :], later[:, ds(g * T + T, T)]).then_inc(qg_ok, 1)
                        elif more:
                            row_max(g + 1, i + 2 - NB)
                        if i % 2 == 0 and i:
                            add(g, i // 2 - 1)
                    add(g, NR - 1)

                row_max(0, 0)
                row_max(0, 1)
                dve.wait_ge(placed, 4)
                dve.sem_inc(s_add, 1)
                blocks(dve, body)

            extra(block)


def conv_passes(nc, m, grid, first, tag, extra=None):
    LINES = H
    FWD, BWD = LINES - 1, LINES - 2
    with ExitStack() as ctx:
        sb, pb, sem = open_pools(nc, ctx)
        conv = [pb(f"conv{tag}{k}", [P, BANK])[:, 0:B * PAIRS].rearrange("p (b q) -> p b q", q=PAIRS) for k in range(2)]
        running = [sb(f"running{tag}{k}", [P, B, ROWP]) for k in range(2)]
        added = [sb(f"added{tag}{k}", [P, B, PAIRS]) for k in range(2)]
        fetch_ok, line_ok, conv_ok, saved, padded = (sem(n + tag) for n in ("line_fetched", "line_ready", "conv_ready", "line_saved", "running_padded"))

        def steps(eng, step):
            step(1, 1, first)
            with eng.Fori(1, (FWD + 1) // 2) as k:
                for odd in range(2):
                    step(k * 2 + odd, odd, first)
            with eng.Fori((FWD + 1) // 2, (FWD + BWD + 1) // 2) as k:
                for odd in range(2):
                    step(k * 2 + odd, odd, first + 1)

        def at(line):
            return grid[:, ds(line, 1), :, PADP:PADP + PAIRS].rearrange("p l b q -> p (l b) q")

        with nc.Block() as block:
            @block.tensor
            def _(pe):
                def step(n, odd, wn):
                    pe.wait_ge(fetch_ok, n)
                    if not isinstance(n, int):
                        pe.wait_ge(line_ok, n - 1)
                    nc.tensor.matmul(conv[odd][:, :, :], m.ident[:, :], added[odd][:, :, :], start=True, stop=False)
                    pe.wait_ge(line_ok, n)
                    for s in range(SHIFTS):
                        mm = nc.tensor.matmul(conv[odd][:, :, :], m.toeplitz[:, wn, s, :], running[1 - odd][:, :, s:s + PAIRS],
                                              start=False, stop=(s == SHIFTS - 1))
                    mm.then_inc(conv_ok, 1)
                steps(pe, step)

            @block.vector
            def _(dve):
                for k in range(2):
                    nc.vector.memset(running[k][:, :, :], 0.0).then_inc(padded, 1)
                dve.wait_ge(padded, 2)
                nc.vector.tensor_copy(running[0][:, :, :], grid[:, 0, :, :]).then_inc(line_ok, 1)

                def step(n, odd, wn):
                    if not isinstance(n, int):
                        dve.wait_ge(saved, n - 1)
                    dve.wait_ge(conv_ok, n)
                    nc.vector.scalar_tensor_tensor(out=running[odd][:, :, PADP:PADP + PAIRS], in0=conv[odd][:, :, :], scalar=m.conv_bias[:, wn:wn + 1],
                                                   in1=added[odd][:, :, :], op0=ALU.add, op1=ALU.max).then_inc(line_ok, 1)
                steps(dve, step)

            @block.scalar
            def _(act):
                act.sem_inc(saved, 1)

                def fetch(line, odd):
                    nc.scalar.copy(added[odd][:, :, :], at(line)).then_inc(fetch_ok, 1)

                def step(n, odd, line, ahead=None):
                    act.wait_ge(line_ok, n + 1)
                    nc.scalar.copy(at(line), running[odd][:, :, PADP:PADP + PAIRS]).then_inc(saved, 1)
                    if isinstance(ahead, int) and ahead >= 2 * TOP - 3:
                        act.wait_ge(saved, n + 1)
                    if ahead is not None:
                        fetch(ahead, odd)

                TOP, END = (FWD + 1) // 2, (FWD + BWD + 1) // 2
                fetch(1, 1)
                fetch(2, 0)
                step(1, 1, 1, 3)
                with act.Fori(1, TOP - 1) as k:
                    for odd in range(2):
                        step(k * 2 + odd, odd, k * 2 + odd, k * 2 + (odd + 2))
                for n in (2 * TOP - 2, 2 * TOP - 1):
                    step(n, n % 2, n, 2 * FWD - n - 2)
                with act.Fori(TOP, END - 1) as k:
                    for odd in range(2):
                        step(k * 2 + odd, odd, k * (-2) + (2 * FWD - odd), k * (-2) + (2 * FWD - 2 - odd))
                for n in (2 * END - 2, 2 * END - 1):
                    step(n, n % 2, 2 * FWD - n)

            if extra is not None:
                extra(block)


def rows_to_cols_stage(nc, m):
    def move(copy, hp, wp):
        src = m.rows[HALF[wp], hp::2, :, PADP:PADP + PAIRS].rearrange("c r b q -> c b q r")
        dst = m.cols[HALF[hp], wp::2, :, PADP:PADP + PAIRS].rearrange("c q b r -> c b q r")
        copy(dst, src)

    with nc.Block() as block:
        @block.vector
        def _(dve):
            move(nc.vector.tensor_copy, 0, 1)
            move(nc.vector.tensor_copy, 1, 0)

        @block.scalar
        def _(act):
            move(nc.scalar.copy, 0, 0)

        @block.gpsimd
        def _(pool):
            move(nc.gpsimd.tensor_copy, 1, 1)


def cols_to_tokens_stage(nc, m):
    def move(copy, hp, p):
        src = m.cols[HALF[hp], :, p::2, PADP:PADP + PAIRS].rearrange("c w g r -> c g r w")
        dst = m.x[HALF[p], :, :].rearrange("c g (r a w) -> c g r a w", a=2, w=W)[:, :, :, hp, :]
        copy(dst, src)

    with nc.Block() as block:
        @block.vector
        def _(dve):
            move(nc.vector.tensor_copy, 0, 1)
            move(nc.vector.tensor_copy, 1, 0)

        @block.scalar
        def _(act):
            move(nc.scalar.copy, 0, 0)

        @block.gpsimd
        def _(pool):
            move(nc.gpsimd.tensor_copy, 1, 1)


def layernorm_stage(nc, m, out_piece, tag, extra=None):
    N = G * T // BANK
    TP = BANK // P
    AHEAD = 3
    with ExitStack() as ctx:
        sb, pb, sem = open_pools(nc, ctx)
        square = [sb(f"square{tag}{k}", [P, 2 * TP, C]) for k in range(2)]
        var, dev, inv = (sb(f"{n}{tag}", [P, N, 2 * TP]) for n in ("var", "dev", "inv"))
        scaled = [sb(f"scaled{tag}{k}", [P, 2 * TP, C]) for k in range(2)]
        centred = [pb(f"centred{tag}{k}", [P, 2 * TP, C]) for k in range(AHEAD + 1)]
        back = [pb(f"back{tag}{k}", [P, BANK]) for k in range(2)]
        cen_ok, sq_ok, var_ok, dev_ok, inv_ok, scaled_ok, back_ok, out_ok = (sem(n + tag) for n in (
            "centred_ready", "square_ready", "var_ready", "dev_ready", "inv_ready", "scaled_ready", "turned_back", "normed_ready"))
        with nc.Block() as block:
            @block.tensor
            def _(pe):
                def centre(u):
                    if u > AHEAD:
                        pe.wait_ge(scaled_ok, u - AHEAD)
                    for j in range(TP):
                        mm = nc.tensor.matmul(centred[u % (AHEAD + 1)][:, 2 * j:2 * j + 2, :].rearrange("p a c -> p (a c)"),
                                              m.x_flat[:, u * BANK + j * P:u * BANK + (j + 1) * P], m.centre[:, :], start=True, stop=True)
                    mm.then_inc(cen_ok, 1)

                for u in range(AHEAD):
                    centre(u)
                for u in range(N):
                    if u + AHEAD < N:
                        centre(u + AHEAD)
                    pe.wait_ge(scaled_ok, u + 1)
                    if u >= 2:
                        pe.wait_ge(out_ok, u - 1)
                    for j in range(TP):
                        mm = nc.tensor.transpose(back[u % 2][:, j * P:(j + 1) * P], scaled[u % 2][:, 2 * j:2 * j + 2, :].rearrange("p a c -> p (a c)"), m.ident[:, :])
                    mm.then_inc(back_ok, 1)

            @block.scalar
            def _(act):
                for u in range(N + AHEAD):
                    if u < N:
                        act.wait_ge(cen_ok, u + 1)
                        if u >= 2:
                            act.wait_ge(var_ok, u - 1)
                        nc.scalar.activation(square[u % 2][:, :, :], centred[u % (AHEAD + 1)][:, :, :], ACT.Square).then_inc(sq_ok, 1)
                    if 1 <= u <= N:
                        act.wait_ge(var_ok, u)
                        nc.scalar.activation(dev[:, u - 1, :], var[:, u - 1, :], ACT.Sqrt, bias=m.eps[:, 0:1], scale=1.0 / C).then_inc(dev_ok, 1)
                    if u >= AHEAD:
                        act.wait_ge(back_ok, u - AHEAD + 1)
                        nc.scalar.copy(out_piece(u - AHEAD), back[(u - AHEAD) % 2][:, :].rearrange("p (c n) -> p c n", n=P)).then_inc(out_ok, 1)

            @block.vector
            def _(dve):
                for u in range(N + 1):
                    if u < N:
                        dve.wait_ge(sq_ok, u + 1)
                        nc.vector.tensor_reduce(var[:, u, :], square[u % 2][:, :, :], axis=AX.X, op=ALU.add).then_inc(var_ok, 1)
                    if u:
                        dve.wait_ge(dev_ok, u)
                        nc.vector.reciprocal(inv[:, u - 1, :], dev[:, u - 1, :]).then_inc(inv_ok, 1)
                        dve.wait_ge(inv_ok, u)
                        if u > 2:
                            dve.wait_ge(back_ok, u - 2)
                        nc.vector.tensor_tensor(scaled[(u - 1) % 2][:, :, :], centred[(u - 1) % (AHEAD + 1)][:, :, :],
                                                inv[:, u - 1, :].to_broadcast([P, 2 * TP, C]), ALU.mult).then_inc(scaled_ok, 1)

            if extra is not None:
                extra(block, out_ok, N)


HEADS = 8
WINDOW = 32
CHUNK = 128
NW = CHUNK // WINDOW
KEYS = 2 * WINDOW
PIECE = WINDOW + CHUNK
CHUNKS = G * T // CHUNK
MASKED = -1e30


def window_norm_stage(nc, m, hankel_load=None):
    def piece(u):
        return m.pieces[:, u * NW:(u + 1) * NW, WINDOW:PIECE]

    def history(block, out_ok, n):
        @block.gpsimd
        def _(pool):
            nc.gpsimd.memset(m.pieces[:, ::T // CHUNK, 0:WINDOW], 0.0)
            pool.wait_ge(out_ok, n)
            per = T // CHUNK
            for g in range(G):
                nc.gpsimd.tensor_copy(m.pieces[:, g * per + 1:(g + 1) * per, 0:WINDOW], m.pieces[:, g * per:(g + 1) * per - 1, CHUNK:PIECE])

        if hankel_load is not None:
            @block.sync
            def _(sp):
                hankel_load(nc, m, sp)

    layernorm_stage(nc, m, piece, "w", history)


def window_attention_stage(nc, m):
    HG = HEADS // 4
    NT = HG * NW * 2
    with ExitStack() as ctx:
        sb, pb, sem = open_pools(nc, ctx)
        queries = sb("queries", [P, NW, HEADS, WINDOW])
        xt = [sb(f"win_xt{k}", [P, NW, P]) for k in range(2)]
        shifted = sb("shifted", [P, HG, NW, P])
        probs = sb("win_probs", [P, HG, NW, P])
        probs_t = sb("win_probs_t", [P, HG, NW, P])
        heads_t = sb("win_heads_t", [P, HG, NW, P])
        rmax, rsum, rinv = (sb(n, [P, NT]) for n in ("win_max", "win_sum", "win_inv"))
        q_ps = pb("q_ps", [P, HEADS, CHUNK])
        s_ps = pb("s_ps", [P, HG, NW, P])
        t_ps = pb("t_ps", [P, HG, NW, P])
        z_ps = pb("z_ps", [P, HG, NW, P])
        xt_ps, o_ps = q_ps[:, 0:NW, :], z_ps[:, 0, 0, :]
        (win_ok, q_ok, q_act, q_dve, s_ok, xt_ok, xt_c, sub_ok, p_ok, pt_ok, pt_act, pt_dve, z_ok, max_ok, sum_ok, inv_ok, n_ok,
         zt_c, o_ok, o_c) = (sem("w_" + n) for n in (
             "windows", "queries", "queries_act", "queries_dve", "scores", "xt", "xt_taken", "shifted", "probs", "probs_turned", "pt_act", "pt_dve",
             "heads", "max", "sum", "inv", "normed", "heads_taken", "out", "added"))
        LAST = CHUNKS - 1

        def pipeline(eng, body):
            body(0, 0)
            with eng.Fori(0, (LAST - 2) // 2) as k:
                for odd in (1, 0):
                    body(k * 2 + (2 - odd), odd)
            for i in range(LAST // 2 * 2 - 1, LAST + 1):
                body(i, i % 2)

        def loops(i, d=0):
            return not isinstance(i, int) or 0 <= i + d <= LAST

        with nc.Block() as block:
            @block.gpsimd
            def _(pool):
                def window(i):
                    if not (isinstance(i, int) and i == 0):
                        pool.wait_ge(s_ok, i)
                        pool.wait_ge(xt_ok, i)
                    for p in range(2):
                        c = m.pieces[HALF[p], ds(i, 1), 0:PIECE]
                        for k in range(2):
                            nc.gpsimd.tensor_copy(m.win_x[HALF[p], k::2, p, :],
                                                  c[:, :, k * WINDOW:k * WINDOW + 2 * KEYS].rearrange("p a (w n) -> p (a w) n", n=KEYS)).then_inc(win_ok, 1)
                window(0)
                with pool.Fori(1, CHUNKS) as i:
                    window(i)

            @block.tensor
            def _(pe):
                def query(i):
                    if not (isinstance(i, int) and i == 0):
                        pe.wait_ge(q_dve, i)
                        pe.wait_ge(q_act, i)
                    x = m.pieces[:, ds(i, 1), WINDOW:PIECE].rearrange("p a n -> p (a n)")
                    for h in range(4, HEADS):
                        mm = nc.tensor.matmul(q_ps[:, h, :], m.win_qk[:, h, :], x, start=True, stop=True)
                    mm.then_inc(q_ok, 1)
                    if not (isinstance(i, int) and i <= 1):
                        pe.wait_ge(xt_c, i)
                    elif i == 1:
                        pe.wait_ge(xt_c, 1)
                    for h in range(4):
                        mm = nc.tensor.matmul(q_ps[:, h, :], m.win_qk[:, h, :], x, start=True, stop=True)
                    mm.then_inc(q_ok, 1)

                def windows_turned(i):
                    pe.wait_ge(q_act, i + 1)
                    pe.wait_ge(win_ok, i * 4 + 4)
                    for w in range(NW):
                        mm = nc.tensor.transpose(xt_ps[:, w, :], m.win_x[:, w, :, :].rearrange("p a n -> p (a n)"), m.ident[:, :])
                    mm.then_inc(xt_ok, 1)

                def scores(i):
                    pe.wait_ge(win_ok, i * 4 + 4)
                    pe.wait_ge(q_act, i + 1)
                    pe.wait_ge(q_dve, i + 1)
                    if not (isinstance(i, int) and i == 0):
                        pe.wait_ge(sub_ok, i * HG)
                    for hg in range(HG):
                        nc.tensor.matmul(s_ps[:, hg, :, :].rearrange("p w n -> p (w n)"), m.ident_bf[:, :], m.win_mask[:, :], start=True, stop=False)
                        for w in range(NW):
                            mm = nc.tensor.matmul(s_ps[:, hg, w, :], queries[:, w, 4 * hg:4 * hg + 4, :].rearrange("p h n -> p (h n)"),
                                                  m.win_x[:, w, :, :].rearrange("p a n -> p (a n)"), start=False, stop=(w == NW - 1))
                    mm.then_inc(s_ok, 1)

                def turn_probs(i):
                    pe.wait_ge(n_ok, i + 1)
                    if not (isinstance(i, int) and i == 0):
                        pe.wait_ge(pt_act, i)
                        pe.wait_ge(pt_dve, i)
                    for hg in range(HG):
                        for w in range(NW):
                            mm = nc.tensor.transpose(t_ps[:, hg, w, :], probs[:, hg, w, :], m.ident[:, :])
                    mm.then_inc(pt_ok, 1)

                def output(i):
                    pe.wait_ge(zt_c, i + 1)
                    for h in range(HEADS):
                        mm = nc.tensor.matmul(o_ps, m.win_vo[:, h, :], heads_t[:, h // 4, :, (h % 4) * WINDOW:(h % 4 + 1) * WINDOW],
                                              start=(h == 0), stop=(h == HEADS - 1))
                    mm.then_inc(o_ok, 1)

                def attend(i, odd):
                    pe.wait_ge(pt_act, i + 1)
                    pe.wait_ge(pt_dve, i + 1)
                    pe.wait_ge(xt_c, i + 1)
                    if not (isinstance(i, int) and i == 0):
                        pe.wait_ge(o_c, i)
                    for hg in range(HG):
                        for w in range(NW):
                            mm = nc.tensor.matmul(z_ps[:, hg, w, :], xt[odd][:, w, :], probs_t[:, hg, w, :], start=True, stop=True)
                    mm.then_inc(z_ok, 1)

                def body(i, odd):
                    if loops(i, 1):
                        scores(i + 1)
                    if loops(i, -1):
                        output(i - 1)
                    turn_probs(i)
                    if loops(i, 1):
                        windows_turned(i + 1)
                    if loops(i, 2):
                        query(i + 2)
                    attend(i, odd)

                query(0)
                scores(0)
                windows_turned(0)
                query(1)
                pipeline(pe, body)
                output(LAST)

            @block.scalar
            def _(act):
                def take_queries(i):
                    act.wait_ge(q_ok, i * 2 + 2)
                    if not (isinstance(i, int) and i == 0):
                        act.wait_ge(s_ok, i)
                    nc.scalar.activation(queries[:, :, 0:4, :], q_ps[:, 0:4, :].rearrange("p h (w n) -> p w h n", w=NW), ACT.Copy).then_inc(q_act, 1)

                def take_windows(i, odd):
                    act.wait_ge(xt_ok, i + 1)
                    if not (isinstance(i, int) and i <= 1):
                        act.wait_ge(z_ok, i - 1)
                    nc.scalar.activation(xt[odd][:, :, :], xt_ps, ACT.Copy).then_inc(xt_c, 1)

                def exps(i):
                    act.wait_ge(sub_ok, (i + 1) * HG)
                    if not (isinstance(i, int) and i == 0):
                        act.wait_ge(pt_ok, i)
                    nc.scalar.activation(probs[:, :, :, :], shifted[:, :, :, :], ACT.Exp).then_inc(p_ok, 1)

                def take_probs(i):
                    act.wait_ge(pt_ok, i + 1)
                    nc.scalar.activation(probs_t[:, 0, :, :], t_ps[:, 0, :, :], ACT.Copy).then_inc(pt_act, 1)

                def take_heads(i):
                    act.wait_ge(z_ok, i + 1)
                    if not (isinstance(i, int) and i == 0):
                        act.wait_ge(o_ok, i)
                    nc.scalar.activation(heads_t[:, :, :, :], z_ps[:, :, :, :], ACT.Copy).then_inc(zt_c, 1)

                def body(i, odd):
                    take_probs(i)
                    if loops(i, 1):
                        take_windows(i + 1, 1 - odd)
                        exps(i + 1)
                    if loops(i, 2):
                        take_queries(i + 2)
                    take_heads(i)

                take_queries(0)
                exps(0)
                take_windows(0, 0)
                take_queries(1)
                pipeline(act, body)

            @block.vector
            def _(dve):
                def take_queries(i):
                    dve.wait_ge(q_ok, i * 2 + 1)
                    if not (isinstance(i, int) and i == 0):
                        dve.wait_ge(s_ok, i)
                    nc.vector.tensor_copy(queries[:, :, 4:HEADS, :], q_ps[:, 4:HEADS, :].rearrange("p h (w n) -> p w h n", w=NW)).then_inc(q_dve, 1)

                def shift(i):
                    dve.wait_ge(s_ok, i + 1)
                    nc.vector.tensor_reduce(rmax[:, :], s_ps[:, :, :, :].rearrange("p g w (a n) -> p (g w a) n", a=2), axis=AX.X, op=ALU.max).then_inc(max_ok, 1)
                    dve.wait_ge(max_ok, i + 1)
                    if not (isinstance(i, int) and i == 0):
                        dve.wait_ge(p_ok, i)
                    for hg in range(HG):
                        half = rmax[:, hg * (NT // HG):(hg + 1) * (NT // HG)]
                        nc.vector.tensor_tensor(shifted[:, hg, :, :].rearrange("p w (a n) -> p (w a) n", a=2),
                                                s_ps[:, hg, :, :].rearrange("p w (a n) -> p (w a) n", a=2),
                                                half.to_broadcast([P, NT // HG, KEYS]), ALU.subtract).then_inc(sub_ok, 1)

                def normalise(i):
                    dve.wait_ge(p_ok, i + 1)
                    nc.vector.tensor_reduce(rsum[:, :], probs[:, :, :, :].rearrange("p g w (a n) -> p (g w a) n", a=2), axis=AX.X, op=ALU.add).then_inc(sum_ok, 1)
                    dve.wait_ge(sum_ok, i + 1)
                    nc.vector.reciprocal(rinv[:, :], rsum[:, :]).then_inc(inv_ok, 1)
                    dve.wait_ge(inv_ok, i + 1)
                    whole = probs[:, :, :, :].rearrange("p g w (a n) -> p (g w a) n", a=2)
                    nc.vector.tensor_tensor(whole, whole, rinv[:, :].to_broadcast([P, NT, KEYS]), ALU.mult).then_inc(n_ok, 1)

                def take_probs(i):
                    dve.wait_ge(pt_ok, i + 1)
                    nc.vector.tensor_copy(probs_t[:, 1, :, :], t_ps[:, 1, :, :]).then_inc(pt_dve, 1)

                def add(i):
                    dve.wait_ge(o_ok, i + 1)
                    x = m.x_flat[:, ds(i * CHUNK, CHUNK)]
                    nc.vector.scalar_tensor_tensor(out=x, in0=o_ps, scalar=m.win_bias[:, 0:1], in1=x, op0=ALU.add, op1=ALU.add).then_inc(o_c, 1)

                def body(i, odd):
                    if loops(i, 1):
                        shift(i + 1)
                    if loops(i, -1):
                        add(i - 1)
                    take_probs(i)
                    if loops(i, 2):
                        take_queries(i + 2)
                    if loops(i, 1):
                        normalise(i + 1)

                take_queries(0)
                shift(0)
                normalise(0)
                take_queries(1)
                pipeline(dve, body)
                add(LAST)


FILTERS = 16
SCALES = 4
AR = 3
SPAN = 2 * P
SPANS = T // SPAN
PIECES16 = 2
PHI_ROW = SPAN + T
PRODUCTS = ((0, 0), (0, 1), (1, 0))
SEGMENTS = [(0, T >> 3), (T >> 3, T >> 3), (T >> 2, T >> 2), (T >> 1, T >> 1)]


def spectral_norm_stage(nc, m):
    def piece(u):
        return m.normed[:, u * (BANK // P):(u + 1) * (BANK // P), :]
    layernorm_stage(nc, m, piece, "s")


def spectral_stage(nc, m):
    KP = FILTERS // 2
    with ExitStack() as ctx:
        sb, pb, sem = open_pools(nc, ctx)
        u = sb("sp_u", [P, T])
        apart = sb("sp_apart", [P, 2, AR - 1 + T])
        ut = sb("sp_ut", [P, PIECES16, 2, SPANS, 2, C], F16)
        sums = [sb(f"sp_sums{k}", [P, 2, T]) for k in range(2)]
        mixk = [sb(f"sp_mix{k}", [P, SCALES, 2, C]) for k in range(2)]
        f_ps = [pb(f"sp_f{b}", [P, T]) for b in range(2)]
        o_ps = pb("sp_o", [P, 2, 2, T // 4])
        (u_ok, apart_ok, ut_hi, ut_ok, ut_c, f_ok, f_act, f_dve, mk_ok, mix_ok, ar_ok, o_c, zero, first_ok) = (sem("st_" + n) for n in (
            "u", "apart", "ut_high", "ut", "ut_taken", "filtered", "taken_act", "taken_dve", "mix_in", "mixed", "ar_done", "added", "zeroed", "first"))

        def out_of(lo, cnt, par):
            half, first = lo // (T // 2), lo % (T // 2) // 2
            return o_ps[HALF[par], half, :, first:first + cnt // 2]

        def tokens(piece, i):
            return ut[:, piece, :, 2 * i:2 * i + 2, :, :].rearrange("p b i a c -> p b (i a) c")

        def turned(i):
            return f_ps[i][:, 0:BANK].rearrange("p (i b c) -> p b i c", b=2, c=C)

        with nc.Block() as block:
            @block.gpsimd
            def _(pool):
                nc.gpsimd.memset(apart[:, :, :], 0.0).then_inc(zero, 1)
                pool.wait_ge(zero, 1)
                with pool.Fori(0, G) as g:
                    pool.wait_ge(ar_ok, g + 1)
                    nc.gpsimd.tensor_copy(u[:, ::-1], m.normed[:, ds(g * (T // 128), T // 128), :].rearrange("p n t -> p (n t)")).then_inc(u_ok, 1)

            @block.tensor
            def _(pe):
                pe.sem_inc(mix_ok, 2)
                pe.sem_inc(ar_ok, 1)
                pe.wait_ge(first_ok, 1)
                pe.wait_ge(m.table_in, 16 * PIECES16 * FILTERS)
                with pe.Fori(0, G) as g:
                    pe.wait_ge(u_ok, g + 1)
                    pe.wait_ge(f_act, g * (2 * FILTERS) + 2)
                    pe.wait_ge(f_dve, g * (2 * FILTERS) + 2)
                    for i in range(SPANS):
                        for par in range(2):
                            first = SPAN * (SPANS - 1 - i) + 1 - par
                            mm = nc.tensor.transpose(f_ps[i // 2][:, (i % 2) * SPAN + par * P:(i % 2) * SPAN + (par + 1) * P],
                                                     u[:, first:first + SPAN - 1:2], m.ident[:, :])
                        mm.then_inc(ut_ok, 1)
                    pe.wait_ge(ut_c, g * 2 + 2)
                    pe.wait_ge(apart_ok, g * 2 + 2)
                    pe.wait_ge(o_c, g + 1)
                    opened = set()
                    for tap in range(AR):
                        for seg, (lo, cnt) in enumerate(SEGMENTS):
                            for par in range(2):
                                first = AR - 1 - tap + lo + par
                                bank = (lo // (T // 2), par)
                                mm = nc.tensor.matmul(out_of(lo, cnt, par), m.ar[:, SCALES - 1 - seg, tap * C:(tap + 1) * C],
                                                      apart[:, :, first:first + cnt - 1:2], start=bank not in opened, stop=False, skip_group_check=True)
                                opened.add(bank)
                    mm.then_inc(ar_ok, 1)

                    def filtered(j, n):
                        for b in range(2):
                            pe.wait_ge(f_act, g * (2 * FILTERS) + j * 4 + (2 * n + b + 1))
                            pe.wait_ge(f_dve, g * (2 * FILTERS) + j * 4 + (2 * n + b + 1))
                            for half in range(2):
                                spans = [i for i in range(SPANS) if i * SPAN < (half + 1) * BANK]
                                for i in spans:
                                    lo = max(half * BANK, i * SPAN)
                                    for hu, hf in PRODUCTS:
                                        mm = nc.tensor.matmul(f_ps[b][:, lo:(half + 1) * BANK], ut[:, hu, b, i, :, :].rearrange("p a c -> p (a c)"),
                                                              m.hankel[:, hf, ds(j * 2 + n, 1), lo - i * SPAN:(half + 1) * BANK - i * SPAN].rearrange("p k t -> p (k t)"),
                                                              start=(i == 0 and (hu, hf) == PRODUCTS[0]), stop=(i == spans[-1] and (hu, hf) == PRODUCTS[-1]))
                            mm.then_inc(f_ok, 1)

                    def mixed(j, n):
                        pe.wait_ge(mk_ok, g * FILTERS + j * 2 + (n + 1))
                        pe.wait_ge(f_act, g * (2 * FILTERS) + j * 4 + (2 * n + 2 + 2))
                        pe.wait_ge(f_dve, g * (2 * FILTERS) + j * 4 + (2 * n + 2 + 2))
                        for seg, (lo, cnt) in enumerate(SEGMENTS):
                            for par in range(2):
                                mm = nc.tensor.matmul(out_of(lo, cnt, par), mixk[n][:, SCALES - 1 - seg, par, :], sums[n][:, :, lo + par:lo + cnt:2],
                                                      start=False, stop=False, skip_group_check=True)
                        mm.then_inc(mix_ok, 1)

                    with pe.Fori(0, KP) as j:
                        filtered(j, 0)
                        filtered(j, 1)
                        mixed(j, 0)
                        mixed(j, 1)

            @block.scalar
            def _(act):
                act.sem_inc(f_act, 2)
                act.wait_ge(zero, 1)
                with act.Fori(0, G) as g:
                    act.wait_ge(ar_ok, g + 1)
                    source = m.normed[:, ds(g * (T // 128), T // 128), :].rearrange("p n t -> p (n t)")
                    for b in range(2):
                        nc.scalar.copy(apart[HALF[b], b, AR - 1:], source[HALF[b], :]).then_inc(apart_ok, 1)
                    act.wait_ge(ut_ok, g * 4 + 4)
                    for i in range(2):
                        nc.scalar.copy(tokens(0, i), turned(i)).then_inc(ut_hi, 1)
                    with act.Fori(0, KP) as j:
                        for n in range(2):
                            for b in range(2):
                                act.wait_ge(f_ok, g * (2 * FILTERS) + j * 4 + (2 * n + b + 1))
                                if b == 0:
                                    act.wait_ge(mix_ok, g * FILTERS + j * 2 + (n + 1))
                                nc.scalar.copy(sums[n][HALF[1], b, 1:T], f_ps[b][HALF[1], 0:T - 1]).then_inc(f_act, 1)

            @block.vector
            def _(dve):
                for n in range(2):
                    last = nc.vector.memset(sums[n][HALF[1], :, 0:1], 0.0)
                last.then_inc(first_ok, 1)
                dve.sem_inc(f_dve, 2)
                dve.sem_inc(o_c, 1)
                with dve.Fori(0, G) as g:
                    for i in range(2):
                        dve.wait_ge(ut_hi, g * 2 + (i + 1))
                        nc.vector.tensor_tensor(tokens(1, i), turned(i), tokens(0, i), ALU.subtract).then_inc(ut_c, 1)
                    with dve.Fori(0, KP) as j:
                        for n in range(2):
                            for b in range(2):
                                dve.wait_ge(f_ok, g * (2 * FILTERS) + j * 4 + (2 * n + b + 1))
                                if b == 0:
                                    dve.wait_ge(mix_ok, g * FILTERS + j * 2 + (n + 1))
                                    nc.vector.tensor_copy(mixk[n][:, :, :, :].rearrange("p s a e -> p (s a e)"),
                                                          m.mix[:, ds(j * 2 + n, 1), :, :, :].rearrange("p k s a e -> p (k s a e)")).then_inc(mk_ok, 1)
                                nc.vector.tensor_copy(sums[n][HALF[0], b, :], f_ps[b][HALF[0], :]).then_inc(f_dve, 1)
                    dve.wait_ge(mix_ok, g * FILTERS + (FILTERS + 2))
                    for b in range(2):
                        for par in range(2):
                            x = m.x[HALF[b], ds(g, 1), par::2].rearrange("c g (h n) -> c (g h) n", h=2)
                            last = nc.vector.tensor_tensor(x, o_ps[HALF[par], :, b, :], x, ALU.add)
                    last.then_inc(o_c, 1)


HEAD_DIM = C // HEADS
TILES = T // P


def norm_stage(nc, m, tag):
    def piece(u):
        return m.normed[:, u * (BANK // P):(u + 1) * (BANK // P), :]
    layernorm_stage(nc, m, piece, tag)


def linear_attention_stage(nc, m):
    NH = P // HEAD_DIM
    UNITS = 2 * G
    HT4 = TILES // 2
    HALVES = (1, 0)
    with ExitStack() as ctx:
        sb, pb, sem = open_pools(nc, ctx)
        kv = [sb(f"lin_kvb{k}", [P, HT4, 2 * P + 1]) for k in range(2)]
        key_e = [sb(f"lin_key_e{k}", [P, HT4, P]) for k in range(2)]
        q_e, q_r = ([sb(f"lin_q_{n}{k}", [P, T]) for k in range(2)] for n in ("e", "r"))
        sums = sb("lin_sums", [P, G, P + NH])
        inv = sb("lin_inv", [P, TILES, NH])
        heads = sb("lin_heads", [P, TILES, P])
        heads_t = sb("lin_heads_t", [P, T])
        big = [pb(f"lin_big{k}", [P, HT4, 2 * P]) for k in range(2)]
        q_ps = pb("lin_qps", [P, T])
        s_ps = [pb(f"lin_sps{k}", [P, BANK]) for k in range(2)]
        (kv_ok, kv_c, ke_ok, mn_ok, phi_ok, s_ok, s_c, ksum, q_ok, qe_ok, pq_ok, v_ok, d_ok, h_ok, t_ok, t_c, o_ok, o_c, ones_ok) = (
            sem("l_" + n) for n in ("kv", "kv_taken", "key_exp", "key_min", "phi_k", "sums", "sums_masked", "key_sums", "q", "q_exp", "phi_q", "heads",
                                    "den", "normed", "turned", "turned_taken", "out", "added", "ones"))

        def tiles(u):
            return range(u * HT4, (u + 1) * HT4)

        with nc.Block() as block:
            @block.tensor
            def _(pe):
                def keys(u):
                    if u >= 2:
                        pe.wait_ge(kv_c, u - 1)
                    for t in tiles(u):
                        mm = nc.tensor.matmul(big[u % 2][:, t % HT4, :], m.normed[:, t, :], m.lin_kv[:, :, :].rearrange("p a c -> p (a c)"), start=True, stop=True)
                    mm.then_inc(kv_ok, 1)

                def sum_up(u):
                    g = u // 2
                    pe.wait_ge(phi_ok, u + 1)
                    if g >= 2:
                        pe.wait_ge(s_c, g - 1)
                    for t in range(HT4):
                        mm = nc.tensor.matmul(s_ps[g % 2][:, 0:P + 1], kv[u % 2][:, t, 0:P], kv[u % 2][:, t, P:2 * P + 1],
                                              start=(u % 2 == 0 and t == 0), stop=(u % 2 == 1 and t == HT4 - 1))
                    mm.then_inc(s_ok, 1)

                def queries(g):
                    for c in range(2):
                        x = m.normed[:, 8 * g + 4 * c:8 * g + 4 * c + 4, :].rearrange("p n t -> p (n t)")
                        mm = nc.tensor.matmul(q_ps[:, c * BANK:(c + 1) * BANK], m.lin_q[:, :], x, start=True, stop=True)
                    mm.then_inc(q_ok, 1)

                pe.wait_ge(ones_ok, 2)
                keys(0)
                keys(1)
                for u in range(UNITS):
                    if u + 2 < UNITS:
                        keys(u + 2)
                    if u == UNITS - 2:
                        queries(0)
                    sum_up(u)
                for g in range(G):
                    pe.wait_ge(pq_ok, g + 1)
                    pe.wait_ge(s_c, G)
                    for half in HALVES:
                        if g and half == 0:
                            pe.wait_ge(o_c, 2 * g)
                        for t in range(HT4):
                            tile = half * HT4 + t
                            mm = nc.tensor.matmul(big[half][:, t, 0:P + NH], q_e[g % 2][:, tile * P:(tile + 1) * P], sums[:, g, :], start=True, stop=True)
                        mm.then_inc(v_ok, 1)
                    if g + 1 < G:
                        queries(g + 1)
                    for n, half in enumerate(HALVES):
                        pe.wait_ge(h_ok, 2 * g + n + 1)
                        if g:
                            pe.wait_ge(t_c, 2 * g - 1 + n)
                        for t in range(HT4):
                            mm = nc.tensor.transpose(s_ps[half][:, t * P:(t + 1) * P], heads[:, half * HT4 + t, :], m.ident[:, :])
                        mm.then_inc(t_ok, 1)
                    for n, c in enumerate(HALVES):
                        pe.wait_ge(t_c, 2 * g + n + 1)
                        out = big[0][:, 2 * c:2 * c + 2, :].rearrange("p a c -> p (a c)")
                        nc.tensor.matmul(out, m.lin_o[:, :], heads_t[:, c * BANK:(c + 1) * BANK], start=True, stop=True).then_inc(o_ok, 1)

            @block.gpsimd
            def _(pool):
                for k in range(2):
                    nc.gpsimd.memset(kv[k][:, :, 2 * P:2 * P + 1], 1.0).then_inc(ones_ok, 1)
                for u in range(UNITS):
                    pool.wait_ge(ke_ok, u + 1)
                    nc.gpsimd.tensor_scalar(key_e[u % 2][:, :, :], key_e[u % 2][:, :, :], 1.0, None, ALU.min).then_inc(mn_ok, 1)

            @block.scalar
            def _(act):
                for u in range(UNITS):
                    act.wait_ge(kv_c, u + 1)
                    if u >= 2:
                        act.wait_ge(phi_ok, u - 1)
                    nc.scalar.activation(key_e[u % 2][:, :, :], kv[u % 2][:, :, 0:P], ACT.Exp).then_inc(ke_ok, 1)

                def exp_queries(g):
                    act.wait_ge(q_ok, g + 1)
                    if g >= 2:
                        act.wait_ge(v_ok, 2 * (g - 1))
                    nc.scalar.activation(q_e[g % 2][:, :], q_ps[:, :], ACT.Exp, bias=m.lin_bias[:, 0:1]).then_inc(qe_ok, 1)

                def relu_queries(g):
                    nc.scalar.activation(q_r[g % 2][:, :], q_ps[:, :], ACT.Relu, bias=m.lin_bias[:, 0:1]).then_inc(qe_ok, 1)

                exp_queries(0)
                relu_queries(0)
                for g in range(G):
                    if g + 1 < G:
                        exp_queries(g + 1)
                    for n, half in enumerate(HALVES):
                        act.wait_ge(t_ok, 2 * g + n + 1)
                        if g:
                            act.wait_ge(o_ok, 2 * g - 1 + n)
                        nc.scalar.copy(heads_t[:, half * BANK:(half + 1) * BANK], s_ps[half][:, :]).then_inc(t_c, 1)
                    if g + 1 < G:
                        relu_queries(g + 1)

            @block.vector
            def _(dve):
                def take_keys(u):
                    dve.wait_ge(kv_ok, u + 1)
                    if u >= 2:
                        dve.wait_ge(s_ok, u - 1)
                    nc.vector.tensor_tensor(kv[u % 2][:, :, 0:2 * P], big[u % 2][:, :, :],
                                            m.lin_rows[:, :, :].rearrange("p a (b c) -> p b (a c)", b=1).to_broadcast([P, HT4, 2 * P]), ALU.add).then_inc(kv_c, 1)

                def phi_keys(u):
                    dve.wait_ge(mn_ok, u + 1)
                    nc.vector.scalar_tensor_tensor(out=kv[u % 2][:, :, 0:P], in0=kv[u % 2][:, :, 0:P], scalar=0.0, in1=key_e[u % 2][:, :, :],
                                                   op0=ALU.max, op1=ALU.add).then_inc(phi_ok, 1)

                def mask(g):
                    dve.wait_ge(s_ok, 2 * g + 2)
                    nc.vector.tensor_tensor(sums[:, g, 0:P], s_ps[g % 2][:, 0:P], m.lin_mask[:, :], ALU.mult).then_inc(ksum, 1)
                    nc.vector.tensor_scalar(sums[:, g, P:P + NH], m.lin_mask[:, ::HEAD_DIM], s_ps[g % 2][:, P:P + 1], None, ALU.mult).then_inc(s_c, 1)

                def phi_queries(g):
                    dve.wait_ge(qe_ok, 2 * g + 2)
                    nc.vector.scalar_tensor_tensor(out=q_e[g % 2][:, :], in0=q_e[g % 2][:, :], scalar=1.0, in1=q_r[g % 2][:, :],
                                                   op0=ALU.min, op1=ALU.add).then_inc(pq_ok, 1)

                take_keys(0)
                for u in range(UNITS):
                    if u + 1 < UNITS:
                        take_keys(u + 1)
                    phi_keys(u)
                    if u and u % 2 == 0:
                        mask(u // 2 - 1)
                phi_queries(0)
                mask(G - 1)
                for g in range(G):
                    for n, half in enumerate(HALVES):
                        part = inv[:, half * HT4:(half + 1) * HT4, :]
                        dve.wait_ge(v_ok, 2 * g + n + 1)
                        nc.vector.tensor_scalar(part, big[half][:, :, P:P + NH], m.eps[:, 0:1], None, ALU.add).then_inc(d_ok, 1)
                        dve.wait_ge(d_ok, 4 * g + 2 * n + 1)
                        nc.vector.reciprocal(part, part).then_inc(d_ok, 1)
                        dve.wait_ge(d_ok, 4 * g + 2 * n + 2)
                        if g:
                            dve.wait_ge(t_ok, 2 * g - 1 + n)
                        nc.vector.tensor_tensor(heads[:, half * HT4:(half + 1) * HT4, :].rearrange("p t (h d) -> p t h d", d=HEAD_DIM),
                                                big[half][:, :, 0:P].rearrange("p t (h d) -> p t h d", d=HEAD_DIM),
                                                part.to_broadcast([P, HT4, NH, HEAD_DIM]), ALU.mult).then_inc(h_ok, 1)
                    if g + 1 < G:
                        phi_queries(g + 1)
                    for n, c in enumerate(HALVES):
                        dve.wait_ge(o_ok, 2 * g + n + 1)
                        x = m.x_flat[:, g * T + c * BANK:g * T + (c + 1) * BANK]
                        nc.vector.scalar_tensor_tensor(out=x, in0=big[0][:, 2 * c:2 * c + 2, :].rearrange("p a c -> p (a c)"), scalar=m.lin_bias[:, 1:2], in1=x,
                                                       op0=ALU.add, op1=ALU.add).then_inc(o_c, 1)


EXPERTS = 32
HIDDEN = 256
HT = HIDDEN // P
TOP = 8
QUADS = B // 4


def expert_stage(nc, m, ins, out):
    with ExitStack() as ctx:
        sb, pb, sem = open_pools(nc, ctx)
        gate = sb("gate_w", [EXPERTS, C])
        gate_t = sb("gate_t", [P, 2 * EXPERTS])
        gate_b = sb("gate_b", [P, 1])
        b2 = sb("ex_b2", [EXPERTS, C])
        b2_t = sb("ex_b2_t", [C, EXPERTS])
        logits = [sb(f"ex_logits{q}", [P, T]) for q in range(QUADS)]
        probs = [sb(f"ex_probs{q}", [P, T]) for q in range(QUADS)]
        kept_t = [sb(f"ex_kept_t{q}", [P, TILES, P]) for q in range(QUADS)]
        xt = sb("ex_xt", [P, G, TILES, P])
        top = [sb(f"ex_top{q}", [P, TOP]) for q in range(QUADS)]
        stat = sb("ex_stat", [P, QUADS, 4])
        pooled = sb("ex_pooled", [C + 1, EXPERTS, B])
        hidden = sb("ex_hidden", [P, EXPERTS, HT, B])
        made = sb("ex_made", [C, B, EXPERTS])
        spread = sb("ex_spread", [P, G, P])
        l_ps = [pb(f"ex_l{q}", [P, T]) for q in range(QUADS)]
        t_ps = [pb(f"ex_t{q}", [P, BANK]) for q in range(2)]
        a_ps, b_ps = pb("ex_a", [P, BANK]), pb("ex_b", [P, BANK])
        kept = logits
        (w_in, g_t, g_c, zeroed, l_ok, x_t, x_c, lg_ok, mx_ok, e_ok, step, keep_ok, k_t, k_c, p_ok, p_c, h_ok, h_c, m_ok, m_c, s_t, s_c, o_ok, o_c, done, b_c) = (
            sem("e_" + n) for n in ("w_in", "gate_turned", "gate_taken", "zeroed", "logits", "x_turned", "x_taken", "lg", "max", "exp", "step", "kept", "kept_turned",
                                    "kept_taken", "pooled", "pooled_taken", "hidden", "gelu", "made", "made_taken", "spread_turned", "spread", "out", "added", "stored", "b2"))
        with nc.Block() as block:
            @block.sync
            def _(sp):
                sp.dma_start(gate[:, :], ins["L3_ffn_gate_w"]).then_inc(w_in, 16)
                for q in range(4):
                    sp.dma_start(gate_b[q * EXPERTS:(q + 1) * EXPERTS, :], ins["L3_ffn_gate_b"].rearrange("(e a) -> e a", a=1)).then_inc(w_in, 16)
                sp.dma_start(b2[:, :], ins["L3_ffn_weight2"][:, HIDDEN, :]).then_inc(w_in, 16)
                for g in range(G):
                    sp.wait_ge(o_c, 2 * g + 2)
                    for p in range(2):
                        sp.dma_start(out[2 * g + p].rearrange("c h w -> c (h w)"), m.x[HALF[p], g, :]).then_inc(done, 16)
                sp.wait_ge(done, 16 * B)

            @block.gpsimd
            def _(pool):
                nc.gpsimd.memset(gate_t[:, :], 0.0).then_inc(zeroed, 1)
                nc.gpsimd.memset(spread[:, :, :], 0.0).then_inc(zeroed, 1)
                pool.wait_ge(zeroed, 2)
                nc.gpsimd.memset(pooled[C:C + 1, :, :], 1.0).then_inc(zeroed, 1)

            @block.tensor
            def _(pe):
                pe.wait_ge(w_in, 96)
                for p in range(2):
                    mm = nc.tensor.transpose(a_ps[0:C, p * EXPERTS:(p + 1) * EXPERTS], (gate, b2)[p][:, :], m.ident[0:EXPERTS, 0:EXPERTS])
                mm.then_inc(g_t, 1)
                for n in range(G * 2):
                    g, half = n // 2, n % 2
                    if n == 1:
                        pe.wait_ge(g_c, 2)
                        for gg in range(G):
                            for c in range(2):
                                mm = nc.tensor.matmul(l_ps[gg // 2][(gg % 2) * C:(gg % 2 + 1) * C, c * BANK:(c + 1) * BANK], gate_t[:, :],
                                                      m.normed[:, gg * 8 + c * 4:gg * 8 + c * 4 + 4, :].rearrange("p n t -> p (n t)"), start=True, stop=True)
                            mm.then_inc(l_ok, 1)
                    if n >= 2:
                        pe.wait_ge(x_c, n - 1)
                    for t in range(4):
                        mm = nc.tensor.transpose(t_ps[n % 2][:, t * P:(t + 1) * P], m.normed[:, g * 8 + half * 4 + t, :], m.ident[:, :])
                    mm.then_inc(x_t, 1)
                pe.wait_ge(x_c, 2 * G)
                for q in range(QUADS):
                    pe.wait_ge(keep_ok, q + 1)
                    for half in range(2):
                        if q:
                            pe.wait_ge(k_c, half + 1)
                        for t in range(4):
                            tile = half * 4 + t
                            mm = nc.tensor.transpose(t_ps[half][:, t * P:(t + 1) * P], kept[q][:, tile * P:(tile + 1) * P], m.ident[:, :])
                        mm.then_inc(k_t, 1)
                for g in range(G):
                    if g % 2 == 0:
                        pe.wait_ge(k_c, g + 2)
                    for t in range(TILES):
                        mm = nc.tensor.matmul(b_ps[:, g * P:(g + 1) * P], xt[:, g, t, :], kept_t[g // 2][:, t, :], start=(t == 0), stop=(t == TILES - 1))
                    mm.then_inc(p_ok, 1)
                pe.wait_ge(p_c, B)
                pe.wait_ge(m.ex_in, 16 * 3)
                for e in range(EXPERTS):
                    for t in range(HT):
                        mm = nc.tensor.matmul(a_ps[:, :].rearrange("p (e t b) -> p e t b", e=EXPERTS, t=HT)[:, e, t, :], m.ex_w1[:, e, t * P:(t + 1) * P],
                                              pooled[:, e, :], start=True, stop=True)
                mm.then_inc(h_ok, 1)
                pe.wait_ge(h_c, 1)
                for e in range(EXPERTS):
                    for t in range(HT):
                        mm = nc.tensor.matmul(b_ps[0:C, e * B:(e + 1) * B], m.ex_w2[:, e, t, :], hidden[:, e, t, :], start=(t == 0), stop=(t == HT - 1))
                mm.then_inc(m_ok, 1)
                pe.wait_ge(m_c, 1)
                for q in range(QUADS):
                    mm = nc.tensor.transpose(a_ps[:, q * C:(q + 1) * C], made[:, 4 * q:4 * q + 4, :].rearrange("c b e -> c (b e)"), m.ident[0:C, 0:C])
                mm.then_inc(s_t, 1)
                pe.wait_ge(s_c, B)
                for g in range(G):
                    for c in range(2):
                        n = 2 * g + c
                        if n >= 2:
                            pe.wait_ge(o_c, n - 1)
                        nc.tensor.matmul(t_ps[n % 2][:, :], spread[:, g, :], kept[g // 2][:, c * BANK:(c + 1) * BANK], start=True, stop=True).then_inc(o_ok, 1)

            @block.scalar
            def _(act):
                for n in range(2 * G):
                    g, half = n // 2, n % 2
                    act.wait_ge(x_t, n + 1)
                    nc.scalar.copy(xt[:, g, half * 4:half * 4 + 4, :], t_ps[n % 2][:, :].rearrange("p (t c) -> p t c", c=P)).then_inc(x_c, 1)
                for q in range(QUADS):
                    act.wait_ge(mx_ok, q + 1)
                    nc.scalar.activation(probs[q][:, :], logits[q][:, :], ACT.Exp, bias=stat[:, q, 0:1], accum_out=stat[:, q, 1:2]).then_inc(e_ok, 1)
                for q in range(QUADS):
                    for half in range(2):
                        act.wait_ge(k_t, 2 * q + half + 1)
                        nc.scalar.copy(kept_t[q][:, half * 4:half * 4 + 4, :], t_ps[half][:, :].rearrange("p (t c) -> p t c", c=P)).then_inc(k_c, 1)
                act.wait_ge(h_ok, 1)
                nc.scalar.activation(hidden[:, :, :, :], a_ps[:, :].rearrange("p (e t b) -> p e t b", e=EXPERTS, t=HT), ACT.Gelu).then_inc(h_c, 1)

            @block.vector
            def _(dve):
                dve.wait_ge(g_t, 1)
                dve.wait_ge(zeroed, 3)
                for p in range(2):
                    nc.vector.tensor_copy(gate_t[HALF[p], p * EXPERTS:(p + 1) * EXPERTS], a_ps[0:C, 0:EXPERTS]).then_inc(g_c, 1)
                nc.vector.tensor_copy(b2_t[:, :], a_ps[0:C, EXPERTS:2 * EXPERTS]).then_inc(b_c, 1)
                dve.wait_ge(w_in, 96)
                for q in range(QUADS):
                    dve.wait_ge(l_ok, 2 * q + 2)
                    nc.vector.tensor_scalar(logits[q][:, :], l_ps[q][:, :], gate_b[:, 0:1], None, ALU.add).then_inc(lg_ok, 1)
                    dve.wait_ge(lg_ok, q + 1)
                    nc.vector.tensor_reduce(stat[:, q, 0:1], logits[q][:, :], axis=AX.X, op=ALU.max, negate=True).then_inc(mx_ok, 1)
                n = 0
                for q in range(QUADS):
                    def link(ins_):
                        nonlocal n
                        n += 1
                        ins_.then_inc(step, 1)
                        dve.wait_ge(step, n)
                    dve.wait_ge(e_ok, q + 1)
                    link(nc.vector.reciprocal(stat[:, q, 2:3], stat[:, q, 1:2]))
                    link(nc.vector.tensor_scalar(probs[q][:, :], probs[q][:, :], stat[:, q, 2:3], None, ALU.mult))
                    link(nc.vector.max(top[q][:, :], probs[q][:, :]))
                    link(nc.vector.match_replace(kept[q][:, :], top[q][:, :], probs[q][:, :], 0.0))
                    nc.vector.tensor_tensor(kept[q][:, :], probs[q][:, :], kept[q][:, :], ALU.subtract).then_inc(keep_ok, 1)
                dve.wait_ge(p_ok, G)
                for g in range(G):
                    for p in range(2):
                        b = 2 * g + p
                        src = b_ps[HALF[p], g * P + (b % 4) * EXPERTS:g * P + (b % 4 + 1) * EXPERTS]
                        nc.vector.tensor_copy(pooled[0:C, :, b], src).then_inc(p_c, 1)
                dve.wait_ge(m_ok, 1)
                nc.vector.tensor_tensor(made[:, :, :].rearrange("c b e -> c e b"), b_ps[0:C, 0:B * EXPERTS].rearrange("c (e b) -> c e b", b=B),
                                        b2_t[:, :].to_broadcast([C, EXPERTS, B]), ALU.add).then_inc(m_c, 1)
                dve.wait_ge(s_t, 1)
                for b in range(B):
                    rows = slice((b % 4) * EXPERTS, (b % 4 + 1) * EXPERTS)
                    nc.vector.tensor_copy(spread[rows, b // 2, (b % 2) * C:(b % 2 + 1) * C], a_ps[rows, (b // 4) * C:(b // 4 + 1) * C]).then_inc(s_c, 1)
                for n in range(2 * G):
                    dve.wait_ge(o_ok, n + 1)
                    x = m.x_flat[:, n * BANK:(n + 1) * BANK]
                    nc.vector.tensor_tensor(x, t_ps[n % 2][:, :], x, ALU.add).then_inc(o_c, 1)


def expert_load(nc, m, ins, eng):
    eng.dma_start(m.ex_w1[:, :, :], ins["L3_ffn_weight1"].rearrange("e d h -> d e h")).then_inc(m.ex_in, 16)
    for t in range(HT):
        eng.dma_start(m.ex_w2[:, :, t, :], ins["L3_ffn_weight2"][:, t * P:(t + 1) * P, :].rearrange("e h o -> h e o")).then_inc(m.ex_in, 16)


TINY = 1e-30
LOADS = 40


class RawWeights:
    pass


def raw_weights(nc, ctx):
    sb, pb, sem = open_pools(nc, ctx)
    raw = RawWeights()
    raw.conv = sb("conv_raw", [C, 4, C * TAPS])
    raw.wq, raw.wk, raw.wv = (sb(n, [C, HEADS, C]) for n in ("win_wq", "win_wk", "win_wv"))
    raw.wu = sb("win_wu", [C, HEADS * C])
    raw.phi = sb("phi_in", [P, T // P, FILTERS])
    raw.sigma = sb("sigma", [FILTERS, 2])
    raw.logits, raw.gumbel = sb("pick_logits", [P, SCALES]), sb("pick_gumbel", [P, SCALES])
    return raw


def weight_loads(m, raw, ins, sp):
    def load(dst, src):
        sp.dma_start(dst, src).then_inc(m.w_in, 16)

    def column(name):
        return ins[name].rearrange("(c a) -> c a", a=1)

    def row(name, n):
        return ins[name].rearrange("(a c) -> a c", a=1).to_broadcast([P, n])

    for n, name in enumerate(("d", "u", "r", "l")):
        load(raw.conv[:, n, :], ins["L1_conv_w_" + name].rearrange("o i k -> o (i k)"))
        for p in range(2):
            load(m.conv_bias[HALF[p], n:n + 1], column("L1_conv_b_" + name))
    load(raw.phi[:, :, :], ins["L2_ffn_phi"][0:T, :].rearrange("(n p) k -> p n k", p=P))
    for dst, n in ((raw.wq, "Wq"), (raw.wk, "Wk"), (raw.wv, "Wv")):
        load(dst[:, :, :], ins["L2_attn_" + n].rearrange("(h e) c -> e h c", h=HEADS))
    load(raw.wu[:, :], ins["L2_attn_Wu"])
    load(raw.sigma[:, 0:1], column("L2_ffn_sigma"))
    load(raw.logits[:, :], row("L2_ffn_log_weights", SCALES))
    load(raw.gumbel[:, :], row("L2_ffn_gumbel", SCALES))
    for p in range(2):
        cols = slice(p * C, (p + 1) * C)
        load(m.win_bias[HALF[p], 0:1], column("L2_attn_bu"))
        load(m.ar[HALF[p], :, :].rearrange("d i (k e) -> d (i k) e", e=C), ins["L2_ffn_M_u"].rearrange("i k d e -> d (i k) e"))
        load(m.lin_q[HALF[p], cols], ins["L3_attn_Wq"])
        load(m.lin_kv[HALF[p], 0, cols], ins["L3_attn_Wk"])
        load(m.lin_kv[HALF[p], 1, cols], ins["L3_attn_Wv"])
        load(m.lin_o[HALF[p], cols], ins["L3_attn_Wo"])
        load(m.lin_bias[HALF[p], 0:1], column("L3_attn_bq"))
        load(m.lin_bias[HALF[p], 1:2], column("L3_attn_bo"))
        load(m.lin_rows[:, 0, cols], row("L3_attn_bk", C))
        load(m.lin_rows[:, 1, cols], row("L3_attn_bv", C))
    for p in range(2):
        for dst, n in ((m.plus, "M_phi_plus"), (m.minus, "M_phi_minus")):
            sp.dma_start(dst[HALF[p], :, :].rearrange("d i (k e) -> d (i k) e", e=C), ins["L2_ffn_" + n].rearrange("i k d e -> d (i k) e")).then_inc(m.mats_in, 16)


def weights_stage(nc, m, raw, phi_rows):
    with ExitStack() as ctx:
        sb, pb, sem = open_pools(nc, ctx)
        NP = TAPS + 2
        padded = sb("conv_padded", [C, 4, NP, C])
        wut = sb("win_wut", [C, HEADS, C])
        mask = sb("win_mask", [P, KEYS])
        phi_n = sb("phi_n", [FILTERS, T])
        phi_t = sb("phi_t", [FILTERS, PIECES16, PHI_ROW], F16)
        size = sb("phi_size", [FILTERS, 4])
        ones, diag = sb("phi_ones", [FILTERS, P]), sb("phi_diag", [FILTERS, FILTERS])
        col = sb("pick_col", [P, 4])
        turned = pb("conv_turned", [P, SHIFTS, 2, C])
        qk_ps, vo_ps, wut_ps = (pb(n, [P, HEADS, C]) for n in ("qk_ps", "vo_ps", "wut_ps"))
        phi_ps, gain_ps = pb("phi_t_ps", [FILTERS, T]), pb("gain_ps", [P, BANK])
        (t_ok, t_c, qk_ok, vo_ok, mk, phi_ok, sig_ok, row_ok, exp_ok, step, pstep, diag_ok, gain_ok, pad_ok, turned_ok, taken, rows_out) = (sem("ws_" + n) for n in (
            "wut", "wut_taken", "qk", "vo", "mask_step", "phi_turned", "sigma", "rows", "exp", "pick_step", "phi_step", "diag", "gain",
            "taps_padded", "taps_turned", "taps_taken", "phi_rows_out"))
        with nc.Block() as block:
            @block.sync
            def _(sp):
                sp.wait_ge(row_ok, 3)
                sp.dma_start(phi_rows, phi_t[:, :, :]).then_inc(rows_out, 16)
                sp.wait_ge(rows_out, 16)

            @block.scalar
            def _(act):
                act.wait_ge(m.w_in, 16 * LOADS)
                act.wait_ge(pad_ok, 2)
                for n in range(4):
                    nc.scalar.copy(padded[:, n, 1:NP - 1, :], raw.conv[:, n, :].rearrange("o (i k) -> o k i", k=TAPS)).then_inc(pad_ok, 1)
                nc.scalar.activation(raw.sigma[:, 1:2], raw.sigma[:, 0:1], ACT.Sqrt).then_inc(sig_ok, 1)
                act.wait_ge(sig_ok, 1)
                nc.scalar.activation(raw.sigma[:, 0:1], raw.sigma[:, 1:2], ACT.Sqrt).then_inc(sig_ok, 1)
                for n in range(4):
                    act.wait_ge(turned_ok, n + 1)
                    nc.scalar.copy(m.toeplitz[:, n, :, :], turned[:, :, :, :].rearrange("p s a c -> p s (a c)")).then_inc(taken, 1)
                act.wait_ge(step, 2)
                nc.scalar.activation(m.soft[:, :], raw.logits[:, :], ACT.Exp, bias=col[:, 0:1], accum_out=col[:, 1:2]).then_inc(exp_ok, 1)

            @block.gpsimd
            def _(pool):
                nc.gpsimd.memset(m.win_x[:, :, :, :], 0.0)
                blocks = m.lin_mask[:, :].rearrange("p (h d) -> p h d", d=HEAD_DIM)
                nc.gpsimd.memset(m.lin_mask[:, :], 1.0).then_inc(mk, 1)
                nc.gpsimd.memset(mask[:, :], 0.0).then_inc(mk, 1)
                pool.wait_ge(mk, 2)
                nc.gpsimd.affine_select(out=blocks, in_=blocks, compare_op=ALU.is_ge, fill=0.0, base=0,
                                        pattern=[[-HEAD_DIM, P // HEAD_DIM], [0, HEAD_DIM]], channel_multiplier=1).then_inc(mk, 1)
                pool.wait_ge(mk, 3)
                nc.gpsimd.affine_select(out=blocks, in_=blocks, compare_op=ALU.is_ge, fill=0.0, base=HEAD_DIM - 1,
                                        pattern=[[HEAD_DIM, P // HEAD_DIM], [0, HEAD_DIM]], channel_multiplier=-1).then_inc(mk, 1)
                pool.wait_ge(mk, 4)
                for q in range(P // WINDOW):
                    rows = mask[q * WINDOW:(q + 1) * WINDOW, :]
                    nc.gpsimd.affine_select(out=rows, in_=rows, compare_op=ALU.is_ge, fill=MASKED, base=-1,
                                            pattern=[[1, KEYS]], channel_multiplier=-1).then_inc(mk, 1)
                    pool.wait_ge(mk, 2 * q + 5)
                    nc.gpsimd.affine_select(out=rows, in_=rows, compare_op=ALU.is_ge, fill=MASKED, base=WINDOW,
                                            pattern=[[-1, KEYS]], channel_multiplier=1).then_inc(mk, 1)
                    pool.wait_ge(mk, 2 * q + 6)
                for n in range(BANK // KEYS):
                    nc.gpsimd.tensor_copy(m.win_mask[:, n * KEYS:(n + 1) * KEYS], mask[:, :])

            @block.tensor
            def _(pe):
                pe.wait_ge(m.w_in, 16 * LOADS)
                for n in range(T // P):
                    mm = nc.tensor.transpose(phi_ps[:, n * P:(n + 1) * P], raw.phi[:, n, :], m.ident[:, :])
                mm.then_inc(phi_ok, 1)
                for h in range(HEADS):
                    mm = nc.tensor.transpose(wut_ps[0:C, h, :], raw.wu[:, h * C:(h + 1) * C], m.ident[0:C, 0:C])
                mm.then_inc(t_ok, 1)
                for p in range(2):
                    for h in range(HEADS):
                        mm = nc.tensor.matmul(qk_ps[HALF[p], h, :], raw.wq[:, h, :], raw.wk[:, h, :], start=True, stop=True)
                mm.then_inc(qk_ok, 1)
                pe.wait_ge(t_c, 1)
                for p in range(2):
                    for h in range(HEADS):
                        mm = nc.tensor.matmul(vo_ps[HALF[p], h, :], raw.wv[:, h, :], wut[:, h, :], start=True, stop=True)
                mm.then_inc(vo_ok, 1)
                pe.wait_ge(pad_ok, 6)
                for n in range(4):
                    if n:
                        pe.wait_ge(taken, n)
                    for s in range(SHIFTS):
                        for po in range(2):
                            first = 2 * s - po + 1
                            mm = nc.tensor.transpose(turned[:, s, po, :], padded[:, n, first:first + 2, :].rearrange("o t i -> o (t i)"), m.ident[0:C, 0:C])
                    mm.then_inc(turned_ok, 1)
                pe.wait_ge(diag_ok, 2)
                nc.tensor.matmul(gain_ps[:, 0:FILTERS], ones[:, :], diag[:, :], start=True, stop=True).then_inc(gain_ok, 1)

            @block.vector
            def _(dve):
                for edge in (0, NP - 1):
                    nc.vector.memset(padded[:, :, edge, :], 0.0).then_inc(pad_ok, 1)
                nc.vector.memset(ones[:, :], 1.0).then_inc(diag_ok, 1)
                nc.vector.memset(phi_t[:, :, 0:SPAN], 0.0).then_inc(row_ok, 1)
                done, filters_done = [0], [0]

                def link(ins_):
                    done[0] += 1
                    ins_.then_inc(step, 1)
                    dve.wait_ge(step, done[0])

                def link_phi(ins_):
                    filters_done[0] += 1
                    ins_.then_inc(pstep, 1)
                    dve.wait_ge(pstep, filters_done[0])

                dve.wait_ge(m.w_in, 16 * LOADS)
                link(nc.vector.tensor_tensor(raw.logits[:, :], raw.logits[:, :], raw.gumbel[:, :], ALU.add))
                link(nc.vector.tensor_reduce(col[:, 0:1], raw.logits[:, :], axis=AX.X, op=ALU.max, negate=True))
                dve.wait_ge(phi_ok, 1)
                link_phi(nc.vector.tensor_reduce(size[:, 0:1], phi_ps[:, :], axis=AX.X, op=ALU.max))
                link_phi(nc.vector.tensor_reduce(size[:, 1:2], phi_ps[:, :], axis=AX.X, op=ALU.min, negate=True))
                link_phi(nc.vector.tensor_tensor(size[:, 0:1], size[:, 0:1], size[:, 1:2], ALU.max))
                link_phi(nc.vector.tensor_scalar(size[:, 0:1], size[:, 0:1], TINY, None, ALU.max))
                link_phi(nc.vector.reciprocal(size[:, 2:3], size[:, 0:1]))
                link_phi(nc.vector.tensor_scalar(phi_n[:, :], phi_ps[:, :], size[:, 2:3], None, ALU.mult))
                nc.vector.tensor_copy(phi_t[:, 0, SPAN:], phi_n[:, :]).then_inc(row_ok, 1)
                dve.wait_ge(t_ok, 1)
                nc.vector.tensor_copy(wut[:, :, :], wut_ps[0:C, :, :]).then_inc(t_c, 1)
                dve.wait_ge(row_ok, 2)
                nc.vector.tensor_tensor(phi_t[:, 1, SPAN:], phi_n[:, :], phi_t[:, 0, SPAN:], ALU.subtract).then_inc(row_ok, 1)
                dve.wait_ge(sig_ok, 2)
                link_phi(nc.vector.tensor_tensor(size[:, 3:4], size[:, 0:1], raw.sigma[:, 0:1], ALU.mult))
                nc.vector.tensor_scalar(diag[:, :], m.ident[0:FILTERS, 0:FILTERS], size[:, 3:4], None, ALU.mult).then_inc(diag_ok, 1)
                dve.wait_ge(qk_ok, 1)
                for p in range(2):
                    nc.vector.tensor_scalar(m.win_qk[HALF[p], :, p * C:(p + 1) * C], qk_ps[HALF[p], :, :], C ** -0.5, None, ALU.mult)
                dve.wait_ge(vo_ok, 1)
                for p in range(2):
                    nc.vector.tensor_copy(m.win_vo[HALF[p], :, p * C:(p + 1) * C], vo_ps[HALF[p], :, :])
                dve.wait_ge(exp_ok, 1)
                link(nc.vector.reciprocal(col[:, 2:3], col[:, 1:2]))
                link(nc.vector.tensor_scalar(m.soft[:, :], m.soft[:, :], col[:, 2:3], None, ALU.mult))
                nc.vector.tensor_reduce(m.best[:, :], m.soft[:, :], axis=AX.X, op=ALU.max)
                dve.wait_ge(gain_ok, 1)
                nc.vector.tensor_copy(m.gain[:, :], gain_ps[:, 0:FILTERS])


def spectral_mixing(nc, m, block, step):
    @block.gpsimd
    def _(pool):
        done = [0]

        def link(ins_):
            done[0] += 1
            ins_.then_inc(step, 1)
            pool.wait_ge(step, done[0])

        pick, free, weights, gains = m.pick[:, 0, :], m.pick[:, 1, :], m.pick[:, 2:4, :], m.gains
        link(nc.gpsimd.tensor_scalar(pick, m.soft[:, :], m.best[:, :], None, ALU.is_equal))
        link(nc.gpsimd.tensor_scalar(free, pick, -1.0, 1.0, ALU.mult, ALU.add))
        for i in range(1, SCALES):
            for j in range(i):
                link(nc.gpsimd.tensor_tensor(pick[:, i:i + 1], pick[:, i:i + 1], free[:, j:j + 1], ALU.mult))
        link(nc.gpsimd.tensor_tensor(pick, pick, m.soft[:, :], ALU.subtract))
        link(nc.gpsimd.tensor_tensor(weights[:, 0, :], pick, m.soft[:, :], ALU.add))
        link(nc.gpsimd.tensor_scalar(weights[HALF[0], 1, :], weights[HALF[0], 0, :], 1.0, None, ALU.mult))
        link(nc.gpsimd.tensor_scalar(weights[HALF[1], 1, :], weights[HALF[1], 0, :], -1.0, None, ALU.mult))
        for i in range(SCALES):
            for sign in range(2):
                link(nc.gpsimd.tensor_scalar(gains[:, sign, i, :], m.gain[:, :], weights[:, sign, i:i + 1], None, ALU.mult))
            link(nc.gpsimd.tensor_scalar(m.ar[:, i, :], m.ar[:, i, :], weights[:, 0, i:i + 1], None, ALU.mult))
            if i:
                link(nc.gpsimd.tensor_tensor(m.ar[:, i, :], m.ar[:, i, :], m.ar[:, i - 1, :], ALU.add))
        pool.wait_ge(m.mats_in, 64)
        for sign, mats in ((0, m.plus), (1, m.minus)):
            for i in range(SCALES):
                by_filter = mats[:, i, :].rearrange("p (k e) -> p k e", e=C)
                link(nc.gpsimd.tensor_tensor(by_filter, by_filter, gains[:, sign, i, :].to_broadcast([P, FILTERS, C]), ALU.mult))
                if i:
                    link(nc.gpsimd.tensor_tensor(mats[:, i, :], mats[:, i, :], mats[:, i - 1, :], ALU.add))
        for i in range(SCALES):
            for par, op in ((0, ALU.add), (1, ALU.subtract)):
                nc.gpsimd.tensor_tensor(m.mix[:, :, i, par, :], m.plus[:, i, :].rearrange("p (k e) -> p k e", e=C),
                                        m.minus[:, i, :].rearrange("p (k e) -> p k e", e=C), op)


def hankel_load(nc, m, phi_rows, sp):
    for piece in range(PIECES16):
        for k in range(FILTERS):
            src = bass.AP(phi_rows.tensor, (k * PIECES16 + piece) * PHI_ROW + SPAN - 2 * (P - 1), [[2, P], [1, T]])
            sp.dma_start(m.hankel[:, piece, k, :], src).then_inc(m.table_in, 16)


def hybrid_program(nc, ins, out):
    with ExitStack() as whole:
        sb, pb, sem = open_pools(nc, whole)
        m = Memory()
        m.x = sb("x", [P, G, T])
        m.x_flat = m.x[:, :, :].rearrange("p g t -> p (g t)")
        m.ident, m.ident_bf = sb("ident", [P, P]), sb("ident_bf", [P, P], BF16)
        m.average, m.centre, m.eps = sb("average", [P, P]), sb("centre", [P, P]), sb("eps", [P, 1])
        m.win_qk, m.win_vo = sb("win_qk", [P, HEADS, P]), sb("win_vo", [P, HEADS, P])
        m.win_x, m.win_mask, m.win_bias = sb("win_x", [P, NW, 2, KEYS]), sb("win_maskb", [P, BANK], BF16), sb("win_bias", [P, 1])
        m.mix, m.ar = sb("mix", [P, FILTERS, SCALES, 2, C]), sb("ar", [P, SCALES, AR * C])
        m.lin_q, m.lin_o, m.lin_kv = sb("lin_q", [P, P]), sb("lin_o", [P, P]), sb("lin_kv", [P, 2, P])
        m.lin_bias, m.lin_rows, m.lin_mask = sb("lin_bias", [P, 2]), sb("lin_rows", [P, 2, P]), sb("lin_mask", [P, P])
        m.w_in, m.mats_in, m.table_in, m.ex_in = sem("weights_in"), sem("mats_in"), sem("table_in"), sem("ex_in")
        phi_rows = nc.dram_tensor("phi_rows", (FILTERS, PIECES16, PHI_ROW), F16).ap()

        with nc.cleanup_on_exit(), ExitStack() as ctx:
            sb, pb, sem = open_pools(nc, ctx)
            m.rows, m.cols = sb("rows", [P, H, B, ROWP]), sb("cols", [P, W, B, ROWP])
            m.toeplitz, m.conv_bias = sb("toeplitz", [P, 4, SHIFTS, P]), sb("conv_bias", [P, 4])
            m.w_theta, m.w_phi, m.w_g = sb("w_theta", [C // 2, C]), sb("w_phi", [C // 2, C]), sb("w_g", [C // 2, C])
            m.w_last = sb("w_last", [C, C // 2])
            m.plus, m.minus = (sb("m_" + n, [P, SCALES, FILTERS * C]) for n in ("plus", "minus"))
            m.soft, m.best, m.pick = sb("pick_soft", [P, SCALES]), sb("pick_best", [P, 1]), sb("pick_weights", [P, 4, SCALES])
            m.gain, m.gains = sb("filter_gain", [P, FILTERS]), sb("filter_gains", [P, 2, SCALES, FILTERS])
            raw = raw_weights(nc, ctx)
            mixing_step = sem("mixing_step")

            def loads(block):
                @block.sync
                def _(sp):
                    weight_loads(m, raw, ins, sp)

            setup_stage(nc, m, ins)
            nonlocal_stage(nc, m, loads)
            weights_stage(nc, m, raw, phi_rows)
            conv_passes(nc, m, m.rows, 0, "v", lambda block: spectral_mixing(nc, m, block, mixing_step))
            rows_to_cols_stage(nc, m)
            conv_passes(nc, m, m.cols, 2, "h")
            cols_to_tokens_stage(nc, m)

        with ExitStack() as late:
            sb, pb, sem = open_pools(nc, late)
            m.normed = sb("normed", [P, G * T // 128, 128])
            with ExitStack() as filters:
                sb, pb, sem = open_pools(nc, filters)
                m.hankel = sb("hankel", [P, PIECES16, FILTERS, T], F16)

                with ExitStack() as ctx:
                    sb, pb, sem = open_pools(nc, ctx)
                    m.pieces = sb("pieces", [P, CHUNKS, PIECE])
                    window_norm_stage(nc, m, lambda nc, m, sp: hankel_load(nc, m, phi_rows, sp))
                    window_attention_stage(nc, m)

                spectral_norm_stage(nc, m)
                spectral_stage(nc, m)

            with ExitStack() as ctx:
                sb, pb, sem = open_pools(nc, ctx)
                m.ex_w1, m.ex_w2 = sb("ex_w1", [C + 1, EXPERTS, HIDDEN]), sb("ex_w2", [P, EXPERTS, HT, C])
                with nc.Block() as block:
                    @block.sync
                    def _(sp):
                        expert_load(nc, m, ins, sp)
                norm_stage(nc, m, "l")
                linear_attention_stage(nc, m)
                norm_stage(nc, m, "e")
                expert_stage(nc, m, ins, out)


def kernel(**inputs):
    import concourse.bacc as bacc
    from concourse.bass_utils import run_bass_kernel_spmd

    nc = bacc.Bacc("TRN2", target_bir_lowering=False, num_devices=1)
    arrays, ins = {}, {}
    for name in inputs:
        a = np.ascontiguousarray(inputs[name])
        arrays["in_" + name] = a
        ins[name] = nc.dram_tensor("in_" + name, a.shape, mybir.dt.from_np(a.dtype), kind="ExternalInput").ap()
    out = nc.dram_tensor("out_0", (B, C, H, W), F32, kind="ExternalOutput").ap()
    hybrid_program(nc, ins, out)
    r = run_bass_kernel_spmd(nc, [arrays], core_ids=[0])
    return r.results[0]["out_0"]
```
